# Optimizing a Trainium2 kernel written in Bass

```python
import numpy as np
import jax
import jax.numpy as jnp

def _softmax(x, axis=-1):
    return jax.nn.softmax(x, axis=axis)

def _gelu(x):
    return jax.nn.gelu(x, approximate=True)

def _silu(x):
    return jax.nn.silu(x)

def _sigmoid(x):
    return jax.nn.sigmoid(x)

def _layernorm(x, axis=-1, eps=1e-05):
    m = jnp.mean(x, axis=axis, keepdims=True)
    v = jnp.var(x, axis=axis, keepdims=True)
    return (x - m) / jnp.sqrt(v + eps)

def _scatter_add(tgt, idx, src, axis=0):
    return tgt.at[idx].add(src)

def _segment_sum(src, seg, n):
    return jax.ops.segment_sum(src, seg, n)
kernel_name = 'mk_early_fusion_d1_tok_img1024_r4_daef81'

def setup_inputs(seed: int=0):
    np.random.seed(seed)
    _w = jnp.asarray

    def _rec_inputs():
        import jax
        import jax.numpy as jnp
        _rk = jax.random.key(seed)
        x = 0.00021031 + 1.00007 * jax.random.normal(jax.random.fold_in(_rk, 1), (8, 1, 256, 256), jnp.float32)
        txt = 0.949517 + 0.151997 * jax.random.normal(jax.random.fold_in(_rk, 2), (8, 77, 256), jnp.float32)
        return (x, txt)
    x, txt = _rec_inputs()

    def _L0_tok_setup():
        import jax, jax.numpy as jnp
        import numpy as np
        KERNEL = jnp.array([[[[1.0, 0.0], [0.0, -1.0]]], [[[0.0, -1.0], [1.0, 0.0]]]], dtype=jnp.float32)
        key = jax.random.key(seed)
        images = jax.random.normal(key, (32, 1, 256, 256), dtype=jnp.float32)
        return {'images': images}
    _L0_tok_all = _L0_tok_setup()
    _L0_tok_in = {k: v for k, v in _L0_tok_all.items() if k in ()}
    del _L0_tok_all

    def _L0_attn_setup():
        import jax, jax.numpy as jnp
        import numpy as np
        LN_EPS = 1e-05
        key = jax.random.key(seed)
        k_u, k_B, k_C = jax.random.split(key, 3)
        Bsz, L, d_model, d_state = (8, 1024, 256, 64)
        u = jax.random.normal(k_u, (Bsz, L, d_model), dtype=jnp.float32)
        log_neg_real = -0.5 * jnp.ones((d_state,), jnp.float32)
        imag = jnp.arange(1, d_state + 1, dtype=jnp.float32)
        B_mat = jax.random.normal(k_B, (d_state, d_model), jnp.float32) / d_model ** 0.5
        C_mat = jax.random.normal(k_C, (d_model, d_state), jnp.float32) / d_state ** 0.5
        D = jnp.zeros((d_model,), jnp.float32)
        gamma = jnp.ones((d_model,), jnp.float32)
        beta = jnp.zeros((d_model,), jnp.float32)
        return {'u': u, 'log_neg_real': log_neg_real, 'imag': imag, 'B_mat': B_mat, 'C_mat': C_mat, 'D': D, 'gamma': gamma, 'beta': beta}
    _L0_attn_all = _L0_attn_setup()
    _L0_attn_in = {k: v for k, v in _L0_attn_all.items() if k in ('log_neg_real', 'imag', 'B_mat', 'C_mat', 'D', 'gamma', 'beta')}
    del _L0_attn_all

    def _L0_ffn_setup():
        import jax, jax.numpy as jnp
        import numpy as np
        D, H, O, E, TOPK = (256, 1024, 256, 8, 2)
        B, L = (2, 512)
        ROUTE_SCALE = 1.0
        key = jax.random.key(seed)
        ks = jax.random.split(key, 7)
        gb = float(np.sqrt(6.0 / (E + D)))
        return {'x': jax.random.normal(ks[0], (B, L, D), dtype=jnp.float32), 'gate_w': jax.random.uniform(ks[1], (E, D), jnp.float32, -gb, gb), 'gate_b': jnp.zeros((E,), jnp.float32), 'w1': jax.random.normal(ks[2], (E, D, H), jnp.float32) * 0.02, 'b1': jnp.zeros((E, H), jnp.float32), 'w2': jax.random.normal(ks[3], (E, H, O), jnp.float32) * 0.02, 'b2': jnp.zeros((E, O), jnp.float32)}
    _L0_ffn_all = _L0_ffn_setup()
    _L0_ffn_in = {k: v for k, v in _L0_ffn_all.items() if k in ('gate_w', 'gate_b', 'w1', 'b1', 'w2', 'b2')}
    del _L0_ffn_all
    return {'x': x, 'txt': txt, 'L0_attn_log_neg_real': _L0_attn_in['log_neg_real'], 'L0_attn_imag': _L0_attn_in['imag'], 'L0_attn_B_mat': _L0_attn_in['B_mat'], 'L0_attn_C_mat': _L0_attn_in['C_mat'], 'L0_attn_D': _L0_attn_in['D'], 'L0_attn_gamma': _L0_attn_in['gamma'], 'L0_attn_beta': _L0_attn_in['beta'], 'L0_ffn_gate_w': _L0_ffn_in['gate_w'], 'L0_ffn_gate_b': _L0_ffn_in['gate_b'], 'L0_ffn_w1': _L0_ffn_in['w1'], 'L0_ffn_b1': _L0_ffn_in['b1'], 'L0_ffn_w2': _L0_ffn_in['w2'], 'L0_ffn_b2': _L0_ffn_in['b2']}

def reference(x, txt, L0_attn_log_neg_real, L0_attn_imag, L0_attn_B_mat, L0_attn_C_mat, L0_attn_D, L0_attn_gamma, L0_attn_beta, L0_ffn_gate_w, L0_ffn_gate_b, L0_ffn_w1, L0_ffn_b1, L0_ffn_w2, L0_ffn_b2):
    import jax
    import jax.numpy as jnp

    def _L0_tok_ref(images):
        import jax, jax.numpy as jnp
        import numpy as np
        KERNEL = jnp.array([[[[1.0, 0.0], [0.0, -1.0]]], [[[0.0, -1.0], [1.0, 0.0]]]], dtype=jnp.float32)
        out = jax.lax.conv_general_dilated(images, KERNEL, window_strides=(1, 1), padding=((0, 1), (0, 1)), dimension_numbers=('NCHW', 'OIHW', 'NCHW'))
        return jnp.clip(jnp.sum(jnp.abs(out), axis=1), 0.0, 1.0)

    def _L0_attn_ref(u, log_neg_real, imag, B_mat, C_mat, D, gamma, beta):
        import jax, jax.numpy as jnp
        import numpy as np
        LN_EPS = 1e-05
        Bsz, L, d_model = u.shape
        d_state = log_neg_real.shape[0]
        a = jax.lax.complex(-jnp.exp(log_neg_real), imag)
        a_bar = jnp.exp(a)
        b_bar = ((a_bar - 1.0) / a)[:, None] * B_mat.astype(a.dtype)
        Bu = jnp.einsum('bld,nd->bln', u.astype(a.dtype), b_bar)

        def step(h, x_t):
            h = h * a_bar + x_t
            return (h, h)
        h0 = jnp.zeros((Bsz, d_state), a.dtype)
        _, hs = jax.lax.scan(step, h0, jnp.swapaxes(Bu, 0, 1))
        hs = jnp.swapaxes(hs, 0, 1)
        y = jnp.einsum('bln,dn->bld', hs, C_mat.astype(a.dtype)).real + D * u
        x = u + y
        mu = jnp.mean(x, axis=-1, keepdims=True)
        var = jnp.mean((x - mu) ** 2, axis=-1, keepdims=True)
        return (x - mu) * jax.lax.rsqrt(var + LN_EPS) * gamma + beta

    def _L0_ffn_ref(x, gate_w, gate_b, w1, b1, w2, b2):
        import jax, jax.numpy as jnp
        import numpy as np
        D, H, O, E, TOPK = (256, 1024, 256, 8, 2)
        B, L = (2, 512)
        ROUTE_SCALE = 1.0
        Bb, Ll, Dd = x.shape
        N = Bb * Ll
        x_flat = x.reshape(N, Dd)
        logits = x_flat @ gate_w.T + gate_b
        probs = jax.nn.softmax(logits * ROUTE_SCALE, axis=-1)
        topk_vals, topk_idx = jax.lax.top_k(probs, TOPK)
        dense_gate = jnp.zeros((N, E), probs.dtype).at[jnp.arange(N)[:, None], topk_idx].set(topk_vals)
        h = jax.nn.relu(jnp.einsum('nd,edh->neh', x_flat, w1) + b1)
        y = jnp.einsum('neh,eho->neo', h, w2) + b2
        out_flat = jnp.einsum('ne,neo->no', dense_gate, y)
        return out_flat.reshape(Bb, Ll, O)
    h = _L0_tok_ref(x)
    h = jnp.concatenate([h, txt], axis=1)
    h = h + _L0_attn_ref(_layernorm(h, axis=-1), L0_attn_log_neg_real, L0_attn_imag, L0_attn_B_mat, L0_attn_C_mat, L0_attn_D, L0_attn_gamma, L0_attn_beta)
    h = h + _L0_ffn_ref(_layernorm(h, axis=-1), L0_ffn_gate_w, L0_ffn_gate_b, L0_ffn_w1, L0_ffn_b1, L0_ffn_w2, L0_ffn_b2)
    return h

_drawn_inputs = setup_inputs


def setup_inputs(seed=0):
    import zlib

    import numpy as np

    out = dict(_drawn_inputs(seed))
    spreads = {'L0_attn_log_neg_real': (-0.5, 0.6),
     'L0_attn_D': (0.0, 0.1),
     'L0_attn_gamma': (1.0, 0.2),
     'L0_attn_beta': (0.0, 0.1),
     'L0_ffn_gate_b': (0.0, 0.737),
     'L0_ffn_b1': (0.0, 0.512),
     'L0_ffn_b2': (0.0, 0.1)}
    factors = {}
    for name, (base, spread) in spreads.items():
        noise = np.random.default_rng([zlib.crc32(name.encode()), seed]).standard_normal(out[name].shape)
        drawn = base * np.exp(spread * noise) if base else spread * noise
        out[name] = jnp.asarray(drawn.astype(out[name].dtype))
    for name, factor in factors.items():
        out[name] = (out[name] * factor).astype(out[name].dtype)
    return out
```

```python
from contextlib import ExitStack

import concourse.bass as bass
from concourse import mybir

F32, F16, BF16 = mybir.dt.float32, mybir.dt.float16, mybir.dt.bfloat16
I32, U32 = mybir.dt.int32, mybir.dt.uint32
ALU, ACT, AX = mybir.AluOpType, mybir.ActivationFunctionType, mybir.AxisListType

P = 128
BATCH, IMG, TXT, D = 8, 256, 77, 256
L = IMG + TXT
NTOK = BATCH * L
NTXT = BATCH * TXT
IMG_TILES = BATCH * IMG // P
TXT_TILES = -(-NTXT // P)
TXT_LAST = NTXT - (TXT_TILES - 1) * P
NT = IMG_TILES + TXT_TILES
STATE = 64
E, HID, TOPK = 8, 1024, 2
KD, KH = D // P, HID // P
SLOT_TILES = (TOPK * NTOK + E * (P - 1)) // P
ROWS = NTOK + P
MID = NTOK // 2
EPS = 1e-5
TWO_PI = 6.283185307179586
PI_A = 6.28125
PI_B = 0.0019350051879882812
PI_C = TWO_PI - PI_A - PI_B
ROUND = 12582912.0
X_SCALE = 2.0 ** 9
TINY = 2.0 ** -60


def build(nc, t, out):
    with ExitStack() as ctx:
        def sb(name, shape, dt=F32):
            return ctx.enter_context(nc.sbuf_tensor(name, shape, dt))

        def sem(name):
            return ctx.enter_context(nc.semaphore(name))

        w1_hi = sb("w1_hi", [P, E, KD, HID], F16)
        w1_lo = sb("w1_lo", [P, E, KD, HID], F16)
        w2_hi = sb("w2_hi", [P, E, KH, D], F16)
        w2_lo = sb("w2_lo", [P, E, KH, D], F16)
        b1_cols = sb("b1_cols", [P, E, KH])
        b1_scaled = sb("b1_scaled", [P, E, KH])
        ident = sb("ident", [P, P])
        small = sb("small", [P, 384])
        slot_token = sb("slot_token", [P, SLOT_TILES], U32)
        tile_expert = sb("tile_expert", [P, SLOT_TILES], I32)
        token_index = sb("token_index", [P, 4], U32)
        txt_rows = sb("txt_rows", [P, TXT_TILES], U32)
        ARENA = 17184
        arena = sb("arena", [P, ARENA])
        cursor = [0]

        def take(*shape, dt=F32, bytes_each=4):
            n = 1
            for k in shape:
                n *= k
            words = -(-n * bytes_each // 4)
            a = arena[:, cursor[0]:cursor[0] + words]
            cursor[0] += words
            assert cursor[0] <= ARENA, cursor[0]
            if dt != F32:
                a = a.bitcast(dt)
            if len(shape) == 1:
                return a
            names = "abcd"[:len(shape)]
            return a.rearrange(f"p ({' '.join(names)}) -> p {' '.join(names)}", **dict(zip(names, shape)))

        w1_stage = take(KD, HID)
        w2_stage = take(KH, D)
        x_top = take(2, D + 1)
        x_below = take(2, D + 1)
        corner = take(2, 2, D)
        h = [take(2, D) for _ in range(2)]
        u = [take(2, D) for _ in range(2)]
        u_t = take(KD, 2, P)
        xn_t = take(KD, 2, P)
        h_txt = take(TXT_TILES, D)
        u_txt = take(TXT_TILES, D)
        u_t_txt = take(KD, TXT_TILES, P)
        tables_at = cursor[0]
        in_table = take(L)
        out_table = take(L)
        decay = take(L)
        drive = take(L)
        state = take(L)
        turned = take(IMG)
        turned_txt = take(TXT_TILES * P)
        b_t = take(KD, P)
        c_t = take(D)
        gate_t = take(KD, E)
        d_row = take(D)
        gamma_row = take(D)
        beta_row = take(D)
        gateb_row = take(E)
        zeros = take(D)
        cursor[0] = tables_at
        cmp8 = take(SLOT_TILES, E)
        cursor[0] = 0
        onehot_slot = take(2 * NT, P, dt=F16, bytes_each=2)
        onehot_tile = take(2 * NT, SLOT_TILES, dt=F16, bytes_each=2)
        cursor[0] = 0
        h_act = [take(HID) for _ in range(2)]
        h_hi = [take(KH, P, dt=F16, bytes_each=2) for _ in range(2)]
        h_lo = [take(KH, P, dt=F16, bytes_each=2) for _ in range(2)]
        cursor[0] = max(cursor[0], 2 * NT * (P + SLOT_TILES) // 2)
        x_slot = [take(D) for _ in range(2)]
        x_hi = [take(KD, P, dt=F16, bytes_each=2) for _ in range(2)]
        x_lo = [take(KD, P, dt=F16, bytes_each=2) for _ in range(2)]
        y_slot = [take(D) for _ in range(2)]
        y_gated = [take(D) for _ in range(2)]
        gate_slot = [take(E) for _ in range(2)]
        b2_rows = take(E, D)
        iota_slot = sb("iota_slot", [P, P], F16)
        iota_tile = sb("iota_tile", [P, SLOT_TILES])
        token_val = sb("token_val", [P, NT])
        valid = sb("valid", [P, NT])
        prefix_w = sb("prefix_w", [P, P], BF16)
        ones_w = sb("ones_w", [P, P], BF16)
        r_a = sb("r_a", [P, NT, E])
        r_b = sb("r_b", [P, NT, E])
        r_c = sb("r_c", [P, NT, E])
        pick = [sb(f"pick{i}", [P, NT, E]) for i in range(2)]
        picked = sb("picked", [P, E, NT], BF16)
        ones_f = sb("ones_f", [P, NT * E])
        desc = sb("desc", [P, E])
        pad_row = sb("pad_row", [P, 1])
        mv = sb("mv", [P, 3, NT, 2])
        rstd = sb("rstd", [P, 3, NT])
        vpe = sb("vpe", [P, 3, NT])
        bst = sb("bst", [P, TXT_TILES, 6])
        mhalf = sb("mhalf", [P, TXT_TILES])
        tr = [sb(f"tr{i}", [P, NT]) for i in range(3)]
        slot_f = sb("slot_f", [P, TOPK, NT])
        tile_f = sb("tile_f", [P, TOPK, NT])
        within_f = sb("within_f", [P, TOPK, NT], F16)
        tile_h = sb("tile_h", [P, TOPK, NT])
        ssm = sb("ssm", [P, 40])
        wmax = sb("wmax", [P, E, 3])
        wmax_all = sb("wmax_all", [P, E, 3])
        pow2 = sb("pow2", [P, E, 3])
        wsc = sb("wsc", [P, E, 3])
        hsc = sb("hsc", [P, 4, E])
        cos_t = drive
        sin_t = state

        bank = [ctx.enter_context(nc.psum_tensor(f"bank{i}", [P, 512], F32)) for i in range(8)]
        ps_ut, ps_v, ps_y, ps_xnt, ps_logit, ps_rank, ps_slot = bank[:7]
        ps_h = [[bank[0], bank[1]], [bank[2], bank[3]]]
        ps_out = bank[4:6]
        ps_x = bank[6:8]

        xn_dram = nc.dram_tensor("xn_rows", [ROWS, D], F32, kind="Internal").ap()
        gate_dram = nc.dram_tensor("gate_rows", [ROWS, E], F32, kind="Internal").ap()

        consts_in = sem("consts_in")
        txt_in = sem("txt_in")
        x_in = sem("x_in")
        w1_in, w2_in = sem("w1_in"), sem("w2_in")
        v_step = sem("v_step")
        p_step = sem("p_step")
        a_step = sem("a_step")
        zeroed = sem("zeroed")
        txt_zeroed = sem("txt_zeroed")
        trig_in = sem("trig_in")
        trig_done = sem("trig_done")
        tables_done = sem("tables_done")
        diff_v, diff_p, abs_done, sum_done = sem("diff_v"), sem("diff_p"), sem("abs_done"), sem("sum_done")
        h_done = sem("h_done")
        stats_done = [sem(f"stats_done{i}") for i in range(3)]
        rstd_done = [sem(f"rstd_done{i}") for i in range(3)]
        u_done = sem("u_done")
        ut_txt, ut_txt_done = sem("ut_txt"), sem("ut_txt_done")
        ut_psum, ut_done = sem("ut_psum"), sem("ut_done")
        skip_done = sem("skip_done")
        v_psum, state_done = sem("v_psum"), sem("state_done")
        drive_done = sem("drive_done")
        turned_done = sem("turned_done")
        y_psum, sum2_done = sem("y_psum"), sem("sum2_done")
        t_done, gamma_done = sem("t_done"), sem("gamma_done")
        h1_done, h1_out = sem("h1_done"), sem("h1_out")
        xn_done, xn_out = sem("xn_done"), sem("xn_out")
        xnt_psum, xnt_done = sem("xnt_psum"), sem("xnt_done")
        logits_done = sem("logits_done")
        max_w, max_all = sem("max_w"), sem("max_all")
        scale_done = sem("scale_done")
        hi1_done, hi2_done = sem("hi1_done"), sem("hi2_done")
        lo1_done, lo2_done = sem("lo1_done"), sem("lo2_done")
        shifted, exped = sem("shifted"), sem("exped")
        gates_done, gates_out = sem("gates_done"), sem("gates_out")
        picked_done, rank_psum = sem("picked_done"), sem("rank_psum")
        onehots_done, slot_psum = sem("onehots_done"), sem("slot_psum")
        slots_done = sem("slots_done")
        h1_txt_out, xn_txt_out, gates_txt_out = sem("h1_txt_out"), sem("xn_txt_out"), sem("gates_txt_out")
        b2_in = sem("b2_in")
        held = sem("held")
        x_idx, y_idx = sem("x_idx"), sem("y_idx")
        x_here = [sem(f"x_here{i}") for i in range(2)]
        g_here = [sem(f"g_here{i}") for i in range(2)]
        x_turned = sem("x_turned")
        xhi_done, xlo_done = sem("xhi_done"), sem("xlo_done")
        mm1_done, relu_done, split_done = sem("mm1_done"), sem("relu_done"), sem("split_done")
        hi_done = sem("hi_done")
        mm2_done, y_scaled, y_done = sem("mm2_done"), sem("y_scaled"), sem("y_done")
        y_out = sem("y_out")

        N_CONST = 20
        TXTG = BATCH

        def group(b):
            if b == TXTG:
                return TXT_TILES, IMG_TILES, h_txt, u_txt
            return 2, 2 * b, h[b % 2], u[b % 2]

        FRONT = [TXTG] + list(range(BATCH))
        BACK = list(range(BATCH)) + [TXTG]

        def f_no(b):
            return FRONT.index(b) + 1

        def b_no(b):
            return BACK.index(b) + 1

        block = ctx.enter_context(nc.Block())

        @block.sync
        def _(sp):
            for name, dst in (("ident", ident[:, :]), ("cols", small[:, 0:16]),
                              ("b1", b1_cols[:, :, :]), ("b_t", b_t), ("d_row", d_row)):
                sp.dma_start(dst, t[name]).then_inc(consts_in, 16)
            sp.wait_ge(txt_zeroed, 1)
            sp.dma_start(h_txt[:, 0:TXT_TILES - 1, :],
                         t["txt"][0:(TXT_TILES - 1) * P].rearrange("(k p) d -> p k d", p=P)).then_inc(txt_in, 16)
            sp.dma_start(h_txt[0:TXT_LAST, TXT_TILES - 1, :], t["txt"][(TXT_TILES - 1) * P:NTXT]).then_inc(txt_in, 16)

            def load_x(b):
                if b >= 1:
                    sp.wait_ge(diff_v, b)
                    sp.wait_ge(diff_p, b)
                sp.dma_start(x_top, t["x"][b, 0:IMG, :].rearrange("(k p) w -> p k w", p=P)).then_inc(x_in, 16)
                sp.dma_start(x_below, t["x"][b, 1:IMG + 1, :].rearrange("(k p) w -> p k w", p=P)).then_inc(x_in, 16)

            def load_w1(e):
                if e >= 1:
                    sp.wait_ge(hi1_done, e)
                    sp.wait_ge(lo1_done, e)
                sp.dma_start(w1_stage, t["w1"][e].rearrange("(k p) h -> p k h", p=P)).then_inc(w1_in, 16)

            def load_w2(e):
                if e >= 1:
                    sp.wait_ge(hi2_done, e)
                    sp.wait_ge(lo2_done, e)
                sp.dma_start(w2_stage, t["w2"][e].rearrange("(k p) o -> p k o", p=P)).then_inc(w2_in, 16)

            load_x(0)
            load_w1(0)
            load_w2(0)
            for name, dst in (("c_t", c_t), ("gate_t", gate_t), ("gamma_row", gamma_row), ("beta_row", beta_row),
                              ("gateb_row", gateb_row), ("txt_rows", txt_rows[:, :]), ("iota_slot", iota_slot[:, :]),
                              ("iota_tile", iota_tile[:, :]), ("token_val", token_val[:, :]), ("valid", valid[:, :]),
                              ("prefix_w", prefix_w[:, :]), ("ones_w", ones_w[:, :]), ("desc", desc[:, :]),
                              ("pad_row", pad_row[:, :]), ("mhalf", mhalf[:, :])):
                sp.dma_start(dst, t[name]).then_inc(consts_in, 16)
            sp.wait_ge(zeroed, 1)
            sp.dma_start(out[NTOK:ROWS, :], zeros).then_inc(h1_out, 16)
            sp.dma_start(xn_dram[NTOK:ROWS, :], zeros).then_inc(xn_out, 16)
            sp.dma_start(gate_dram[NTOK:ROWS, :], zeros[:, 0:E]).then_inc(gates_out, 16)

            def store_h1(b):
                sp.wait_ge(h1_done, b_no(b))
                sp.dma_start(out[L * b:L * b + IMG].rearrange("(k p) d -> p k d", p=P), h[b % 2]).then_inc(h1_out, 16)

            def store_xn(b):
                sp.wait_ge(xn_done, b_no(b))
                sp.dma_start(xn_dram[L * b:L * b + IMG].rearrange("(k p) d -> p k d", p=P),
                             u[b % 2]).then_inc(xn_out, 16)

            load_x(1)
            for b in range(1, BATCH + 1):
                if b + 1 < BATCH:
                    load_x(b + 1)
                if b < BATCH:
                    load_w1(b)
                    load_w2(b)
                store_h1(b - 1)
                store_xn(b - 1)
            sp.wait_ge(gates_done, 1)
            sp.wait_ge(h1_out, 16 * (1 + BATCH))
            sp.wait_ge(h1_txt_out, 16 * TXT_TILES)
            sp.wait_ge(xn_out, 16 * (1 + BATCH))
            sp.wait_ge(xn_txt_out, 16 * TXT_TILES)
            sp.dma_start(b2_rows, t["b2"]).then_inc(b2_in, 16)
            for b in range(BATCH):
                sp.dma_start(gate_dram[L * b:L * b + IMG].rearrange("(k p) e -> p k e", p=P),
                             r_a[:, 2 * b:2 * b + 2, :]).then_inc(gates_out, 16)

        @block.gpsimd
        def _(pool):
            n = [0]

            def link(ins):
                n[0] += 1
                ins.then_inc(p_step, 1)
                pool.wait_ge(p_step, n[0])

            nc.gpsimd.memset(h_txt[96:P, TXT_TILES - 1, :], 0.0).then_inc(txt_zeroed, 1)
            pool.wait_ge(txt_zeroed, 1)
            nc.gpsimd.memset(zeros, 0.0).then_inc(zeroed, 1)
            pool.wait_ge(zeroed, 1)
            link(nc.gpsimd.memset(turned_txt[:, NTXT:], 0.0))
            pool.wait_ge(consts_in, 16 * N_CONST)

            def rstd_of(b, which, no):
                k, t0, _, _ = group(b)
                pool.wait_ge(stats_done[which], no)
                link(nc.gpsimd.tensor_scalar(vpe[:, which, t0:t0 + k], mv[:, which, t0:t0 + k, 1], EPS, None, ALU.add))
                nc.gpsimd.tensor_tensor(rstd[:, which, t0:t0 + k], vpe[:, which, t0:t0 + k], mhalf[:, 0:k],
                                        ALU.pow).then_inc(rstd_done[which], 1)

            def diffs(b):
                pool.wait_ge(x_in, 32 * (b + 1))
                if b >= 1:
                    pool.wait_ge(sum_done, b)
                nc.gpsimd.tensor_tensor(corner[:, 1, :, :], x_below[:, :, 0:D], x_top[:, :, 1:D + 1],
                                        ALU.subtract).then_inc(diff_p, 1)

            def sums(b):
                pool.wait_ge(abs_done, b + 1)
                if b >= 2:
                    pool.wait_ge(h1_out, 16 * (b - 1) + 16)
                    pool.wait_ge(xn_done, b - 1)
                nc.gpsimd.tensor_tensor(h[b % 2], corner[:, 0, :, :], corner[:, 1, :, :], ALU.add).then_inc(sum_done, 1)

            def skip(b):
                k, _, _, ub = group(b)
                pool.wait_ge(u_done, f_no(b))
                pool.wait_ge(ut_psum, f_no(b))
                nc.gpsimd.tensor_tensor(ub, ub, d1.rearrange("p (a d) -> p a d", a=1).broadcast_to([P, k, D]),
                                        ALU.mult).then_inc(skip_done, 1)

            d1 = d_row
            link(nc.gpsimd.tensor_scalar(d_row, d_row, 1.0, None, ALU.add))

            def front(b):
                if b == TXTG:
                    rstd_of(b, 0, f_no(b))
                    skip(b)
                    return
                rstd_of(b, 0, f_no(b))
                if b + 1 < BATCH:
                    diffs(b + 1)
                skip(b)

            def turn(b):
                pool.wait_ge(state_done, b + 1)
                if b == 0:
                    pool.wait_ge(tables_done, 1)
                else:
                    pool.wait_ge(y_psum, b)
                link(nc.gpsimd.tensor_tensor(turned, state[:, 0:IMG], out_table[:, 0:IMG], ALU.mult))
                nc.gpsimd.tensor_tensor(turned_txt[:, TXT * b:TXT * (b + 1)], state[:, IMG:L], out_table[:, IMG:L],
                                        ALU.mult).then_inc(turned_done, 1)

            def back(b):
                k, _, hb, ub = group(b)
                pool.wait_ge(h_done, f_no(b))
                pool.wait_ge(stats_done[0], f_no(b))
                pool.wait_ge(u_done, f_no(b))
                link(nc.gpsimd.tensor_tensor(hb, hb, beta_row.rearrange("p (a d) -> p a d", a=1).broadcast_to([P, k, D]),
                                             ALU.add))
                rstd_of(b, 1, b_no(b))
                pool.wait_ge(t_done, b_no(b))
                nc.gpsimd.tensor_tensor(ub, ub, gamma_row.rearrange("p (a d) -> p a d", a=1).broadcast_to([P, k, D]),
                                        ALU.mult).then_inc(gamma_done, 1)
                rstd_of(b, 2, b_no(b))

            def weights(e):
                pool.wait_ge(max_w, e + 1)
                nc.gpsimd.partition_all_reduce(wmax_all[:, e, :], wmax[:, e, :], P,
                                               bass.bass_isa.ReduceOp.max).then_inc(max_all, 1)

            def weights_lo(e):
                pool.wait_ge(hi2_done, e + 1)
                nc.gpsimd.tensor_tensor(w2_lo[:, e, :, :], w2_stage, w2_hi[:, e, :, :],
                                        ALU.subtract).then_inc(lo2_done, 1)

            diffs(0)
            sums(0)
            front(TXTG)
            for b in range(BATCH):
                front(b)
                if b >= 1:
                    turn(b - 1)
                weights(b)
                if b >= 1:
                    back(b - 1)
                weights_lo(b)
                if b + 1 < BATCH:
                    sums(b + 1)
            turn(BATCH - 1)
            back(BATCH - 1)
            back(TXTG)
            pool.wait_ge(xn_out, 16)
            pool.wait_ge(h1_out, 16)
            pool.wait_ge(h1_done, b_no(TXTG))
            for k in range(TXT_TILES):
                nc.gpsimd.indirect_dma_start(out, bass.IndirectOffsetOnAxis(ap=txt_rows[:, k:k + 1], axis=0),
                                             h_txt[:, k, :], None).then_inc(h1_txt_out, 16)
            pool.wait_ge(xn_done, b_no(TXTG))
            for k in range(TXT_TILES):
                nc.gpsimd.indirect_dma_start(xn_dram, bass.IndirectOffsetOnAxis(ap=txt_rows[:, k:k + 1], axis=0),
                                             u_txt[:, k, :], None).then_inc(xn_txt_out, 16)
            pool.wait_ge(gates_done, 1)
            pool.wait_ge(gates_out, 16)
            for k in range(TXT_TILES):
                nc.gpsimd.indirect_dma_start(gate_dram, bass.IndirectOffsetOnAxis(ap=txt_rows[:, k:k + 1], axis=0),
                                             r_a[:, IMG_TILES + k, :], None).then_inc(gates_txt_out, 16)

            def hold():
                pool.sem_inc(held, 1)

            def gather_x(j, s):
                nc.gpsimd.tensor_copy(token_index[:, s:s + 1], slot_token[:, bass.ds(j, 1)]).then_inc(x_idx, 1)
                pool.wait_ge(x_idx, j + 1)
                hold()
                nc.gpsimd.indirect_dma_start(x_slot[s], None, xn_dram,
                                             bass.IndirectOffsetOnAxis(ap=token_index[:, s:s + 1], axis=0)
                                             ).then_inc(x_here[s], 16)

            def gather_gates(j, s):
                nc.gpsimd.tensor_copy(token_index[:, 2 + s:3 + s], slot_token[:, bass.ds(j, 1)]).then_inc(y_idx, 1)
                pool.wait_ge(y_idx, j + 1)
                hold()
                nc.gpsimd.indirect_dma_start(gate_slot[s], None, gate_dram,
                                             bass.IndirectOffsetOnAxis(ap=token_index[:, 2 + s:3 + s], axis=0)
                                             ).then_inc(g_here[s], 16)

            def scatter(j, s, first=False):
                pool.wait_ge(y_done, j + 1)
                if not first:
                    hold()
                    pool.wait_ge(y_out, j * 16)
                hold()
                nc.gpsimd.indirect_dma_start(out, bass.IndirectOffsetOnAxis(ap=token_index[:, 2 + s:3 + s], axis=0),
                                             y_gated[s], None, compute_op=ALU.add).then_inc(y_out, 16)

            def pool_step(j, s, first=False, x=True, g=True):
                if x:
                    pool.wait_ge(x_turned, j + 3)
                    hold()
                    gather_x(j + 4, s)
                scatter(j, s, first)
                if g:
                    pool.wait_ge(y_out, (j + 1) * 16)
                    hold()
                    gather_gates(j + 2, s)

            pool.wait_ge(slots_done, 1)
            pool.wait_ge(xn_out, 16 * (1 + BATCH))
            pool.wait_ge(xn_txt_out, 16 * TXT_TILES)
            pool.wait_ge(h1_out, 16 * (1 + BATCH))
            pool.wait_ge(h1_txt_out, 16 * TXT_TILES)
            pool.wait_ge(gates_out, 16 * (1 + BATCH))
            pool.wait_ge(gates_txt_out, 16 * TXT_TILES)
            gather_x(0, 0)
            gather_x(1, 1)
            gather_gates(0, 0)
            gather_gates(1, 1)
            for j in range(2, 4):
                pool.wait_ge(x_turned, j - 1)
                gather_x(j, j % 2)
            pool_step(0, 0, first=True)
            with pool.Fori(0, (SLOT_TILES - 5) // 2) as i:
                for s in range(2):
                    pool_step(i * 2 + (1 + s), (1 + s) % 2)
            for j in range(SLOT_TILES - 4, SLOT_TILES):
                pool_step(j, j % 2, x=False, g=j + 2 < SLOT_TILES)
            pool.wait_ge(y_out, 16 * SLOT_TILES)

        @block.scalar
        def _(act):
            n = [0]

            def link(ins):
                n[0] += 1
                ins.then_inc(a_step, 1)
                act.wait_ge(a_step, n[0])

            act.wait_ge(trig_in, 1)
            link(nc.scalar.activation(ssm[:, 0:1], small[:, 0:1], ACT.Exp))
            link(nc.scalar.activation(ssm[:, 1:2], ssm[:, 0:1], ACT.Exp, scale=-1.0))
            link(nc.scalar.activation(ssm[:, 2:3], ssm[:, 20:21], ACT.Sin))
            nc.scalar.activation(ssm[:, 3:4], ssm[:, 21:22], ACT.Sin).then_inc(trig_done, 1)

            def absolute(b):
                act.wait_ge(diff_v, b + 1)
                act.wait_ge(diff_p, b + 1)
                nc.scalar.activation(corner, corner, ACT.Abs).then_inc(abs_done, 1)

            def copy_ut(b):
                k, _, _, _ = group(b)
                if b == TXTG:
                    for i in range(KD * 2):
                        kd, part = i // 2, i % 2
                        lo, hi_ = (0, 4) if part == 0 else (4, 5)
                        act.wait_ge(ut_txt, i + 1)
                        ins = nc.scalar.activation(u_t_txt[:, kd, lo:hi_, :], ps_ut[:, 0:(hi_ - lo) * P].rearrange(
                            "p (a c) -> p a c", c=P), ACT.Copy)
                        ins.then_inc(ut_txt_done, 1)
                    return
                act.wait_ge(ut_psum, f_no(b))
                if b >= 1:
                    act.wait_ge(v_psum, b)
                nc.scalar.activation(u_t, ps_ut[:, :].rearrange("p (k a c) -> p k a c", k=KD, a=2),
                                     ACT.Copy).then_inc(ut_done, 1)

            def copy_xnt(i):
                act.wait_ge(xnt_psum, i + 1)
                if i >= 1:
                    act.wait_ge(logits_done, i)
                nc.scalar.activation(xn_t, ps_xnt[:, :].rearrange("p (k a c) -> p k a c", k=KD, a=2),
                                     ACT.Copy).then_inc(xnt_done, 1)

            def weights_hi(e):
                act.wait_ge(scale_done, e + 1)
                nc.scalar.activation(w1_hi[:, e, :, :], w1_stage, ACT.Copy, scale=wsc[:, e, 0:1]).then_inc(hi1_done, 1)
                link(nc.scalar.activation(w2_stage, w2_stage, ACT.Copy, scale=wsc[:, e, 1:2]))
                nc.scalar.activation(w2_hi[:, e, :, :], w2_stage, ACT.Copy).then_inc(hi2_done, 1)

            absolute(0)
            copy_ut(TXTG)
            for b in range(BATCH):
                if b + 1 < BATCH:
                    absolute(b + 1)
                copy_ut(b)
                weights_hi(b)
                if b >= 1:
                    copy_xnt(b - 1)
            copy_xnt(BATCH - 1)
            for i in range(BATCH, BATCH + 3):
                copy_xnt(i)
            act.wait_ge(shifted, 1)
            nc.scalar.activation(r_b[:, :, :], r_a[:, :, :], ACT.Exp).then_inc(exped, 1)

            def hold():
                act.sem_inc(held, 1)

            def x_high(j, s, early=False):
                act.wait_ge(x_turned, j + 1)
                if not early:
                    act.wait_ge(mm1_done, j * 2 - 2)
                nc.scalar.activation(x_hi[s], ps_x[s][:, 0:D].rearrange("p (k c) -> p k c", k=KD), ACT.Copy,
                                     scale=X_SCALE).then_inc(xhi_done, 1)

            def relu(j, s, early=False):
                e = act.value_load(tile_expert[0:1, bass.ds(j, 1)], min_val=0, max_val=E - 1)
                for half in range(2):
                    act.wait_ge(mm1_done, j * 2 + (half + 1))
                    if not early:
                        hold()
                        act.wait_ge(split_done, j * 2 + (half - 3))
                    hold()
                    for c in range(4 * half, 4 * half + 4):
                        ins = nc.scalar.activation(h_act[s][:, c * P:(c + 1) * P],
                                                   ps_h[s][half][:, (c % 4) * P:(c % 4 + 1) * P], ACT.Relu,
                                                   bias=b1_scaled[:, bass.ds(e, 1), c],
                                                   scale=hsc[:, 2, bass.ds(e, 1)])
                    ins.then_inc(relu_done, 1)

            act.wait_ge(slots_done, 1)
            x_high(0, 0, early=True)
            x_high(1, 1, early=True)
            relu(0, 0, early=True)
            x_high(2, 0)
            relu(1, 1, early=True)
            with act.Fori(0, (SLOT_TILES - 3) // 2) as i:
                for s in range(2):
                    x_high(i * 2 + (3 + s), (1 + s) % 2)
                    relu(i * 2 + (2 + s), s)
            relu(SLOT_TILES - 1, (SLOT_TILES - 1) % 2)

        @block.tensor
        def _(pe):
            pe.wait_ge(consts_in, 16 * N_CONST)

            def turn_txt():
                pe.wait_ge(u_done, 1)
                for i in range(KD * 2):
                    kd, part = i // 2, i % 2
                    lo, hi_ = (0, 4) if part == 0 else (4, 5)
                    if i:
                        pe.wait_ge(ut_txt_done, i)
                    for k in range(lo, hi_):
                        ins = pe.transpose(ps_ut[:, (k - lo) * P:(k - lo + 1) * P], u_txt[:, k, kd * P:(kd + 1) * P],
                                           ident[:, :])
                    ins.then_inc(ut_txt, 1)
                pe.wait_ge(ut_txt_done, 2 * KD)
                pe.sem_inc(ut_psum, 1)

            def turn_u(b):
                pe.wait_ge(u_done, f_no(b))
                if b >= 1:
                    pe.wait_ge(ut_done, b)
                for kd in range(KD):
                    for a in range(2):
                        ins = pe.transpose(ps_ut[:, (2 * kd + a) * P:(2 * kd + a + 1) * P],
                                           u[b % 2][:, a, kd * P:(kd + 1) * P], ident[:, :])
                ins.then_inc(ut_psum, 1)

            def project_in(b):
                pe.wait_ge(ut_done, b + 1)
                if b >= 1:
                    pe.wait_ge(drive_done, b)
                for kd in range(KD):
                    pe.matmul(ps_v[:, 0:IMG], b_t[:, kd, :], u_t[:, kd, :, :].rearrange("p a c -> p (a c)"),
                              start=(kd == 0), stop=(kd == KD - 1))
                flat = u_t_txt.rearrange("p k a c -> p k (a c)")
                for kd in range(KD):
                    ins = pe.matmul(ps_v[:, IMG:L], b_t[:, kd, :], flat[:, kd, TXT * b:TXT * (b + 1)],
                                    start=(kd == 0), stop=(kd == KD - 1))
                ins.then_inc(v_psum, 1)

            def project_out(b):
                pe.wait_ge(turned_done, b + 1)
                if b >= 1:
                    pe.wait_ge(sum2_done, b)
                for a in range(2):
                    ins = pe.matmul(ps_y[:, a * D:(a + 1) * D], turned[:, a * P:(a + 1) * P], c_t, start=True, stop=True)
                ins.then_inc(y_psum, 1)

            def project_out_txt(i, tiles):
                if i == 0:
                    pe.wait_ge(turned_done, BATCH)
                pe.wait_ge(sum2_done, BATCH + i)
                for a, k in enumerate(tiles):
                    ins = pe.matmul(ps_y[:, a * D:(a + 1) * D], turned_txt[:, k * P:(k + 1) * P], c_t,
                                    start=True, stop=True)
                ins.then_inc(y_psum, 1)

            def logits(i, tiles, src, t0):
                if i >= 1:
                    pe.wait_ge(xnt_done, i)
                for kd in range(KD):
                    for a, k in enumerate(tiles):
                        ins = pe.transpose(ps_xnt[:, (2 * kd + a) * P:(2 * kd + a + 1) * P],
                                           src[:, k, kd * P:(kd + 1) * P], ident[:, :])
                ins.then_inc(xnt_psum, 1)
                pe.wait_ge(xnt_done, i + 1)
                for a, k in enumerate(tiles):
                    for kd in range(KD):
                        ins = pe.matmul(ps_logit[:, (t0 + a) * E:(t0 + a + 1) * E], xn_t[:, kd, a, :], gate_t[:, kd, :],
                                        start=(kd == 0), stop=(kd == KD - 1))
                ins.then_inc(logits_done, 1)

            turn_txt()
            for b in range(BATCH):
                turn_u(b)
                project_in(b)
                if b >= 1:
                    project_out(b - 1)
                    pe.wait_ge(xn_done, b_no(b - 1))
                    logits(b - 1, (0, 1), u[(b - 1) % 2], 2 * (b - 1))
            project_out(BATCH - 1)
            pe.wait_ge(xn_done, b_no(BATCH - 1))
            logits(BATCH - 1, (0, 1), u[(BATCH - 1) % 2], 2 * (BATCH - 1))
            for i, tiles in enumerate(((0, 1), (2, 3), (4,))):
                project_out_txt(i, tiles)
            pe.wait_ge(xn_done, b_no(TXTG))
            for i, tiles in enumerate(((0, 1), (2, 3), (4, 4))):
                logits(BATCH + i, tiles, u_txt, IMG_TILES + 2 * i)

            pe.wait_ge(picked_done, 1)
            flat = picked[:, :, :].rearrange("p e t -> p (e t)")
            pe.matmul(ps_rank[:, 0:NT * E], prefix_w[:, :], flat, start=True, stop=True)
            pe.matmul(ps_rank[:, NT * E:2 * NT * E], ones_w[:, :], flat, start=True, stop=True).then_inc(rank_psum, 1)
            pe.wait_ge(onehots_done, 2)
            for k in range(2 * NT):
                ins = pe.matmul(ps_slot[:, 0:SLOT_TILES], onehot_slot[:, k, :], onehot_tile[:, k, :],
                                start=(k == 0), stop=(k == 2 * NT - 1))
            ins.then_inc(slot_psum, 1)

            def turn_x(j, s, cycle, early=False):
                pe.wait_ge(x_here[s], cycle * 16 + 16)
                if not early:
                    pe.wait_ge(xlo_done, j - 1)
                for kd in range(KD):
                    ins = pe.transpose(ps_x[s][:, kd * P:(kd + 1) * P], x_slot[s][:, kd * P:(kd + 1) * P], ident[:, :])
                ins.then_inc(x_turned, 1)

            def product1(j, s, early=False):
                e = pe.value_load(tile_expert[0:1, bass.ds(j, 1)], min_val=0, max_val=E - 1)
                pe.wait_ge(xhi_done, j + 1)
                pe.wait_ge(xlo_done, j + 1)
                if not early:
                    pe.wait_ge(relu_done, j * 2 - 2)
                for c in range(KH):
                    o = ps_h[s][c // 4][:, (c % 4) * P:(c % 4 + 1) * P]
                    cols = slice(c * P, (c + 1) * P)
                    for kd in range(KD):
                        hi_w = w1_hi[:, bass.ds(e, 1), kd, cols].rearrange("p a c -> p (a c)")
                        lo_w = w1_lo[:, bass.ds(e, 1), kd, cols].rearrange("p a c -> p (a c)")
                        pe.matmul(o, hi_w, x_hi[s][:, kd, :], start=(kd == 0), stop=False)
                        pe.matmul(o, hi_w, x_lo[s][:, kd, :], start=False, stop=False)
                        ins = pe.matmul(o, lo_w, x_hi[s][:, kd, :], start=False, stop=(kd == KD - 1))
                    if c % 4 == 3:
                        ins.then_inc(mm1_done, 1)

            def product2(j, s, early=False):
                e = pe.value_load(tile_expert[0:1, bass.ds(j, 1)], min_val=0, max_val=E - 1)
                if not early:
                    pe.wait_ge(y_scaled, j - 1)
                for c in range(KH):
                    if c % 4 == 0:
                        pe.wait_ge(split_done, j * 2 + (c // 4 + 1))
                    hi_w = w2_hi[:, bass.ds(e, 1), c, :].rearrange("p a o -> p (a o)")
                    lo_w = w2_lo[:, bass.ds(e, 1), c, :].rearrange("p a o -> p (a o)")
                    o = ps_out[s][:, 0:D]
                    pe.matmul(o, h_hi[s][:, c, :], hi_w, start=(c == 0), stop=False)
                    pe.matmul(o, h_hi[s][:, c, :], lo_w, start=False, stop=False)
                    ins = pe.matmul(o, h_lo[s][:, c, :], hi_w, start=False, stop=(c == KH - 1))
                ins.then_inc(mm2_done, 1)

            pe.wait_ge(slots_done, 1)
            turn_x(0, 0, 0, early=True)
            turn_x(1, 1, 0, early=True)
            product1(0, 0, early=True)
            turn_x(2, 0, 1)
            product1(1, 1, early=True)
            product2(0, 0, early=True)
            turn_x(3, 1, 1)
            product1(2, 0)
            product2(1, 1, early=True)
            with pe.Fori(0, (SLOT_TILES - 5) // 2) as i:
                for s in range(2):
                    turn_x(i * 2 + (4 + s), s, i + 2)
                    product1(i * 2 + (3 + s), (1 + s) % 2)
                    product2(i * 2 + (2 + s), s)
            turn_x(SLOT_TILES - 1, 0, (SLOT_TILES - 1) // 2)
            product1(SLOT_TILES - 2, 1)
            product2(SLOT_TILES - 3, 0)
            product1(SLOT_TILES - 1, 0)
            product2(SLOT_TILES - 2, 1)
            product2(SLOT_TILES - 1, 0)

        @block.vector
        def _(dve):
            V = nc.vector
            n = [0]

            def link(ins):
                n[0] += 1
                ins.then_inc(v_step, 1)
                dve.wait_ge(v_step, n[0])

            def col(i):
                return ssm[:, i:i + 1]

            dve.wait_ge(consts_in, 16 * N_CONST)
            theta = small[:, 1:2]
            link(V.tensor_scalar(col(22), theta, 1.0 / TWO_PI, ROUND, ALU.mult, ALU.add))
            link(V.tensor_scalar(col(22), col(22), ROUND, None, ALU.subtract))
            link(V.scalar_tensor_tensor(col(23), col(22), -PI_A, theta, ALU.mult, ALU.add))
            link(V.scalar_tensor_tensor(col(23), col(22), -PI_B, col(23), ALU.mult, ALU.add))
            link(V.scalar_tensor_tensor(col(23), col(22), -PI_C, col(23), ALU.mult, ALU.add))
            link(V.tensor_scalar(col(20), col(23), 0.5, None, ALU.mult))
            V.tensor_scalar(col(21), col(20), TWO_PI / 4, None, ALU.add).then_inc(trig_in, 1)

            def stats(b, which, src, no):
                k, t0, _, _ = group(b)
                for a in range(k):
                    link(V.bn_stats(bst[:, a, :], src[:, a, :]))
                for a in range(k):
                    ins = V.bn_aggr(mv[:, which, t0 + a, :], bst[:, a, :])
                    if a < k - 1:
                        link(ins)
                ins.then_inc(stats_done[which], 1)

            def normalise(b, which, dst, src, signal, no):
                k, t0, _, _ = group(b)
                dve.wait_ge(rstd_done[which], no)
                for a in range(k):
                    ins = V.tensor_scalar(dst[:, a, :], src[:, a, :], mv[:, which, t0 + a, 0:1],
                                          rstd[:, which, t0 + a:t0 + a + 1], ALU.subtract, ALU.mult)
                    if a < k - 1:
                        link(ins)
                ins.then_inc(signal, 1)

            def diffs(b):
                dve.wait_ge(x_in, 32 * (b + 1))
                if b >= 1:
                    dve.wait_ge(sum_done, b)
                V.tensor_tensor(corner[:, 0, :, :], x_top[:, :, 0:D], x_below[:, :, 1:D + 1],
                                ALU.subtract).then_inc(diff_v, 1)

            def front(b):
                _, _, hb, ub = group(b)
                if b == TXTG:
                    dve.wait_ge(txt_in, 32)
                    dve.sem_inc(h_done, 1)
                else:
                    dve.wait_ge(sum_done, b + 1)
                    V.tensor_scalar(hb, hb, 1.0, None, ALU.min).then_inc(h_done, 1)
                    dve.wait_ge(h_done, f_no(b))
                stats(b, 0, hb, f_no(b))
                if b < BATCH - 1:
                    diffs(b + 1)
                if b >= 2 and b != TXTG:
                    dve.wait_ge(xn_out, 16 * b)
                    dve.wait_ge(logits_done, b - 1)
                normalise(b, 0, ub, hb, u_done, f_no(b))

            def recur(b):
                dve.wait_ge(v_psum, b + 1)
                if b == 0:
                    dve.wait_ge(tables_done, 1)
                V.tensor_tensor(drive, ps_v[:, 0:L], in_table, ALU.mult).then_inc(drive_done, 1)
                dve.wait_ge(drive_done, b + 1)
                if b >= 1:
                    dve.wait_ge(turned_done, b)
                V.tensor_tensor_scan(state, decay, drive, 0.0, ALU.mult, ALU.add).then_inc(state_done, 1)

            def add_y(b):
                _, _, hb, ub = group(b)
                dve.wait_ge(skip_done, f_no(b))
                if b == TXTG:
                    for i, (k0, k1) in enumerate(((0, 2), (2, 4), (4, 5))):
                        dve.wait_ge(y_psum, BATCH + i + 1)
                        V.tensor_tensor(ub[:, k0:k1, :], ub[:, k0:k1, :],
                                        ps_y[:, 0:(k1 - k0) * D].rearrange("p (a d) -> p a d", d=D),
                                        ALU.add).then_inc(sum2_done, 1)
                        dve.wait_ge(sum2_done, BATCH + i + 1)
                    return
                dve.wait_ge(y_psum, b + 1)
                V.tensor_tensor(ub, ub, ps_y[:, :].rearrange("p (a d) -> p a d", d=D), ALU.add).then_inc(sum2_done, 1)
                dve.wait_ge(sum2_done, b + 1)

            def back_a(b):
                _, _, hb, ub = group(b)
                add_y(b)
                stats(b, 1, ub, b_no(b))

            def back_b(b):
                _, _, hb, ub = group(b)
                normalise(b, 1, ub, ub, t_done, b_no(b))

            def back_c(b):
                _, _, hb, ub = group(b)
                dve.wait_ge(gamma_done, b_no(b))
                V.tensor_tensor(hb, hb, ub, ALU.add).then_inc(h1_done, 1)
                dve.wait_ge(h1_done, b_no(b))
                stats(b, 2, hb, b_no(b))

            def back_d(b):
                _, _, hb, ub = group(b)
                normalise(b, 2, ub, hb, xn_done, b_no(b))

            def weights_a(e):
                dve.wait_ge(w1_in, 16 * (e + 1))
                dve.wait_ge(w2_in, 16 * (e + 1))
                link(V.tensor_reduce(wmax[:, e, 0:1], w1_stage.rearrange("p k h -> p (k h)"), AX.X, ALU.max,
                                     apply_absolute_value=True))
                link(V.tensor_reduce(wmax[:, e, 1:2], w2_stage.rearrange("p k h -> p (k h)"), AX.X, ALU.max,
                                     apply_absolute_value=True))
                V.tensor_reduce(wmax[:, e, 2:3], b1_cols[:, e, :], AX.X, ALU.max,
                                apply_absolute_value=True).then_inc(max_w, 1)

            def weights_b(e):
                dve.wait_ge(max_all, e + 1)
                link(V.tensor_scalar(pow2[:, e, :].bitcast(I32), wmax_all[:, e, :].bitcast(I32), 0x7F800000, None,
                                     ALU.bitwise_and))
                link(V.tensor_scalar(pow2[:, e, :], pow2[:, e, :], TINY, 2.0 ** -13, ALU.max, ALU.mult))
                V.reciprocal(wsc[:, e, :], pow2[:, e, :]).then_inc(scale_done, 1)

            def weights_c(e):
                dve.wait_ge(hi1_done, e + 1)
                V.scalar_tensor_tensor(w1_lo[:, e, :, :], w1_stage, wsc[:, e, 0:1], w1_hi[:, e, :, :],
                                       ALU.mult, ALU.subtract).then_inc(lo1_done, 1)

            def tables():
                dve.wait_ge(trig_done, 1)
                s2, c2 = col(2), col(3)
                sin_1, cos_1 = col(4), col(5)
                link(V.tensor_tensor(sin_1, s2, c2, ALU.mult))
                link(V.tensor_scalar(sin_1, sin_1, 2.0, None, ALU.mult))
                link(V.tensor_tensor(cos_1, s2, s2, ALU.mult))
                link(V.tensor_scalar(cos_1, cos_1, -2.0, 1.0, ALU.mult, ALU.add))
                link(V.memset(cos_t[:, 0:1], 1.0))
                link(V.memset(sin_t[:, 0:1], 0.0))
                link(V.tensor_copy(cos_t[:, 1:2], cos_1))
                link(V.tensor_copy(sin_t[:, 1:2], sin_1))
                m = 1
                while m < L - 1:
                    cm, sm, f = cos_t[:, m:m + 1], sin_t[:, m:m + 1], col(6)
                    link(V.tensor_tensor(f, cm, cm, ALU.mult))
                    link(V.scalar_tensor_tensor(f, sm, sm, f, ALU.mult, ALU.add))
                    link(V.tensor_scalar(f, f, -0.5, 1.5, ALU.mult, ALU.add))
                    link(V.tensor_scalar(cm, cm, f, None, ALU.mult))
                    link(V.tensor_scalar(sm, sm, f, None, ALU.mult))
                    k = min(m, L - 1 - m)
                    c0, s0 = cos_t[:, 1:k + 1], sin_t[:, 1:k + 1]
                    c1, s1 = cos_t[:, m + 1:m + k + 1], sin_t[:, m + 1:m + k + 1]
                    tmp = out_table[:, 0:k]
                    link(V.tensor_copy(col(8), cm))
                    link(V.tensor_copy(col(9), sm))
                    link(V.tensor_scalar(tmp, s0, col(9), None, ALU.mult))
                    link(V.scalar_tensor_tensor(c1, c0, col(8), tmp, ALU.mult, ALU.subtract))
                    link(V.tensor_scalar(tmp, c0, col(9), None, ALU.mult))
                    link(V.scalar_tensor_tensor(s1, s0, col(8), tmp, ALU.mult, ALU.add))
                    m *= 2
                q, r = col(0), col(1)
                re, im, den, cr, ci = col(10), col(11), col(12), col(13), col(14)
                link(V.tensor_scalar(re, cos_1, r, -1.0, ALU.mult, ALU.add))
                link(V.tensor_scalar(im, sin_1, r, None, ALU.mult))
                link(V.tensor_tensor(den, q, q, ALU.mult))
                link(V.scalar_tensor_tensor(den, theta, theta, den, ALU.mult, ALU.add))
                link(V.reciprocal(den, den))
                link(V.tensor_tensor(cr, im, theta, ALU.mult))
                link(V.tensor_tensor(col(15), re, q, ALU.mult))
                link(V.tensor_tensor(cr, cr, col(15), ALU.subtract))
                link(V.tensor_tensor(cr, cr, den, ALU.mult))
                link(V.tensor_tensor(ci, im, q, ALU.mult))
                link(V.scalar_tensor_tensor(ci, re, theta, ci, ALU.mult, ALU.add))
                link(V.tensor_tensor(ci, ci, den, ALU.mult))
                link(V.tensor_scalar(ci, ci, -1.0, None, ALU.mult))
                top, bottom = small[:, 2:3], small[:, 3:4]
                p_, q_ = col(16), col(17)
                link(V.tensor_tensor(p_, ci, bottom, ALU.mult))
                link(V.scalar_tensor_tensor(p_, cr, top, p_, ALU.mult, ALU.add))
                link(V.tensor_tensor(q_, cr, bottom, ALU.mult))
                link(V.scalar_tensor_tensor(q_, ci, top, q_, ALU.mult, ALU.subtract))
                link(V.tensor_scalar(in_table, sin_t, q_, None, ALU.mult))
                link(V.scalar_tensor_tensor(in_table, cos_t, p_, in_table, ALU.mult, ALU.add))
                link(V.tensor_scalar(out_table, sin_t, bottom, None, ALU.mult))
                link(V.scalar_tensor_tensor(out_table, cos_t, top, out_table, ALU.mult, ALU.subtract))
                link(V.memset(decay, 1.0))
                V.tensor_scalar(decay, decay, r, None, ALU.mult).then_inc(tables_done, 1)

            link(V.memset(ones_f[:, :], 1.0))
            diffs(0)
            front(TXTG)
            tables()
            for b in range(BATCH):
                front(b)
                weights_a(b)
                if b >= 1:
                    back_a(b - 1)
                weights_b(b)
                if b >= 1:
                    back_b(b - 1)
                weights_c(b)
                if b >= 1:
                    back_c(b - 1)
                recur(b)
                if b >= 1:
                    back_d(b - 1)
            for b in (BATCH - 1, TXTG):
                back_a(b)
                back_b(b)
                back_c(b)
                back_d(b)

            P1, P2, PB = pow2[:, :, 0], pow2[:, :, 1], pow2[:, :, 2]
            bound, h_scale, relu_scale, y_scale = (hsc[:, i, :] for i in range(4))
            link(V.tensor_scalar(bound, P1, 2.0 ** 8, None, ALU.mult))
            link(V.tensor_tensor(bound, bound, PB, ALU.add))
            link(V.tensor_scalar(bound, bound, 2.0 ** 14, None, ALU.mult))
            link(V.tensor_scalar(bound.bitcast(I32), bound.bitcast(I32), 0x7F800000, None, ALU.bitwise_and))
            link(V.reciprocal(h_scale, bound))
            link(V.tensor_scalar(h_scale, h_scale, 2.0 ** 14, None, ALU.mult))
            link(V.tensor_tensor(relu_scale, h_scale, P1, ALU.mult))
            link(V.tensor_scalar(relu_scale, relu_scale, 1.0 / X_SCALE, None, ALU.mult))
            link(V.tensor_tensor(y_scale, bound, P2, ALU.mult))
            link(V.tensor_scalar(y_scale, y_scale, 2.0 ** -14, None, ALU.mult))
            link(V.tensor_tensor(b1_scaled[:, :, :], b1_cols[:, :, :],
                                 h_scale.rearrange("p (e a) -> p e a", a=1).broadcast_to([P, E, KH]), ALU.mult))

            def over_e(x):
                return x.rearrange("p (t a) -> p t a", a=1).broadcast_to([P, NT, E])

            def over_t(x):
                return x.rearrange("p (a e) -> p a e", a=1).broadcast_to([P, NT, E])

            dve.wait_ge(logits_done, BATCH + 3)
            logit = ps_logit[:, 0:NT * E].rearrange("p (t e) -> p t e", e=E)
            link(V.tensor_tensor(r_a[:, :, :], logit, over_t(gateb_row), ALU.add))
            link(V.tensor_reduce(tr[0][:, :], r_a[:, :, :], AX.X, ALU.max))
            V.tensor_tensor(r_a[:, :, :], r_a[:, :, :], over_e(tr[0][:, :]), ALU.subtract).then_inc(shifted, 1)
            dve.wait_ge(exped, 1)
            link(V.tensor_reduce(tr[0][:, :], r_b[:, :, :], AX.X, ALU.add))
            link(V.reciprocal(tr[1][:, :], tr[0][:, :]))
            link(V.tensor_tensor(r_b[:, :, :], r_b[:, :, :], over_e(tr[1][:, :]), ALU.mult))
            for c in range(TOPK):
                src = r_b if c == 0 else r_c
                link(V.tensor_reduce(tr[0][:, :], src[:, :, :], AX.X, ALU.max))
                link(V.tensor_tensor(r_a[:, :, :], src[:, :, :], over_e(tr[0][:, :]), ALU.is_equal))
                link(V.tensor_tensor(r_a[:, :, :], r_a[:, :, :], over_t(desc[:, :]), ALU.mult))
                link(V.tensor_reduce(tr[0][:, :], r_a[:, :, :], AX.X, ALU.max))
                link(V.tensor_tensor(pick[c][:, :, :], r_a[:, :, :], over_e(tr[0][:, :]), ALU.is_equal))
                if c == 0:
                    link(V.scalar_tensor_tensor(r_c[:, :, :], pick[0][:, :, :], -2.0, r_b[:, :, :], ALU.mult, ALU.add))
            link(V.tensor_tensor(r_c[:, :, :], pick[0][:, :, :], pick[1][:, :, :], ALU.add))
            V.tensor_tensor(r_a[:, :, :], r_b[:, :, :], r_c[:, :, :], ALU.mult).then_inc(gates_done, 1)
            V.tensor_tensor(picked[:, :, :].rearrange("p e t -> p t e"), r_c[:, :, :], over_e(valid[:, :]),
                            ALU.mult).then_inc(picked_done, 1)
            dve.wait_ge(rank_psum, 1)
            total = ps_rank[:, NT * E:2 * NT * E]
            cum, before = cmp8[:, 0:NT, :].rearrange("p a b -> p (a b)"), cmp8[:, NT:2 * NT, :].rearrange("p a b -> p (a b)")
            link(V.tensor_tensor_scan(cum, ones_f[:, :], total, 0.0, ALU.mult, ALU.add))
            link(V.tensor_tensor(before, cum, total, ALU.subtract))
            cum_e = cum.rearrange("p (e t) -> p e t", t=NT)
            before_e = before.rearrange("p (e t) -> p e t", t=NT)
            count, tiles, tiles_cum, base = (small[:, 32 + E * i:32 + E * (i + 1)] for i in range(4))
            link(V.tensor_tensor(count, cum_e[:, :, NT - 1], before_e[:, :, 0], ALU.subtract))
            link(V.tensor_scalar(tiles, count, 1.0 / P, 127.0 / 256.0, ALU.mult, ALU.add))
            link(V.tensor_scalar(tiles, tiles, ROUND, ROUND, ALU.add, ALU.subtract))
            link(V.tensor_tensor_scan(tiles_cum, ones_f[:, 0:E], tiles, 0.0, ALU.mult, ALU.add))
            link(V.tensor_tensor(base, tiles_cum, tiles, ALU.subtract))
            link(V.scalar_tensor_tensor(base, base, float(P), before_e[:, :, 0], ALU.mult, ALU.subtract))
            link(V.tensor_tensor(before, before, ps_rank[:, 0:NT * E], ALU.add))
            slot_of = r_c[:, :, :]
            link(V.tensor_tensor(slot_of, before_e.rearrange("p e t -> p t e"), over_t(base), ALU.add))
            for c in range(TOPK):
                link(V.tensor_tensor(pick[c][:, :, :], pick[c][:, :, :], slot_of, ALU.mult))
                link(V.tensor_reduce(slot_f[:, c, :], pick[c][:, :, :], AX.X, ALU.add))
            link(V.tensor_scalar(tile_f[:, :, :], slot_f[:, :, :], 1.0 / P, -127.0 / 256.0, ALU.mult, ALU.add))
            link(V.tensor_scalar(tile_f[:, :, :], tile_f[:, :, :], ROUND, ROUND, ALU.add, ALU.subtract))
            link(V.scalar_tensor_tensor(within_f[:, :, :], tile_f[:, :, :], -float(P), slot_f[:, :, :],
                                        ALU.mult, ALU.add))
            link(V.tensor_tensor(cmp8[:, :, :], iota_tile[:, :].rearrange("p (t a) -> p t a", a=1)
                                 .broadcast_to([P, SLOT_TILES, E]),
                                 tiles_cum.rearrange("p (a e) -> p a e", a=1).broadcast_to([P, SLOT_TILES, E]),
                                 ALU.is_ge))
            ends = small[:, 128:128 + SLOT_TILES]
            link(V.tensor_reduce(ends, cmp8[:, :, :], AX.X, ALU.add))
            link(V.tensor_scalar(tile_expert[:, :], ends, float(E - 1), None, ALU.min))
            dve.wait_ge(xn_out, 16 * (1 + BATCH))
            for c in range(TOPK):
                k = slice(c * NT, (c + 1) * NT)
                V.tensor_tensor(onehot_slot[:, k, :], iota_slot[:, :].rearrange("p (a r) -> p a r", a=1)
                                .broadcast_to([P, NT, P]),
                                within_f[:, c, :].rearrange("p (t a) -> p t a", a=1).broadcast_to([P, NT, P]),
                                ALU.is_equal)
                for tt in range(NT):
                    ins = V.tensor_scalar(onehot_tile[:, c * NT + tt, :], iota_tile[:, :], tile_f[:, c, tt:tt + 1],
                                          token_val[:, tt:tt + 1], ALU.is_equal, ALU.mult)
                ins.then_inc(onehots_done, 1)
            dve.wait_ge(slot_psum, 1)
            val, is_pos, is_pad = ps_slot[:, 0:SLOT_TILES], small[:, 192:192 + SLOT_TILES], small[:, 256:256 + SLOT_TILES]
            tok = small[:, 320:320 + SLOT_TILES]
            link(V.tensor_scalar(is_pos, val, 0.0, None, ALU.is_gt))
            link(V.tensor_scalar(is_pad, val, 0.0, pad_row[:, 0:1], ALU.is_equal, ALU.mult))
            link(V.scalar_tensor_tensor(tok, val, float(MID), is_pos, ALU.add, ALU.subtract))
            V.tensor_tensor(slot_token[:, :], tok, is_pad, ALU.add).then_inc(slots_done, 1)

            def x_low(j, s, early=False):
                dve.wait_ge(xhi_done, j + 1)
                if not early:
                    dve.wait_ge(mm1_done, j * 2 - 2)
                V.scalar_tensor_tensor(x_lo[s], ps_x[s][:, 0:D].rearrange("p (k c) -> p k c", k=KD), X_SCALE, x_hi[s],
                                       ALU.mult, ALU.subtract).then_inc(xlo_done, 1)

            def split(j, s, early=False):
                if not early:
                    dve.wait_ge(mm2_done, j - 1)
                for half in range(2):
                    dve.wait_ge(relu_done, j * 2 + (half + 1))
                    a = h_act[s][:, half * 512:(half + 1) * 512].rearrange("p (k c) -> p k c", c=P)
                    k = slice(4 * half, 4 * half + 4)
                    V.tensor_copy(h_hi[s][:, k, :], a).then_inc(hi_done, 1)
                    dve.wait_ge(hi_done, j * 2 + (half + 1))
                    V.tensor_tensor(h_lo[s][:, k, :], a, h_hi[s][:, k, :], ALU.subtract).then_inc(split_done, 1)

            def weigh(j, s, cycle, early=False):
                e = dve.value_load(tile_expert[0:1, bass.ds(j, 1)], min_val=0, max_val=E - 1)
                dve.wait_ge(mm2_done, j + 1)
                V.scalar_tensor_tensor(y_slot[s], ps_out[s][:, 0:D], hsc[:, 3, bass.ds(e, 1)],
                                       b2_rows[:, bass.ds(e, 1), :].rearrange("p a d -> p (a d)"),
                                       ALU.mult, ALU.add).then_inc(y_scaled, 1)
                dve.wait_ge(y_scaled, j + 1)
                dve.wait_ge(g_here[s], cycle * 16 + 16)
                if not early:
                    dve.wait_ge(y_out, j * 16 - 16)
                V.tensor_scalar(y_gated[s], y_slot[s], gate_slot[s][:, bass.ds(e, 1)], None,
                                ALU.mult).then_inc(y_done, 1)

            dve.wait_ge(b2_in, 16)
            x_low(0, 0, early=True)
            x_low(1, 1, early=True)
            split(0, 0, early=True)
            x_low(2, 0)
            split(1, 1, early=True)
            weigh(0, 0, 0, early=True)
            x_low(3, 1)
            split(2, 0)
            weigh(1, 1, 0, early=True)
            with dve.Fori(0, (SLOT_TILES - 5) // 2) as i:
                for s in range(2):
                    x_low(i * 2 + (4 + s), s)
                    split(i * 2 + (3 + s), (1 + s) % 2)
                    weigh(i * 2 + (2 + s), s, i + 1)
            x_low(SLOT_TILES - 1, 0)
            split(SLOT_TILES - 2, 1)
            weigh(SLOT_TILES - 3, 0, (SLOT_TILES - 3) // 2)
            split(SLOT_TILES - 1, 0)
            weigh(SLOT_TILES - 2, 1, (SLOT_TILES - 2) // 2)
            weigh(SLOT_TILES - 1, 0, (SLOT_TILES - 1) // 2)


def kernel(x, txt, L0_attn_log_neg_real, L0_attn_imag, L0_attn_B_mat, L0_attn_C_mat, L0_attn_D, L0_attn_gamma,
           L0_attn_beta, L0_ffn_gate_w, L0_ffn_gate_b, L0_ffn_w1, L0_ffn_b1, L0_ffn_w2, L0_ffn_b2):
    import ml_dtypes
    import numpy as np
    import concourse.bacc as bacc
    from concourse.bass_utils import run_bass_kernel_spmd

    f = np.float32
    a = np.asarray

    def rows(v):
        return np.broadcast_to(a(v).reshape(1, -1), (P, a(v).size)).copy()

    tok = np.zeros((P, NT), np.int64)
    real = np.ones((P, NT), bool)
    for k in range(IMG_TILES):
        tok[:, k] = (k // 2) * L + (k % 2) * P + np.arange(P)
    for k in range(TXT_TILES):
        flat = k * P + np.arange(P)
        real[:, IMG_TILES + k] = flat < NTXT
        tok[:, IMG_TILES + k] = np.where(flat < NTXT, (flat // TXT) * L + IMG + flat % TXT, NTOK + np.arange(P))
    half = (np.arange(P) < STATE)
    cols = np.zeros((P, 16), f)
    cols[:, 0] = np.tile(a(L0_attn_log_neg_real), 2)
    cols[:, 1] = np.tile(a(L0_attn_imag), 2)
    cols[:, 2] = half
    cols[:, 3] = ~half
    ts = {
        "x": np.pad(a(x)[:, 0], ((0, 0), (0, 1), (0, 1))),
        "txt": a(txt).reshape(NTXT, D),
        "ident": np.eye(P, dtype=f),
        "cols": cols,
        "b1": a(L0_ffn_b1).reshape(E, KH, P).transpose(2, 0, 1).copy(),
        "b_t": np.concatenate([a(L0_attn_B_mat).T] * 2, 1).reshape(KD, P, P).transpose(1, 0, 2).copy(),
        "c_t": np.concatenate([a(L0_attn_C_mat).T] * 2, 0),
        "gate_t": a(L0_ffn_gate_w).T.reshape(KD, P, E).transpose(1, 0, 2).copy(),
        "d_row": rows(L0_attn_D), "gamma_row": rows(L0_attn_gamma), "beta_row": rows(L0_attn_beta),
        "gateb_row": rows(L0_ffn_gate_b),
        "txt_rows": tok[:, IMG_TILES:].astype(np.uint32),
        "iota_slot": rows(np.arange(P, dtype=np.float16)),
        "iota_tile": rows(np.arange(SLOT_TILES, dtype=f)),
        "token_val": np.where(real, np.where(tok < MID, tok - MID, tok - MID + 1), 0).astype(f),
        "valid": real.astype(f),
        "prefix_w": np.triu(np.ones((P, P)), 1).astype(ml_dtypes.bfloat16),
        "ones_w": np.ones((P, P), ml_dtypes.bfloat16),
        "desc": rows(np.arange(E, 0, -1, dtype=f)),
        "pad_row": (NTOK - MID + np.arange(P, dtype=f)).reshape(P, 1),
        "mhalf": np.full((P, TXT_TILES), -0.5, f),
        "b2": rows(L0_ffn_b2).reshape(P, E, D),
        "w1": a(L0_ffn_w1), "w2": a(L0_ffn_w2),
    }
    ts = {k: np.ascontiguousarray(v) for k, v in ts.items()}
    nc = bacc.Bacc("TRN2", target_bir_lowering=False, num_devices=1)
    aps = {k: nc.dram_tensor(f"in_{k}", v.shape, mybir.dt.from_np(v.dtype), kind="ExternalInput").ap()
           for k, v in ts.items()}
    out = nc.dram_tensor("out", (ROWS, D), F32, kind="ExternalOutput").ap()
    build(nc, aps, out)
    r = run_bass_kernel_spmd(nc, [{f"in_{k}": v for k, v in ts.items()}], core_ids=[0])
    return r.results[0]["out"][:NTOK].reshape(BATCH, L, D)
```

```python
from contextlib import ExitStack

import concourse.bass as bass
from concourse import mybir

F32, F16, BF16 = mybir.dt.float32, mybir.dt.float16, mybir.dt.bfloat16
I32, U32 = mybir.dt.int32, mybir.dt.uint32
ALU, ACT, AX = mybir.AluOpType, mybir.ActivationFunctionType, mybir.AxisListType

P = 128
BATCH, IMG, TXT, D = 8, 256, 77, 256
L = IMG + TXT
NTOK = BATCH * L
NTXT = BATCH * TXT
IMG_TILES = BATCH * IMG // P
TXT_TILES = -(-NTXT // P)
TXT_LAST = NTXT - (TXT_TILES - 1) * P
NT = IMG_TILES + TXT_TILES
STATE = 64
E, HID, TOPK = 8, 1024, 2
KD, KH = D // P, HID // P
SLOT_TILES = (TOPK * NTOK + E * (P - 1)) // P
ROWS = NTOK + P
MID = NTOK // 2
XW = D + E
EPS = 1e-5
TWO_PI = 6.283185307179586
PI_A = 6.28125
PI_B = 0.0019350051879882812
PI_C = TWO_PI - PI_A - PI_B
ROUND = 12582912.0
X_SCALE = 2.0 ** 9
TINY = 2.0 ** -60
UNROLL = 8
PEEL = 2
LOOPS = (SLOT_TILES - PEEL - 3) // UNROLL
REST = range(PEEL + LOOPS * UNROLL, SLOT_TILES)


def build(nc, t, out):
    with ExitStack() as ctx:
        def sb(name, shape, dt=F32):
            return ctx.enter_context(nc.sbuf_tensor(name, shape, dt))

        def sem(name):
            return ctx.enter_context(nc.semaphore(name))

        w1_parts = sb("w1_parts", [P, E, 2, KD, HID], F16)
        w2_parts = sb("w2_parts", [P, E, KH, 2, D], F16)
        b1_cols = sb("b1_cols", [P, E, KH])
        b1_scaled = sb("b1_scaled", [P, E, KH])
        ident = sb("ident", [P, P])
        small = sb("small", [P, 384])
        slot_token = sb("slot_token", [P, SLOT_TILES], U32)
        tile_expert = sb("tile_expert", [P, SLOT_TILES], I32)
        token_index = sb("token_index", [P, 4], U32)
        ARENA = 18216
        arena = sb("arena", [P, ARENA])
        cursor = [0]

        def take(*shape, dt=F32, bytes_each=4):
            n = 1
            for k in shape:
                n *= k
            words = -(-n * bytes_each // 4)
            a = arena[:, cursor[0]:cursor[0] + words]
            cursor[0] += words
            assert cursor[0] <= ARENA, cursor[0]
            if dt != F32:
                a = a.bitcast(dt)
            if len(shape) == 1:
                return a
            names = "abcd"[:len(shape)]
            return a.rearrange(f"p ({' '.join(names)}) -> p {' '.join(names)}", **dict(zip(names, shape)))

        w1_buf = [take(KD, HID), w1_parts[:, E - 1].rearrange("p a k h -> p (a k h)").bitcast(F32)
                  .rearrange("p (k h) -> p k h", k=KD)]
        w2_buf = [take(KH, D), w2_parts[:, E - 1].rearrange("p k a o -> p (k a o)").bitcast(F32)
                  .rearrange("p (k o) -> p k o", k=KH)]

        def w_buf(e):
            return e % 2 if e < E - 1 else 0

        def w_turn(e):
            return e // 2 + 1 if e < E - 1 else E // 2 + 1

        def w1_stage(e):
            return w1_buf[w_buf(e)]

        def w2_stage(e):
            return w2_buf[w_buf(e)]

        x_top = take(2, D + 1)
        x_below = take(2, D + 1)
        corner = take(2, 2, D)
        h = [take(2, D) for _ in range(3)]
        u = [take(2, D) for _ in range(3)]
        u_t = take(KD, 2, P)
        xn_t = take(KD, 2, P)
        h_txt = take(TXT_TILES, D)
        u_txt = take(TXT_TILES, D)
        u_t_txt = take(KD, TXT_TILES, P)
        tables_at = cursor[0]
        in_table = take(L)
        out_table = take(L)
        decay = take(L)
        drive = take(L)
        state = take(L)
        tables_end = cursor[0]
        turned = take(IMG)
        turned_txt = take(TXT_TILES * P)
        b_t = take(KD, P)
        c_t = take(D)
        gate_t = take(KD, E)
        d_row = take(D)
        gamma_row = take(D)
        beta_row = take(D)
        gateb_row = take(E)
        zeros = take(XW)
        cursor[0] = tables_at
        cmp8 = take(SLOT_TILES, E)
        r_a, r_b, r_c = (take(NT, E) for _ in range(3))
        pick = [take(NT, E) for _ in range(2)]
        assert cursor[0] <= tables_end
        cursor[0] = 0
        onehot_slot = take(2 * NT, P, dt=F16, bytes_each=2)
        onehot_tile = take(2 * NT, SLOT_TILES, dt=F16, bytes_each=2)
        cursor[0] = 0
        h_act = [take(HID) for _ in range(2)]
        h_hi = [take(KH, P, dt=F16, bytes_each=2) for _ in range(2)]
        h_lo = [take(KH, P, dt=F16, bytes_each=2) for _ in range(2)]
        cursor[0] = max(cursor[0], 2 * NT * (P + SLOT_TILES) // 2)
        x_slot = [take(XW) for _ in range(2)]
        x_hi = [take(KD, P, dt=F16, bytes_each=2) for _ in range(2)]
        x_lo = [take(KD, P, dt=F16, bytes_each=2) for _ in range(2)]
        y_slot = [take(D) for _ in range(2)]
        y_gated = [take(D) for _ in range(2)]
        gate_slot = [take(E) for _ in range(2)]
        b2_rows = take(E, D)
        iota_slot = sb("iota_slot", [P, P], F16)
        iota_tile = sb("iota_tile", [P, SLOT_TILES])
        token_val = sb("token_val", [P, NT])
        valid = sb("valid", [P, NT])
        prefix_w = sb("prefix_w", [P, P], BF16)
        ones_w = sb("ones_w", [P, P], BF16)
        picked = sb("picked", [P, E, NT], BF16)
        ones_f = sb("ones_f", [P, NT * E])
        desc = sb("desc", [P, E])
        pad_row = sb("pad_row", [P, 1])
        mv = sb("mv", [P, 3, NT, 2])
        rstd = sb("rstd", [P, 3, NT])
        vpe = sb("vpe", [P, 3, NT])
        shift = sb("shift", [P, NT])
        bst = sb("bst", [P, TXT_TILES, 6])
        mhalf = sb("mhalf", [P, TXT_TILES])
        tr = [sb(f"tr{i}", [P, NT]) for i in range(3)]
        slot_f = sb("slot_f", [P, TOPK, NT])
        tile_f = sb("tile_f", [P, TOPK, NT])
        within_f = sb("within_f", [P, TOPK, NT], F16)
        tile_h = sb("tile_h", [P, TOPK, NT])
        ssm = sb("ssm", [P, 40])
        wmax = sb("wmax", [P, E, 3])
        wmax_all = sb("wmax_all", [P, E, 3])
        pow2 = sb("pow2", [P, E, 3])
        wsc = sb("wsc", [P, E, 3])
        hsc = sb("hsc", [P, 4, E])
        cos_t = drive
        sin_t = state

        bank = [ctx.enter_context(nc.psum_tensor(f"bank{i}", [P, 512], F32)) for i in range(8)]
        ps_ut, ps_v, ps_xnt, ps_logit, ps_rank, ps_slot = (bank[i] for i in (0, 1, 3, 4, 5, 6))
        ps_y = [bank[2], bank[7]]
        ps_h = [[bank[0], bank[1]], [bank[2], bank[3]]]
        ps_out = bank[4:6]
        ps_x = bank[6:8]

        xn_dram = nc.dram_tensor("xn_rows", [ROWS, XW], F32, kind="Internal").ap()

        cols_in, consts_in, consts2_in = sem("cols_in"), sem("consts_in"), sem("consts2_in")
        txt_in = sem("txt_in")
        x_in = sem("x_in")
        w1_in, w2_in = ([sem(f"w{w}_in{i}") for i in range(2)] for w in (1, 2))
        v_step = sem("v_step")
        p_step = sem("p_step")
        a_step = sem("a_step")
        zeroed = sem("zeroed")
        txt_zeroed = sem("txt_zeroed")
        trig_in = sem("trig_in")
        trig_done = sem("trig_done")
        tables_done = sem("tables_done")
        diff_v, diff_p, abs_done, sum_done = sem("diff_v"), sem("diff_p"), sem("abs_done"), sem("sum_done")
        h_done = sem("h_done")
        stats_done = [sem(f"stats_done{i}") for i in range(3)]
        rstd_done = [sem(f"rstd_done{i}") for i in range(3)]
        u_done = sem("u_done")
        ut_txt, ut_txt_done = sem("ut_txt"), sem("ut_txt_done")
        ut_psum, ut_done = sem("ut_psum"), sem("ut_done")
        skip_done = sem("skip_done")
        v_psum, state_done = sem("v_psum"), sem("state_done")
        drive_done = sem("drive_done")
        turned_done = sem("turned_done")
        y_psum, sum2_done = sem("y_psum"), sem("sum2_done")
        t_done, gamma_done, beta_done = sem("t_done"), sem("gamma_done"), sem("beta_done")
        h1_done, h1_out = sem("h1_done"), [sem(f"h1_out{i}") for i in range(3)]
        xn_done, xn_out = sem("xn_done"), [sem(f"xn_out{i}") for i in range(3)]
        rest_out = sem("rest_out")
        xnt_psum, xnt_done = sem("xnt_psum"), sem("xnt_done")
        logits_done = sem("logits_done")
        squares_done, max_all = sem("squares_done"), sem("max_all")
        b1_max = sem("b1_max")
        scale_done = sem("scale_done")
        hi1_done, hi2_done = sem("hi1_done"), sem("hi2_done")
        lo1_done, lo2_done = sem("lo1_done"), sem("lo2_done")
        shifted, exped = sem("shifted"), sem("exped")
        gates_done, gates_out = sem("gates_done"), sem("gates_out")
        picked_done, rank_psum = sem("picked_done"), sem("rank_psum")
        onehots_done, onehot_pool, slot_psum = sem("onehots_done"), sem("onehot_pool"), sem("slot_psum")
        slots_done = sem("slots_done")
        b2_in = sem("b2_in")
        held = sem("held")
        x_idx, y_idx = sem("x_idx"), sem("y_idx")
        tile_onehot = sem("tile_onehot")
        x_here = [sem(f"x_here{i}") for i in range(2)]
        gates_kept = sem("gates_kept")
        x_turned = sem("x_turned")
        xhi_done, xlo_done = sem("xhi_done"), sem("xlo_done")
        mm1_done, relu_done, split_done = sem("mm1_done"), sem("relu_done"), sem("split_done")
        hi_done = sem("hi_done")
        mm2_done, y_half, y_scaled, y_done = sem("mm2_done"), sem("y_half"), sem("y_scaled"), sem("y_done")
        y_out = sem("y_out")

        N_CONST, N_CONST2 = 8, 10
        TXTG = "text"

        PARTS = {"t0": (0, 2), "t1": (2, 4), "t2": (4, 5)}
        BACKS = {b + 1: [b] for b in range(BATCH)}
        for part, (k0, k1) in PARTS.items():
            BACKS[-(-min(k1 * P, NTXT) // TXT)].append(part)
        BACK = [g for step in sorted(BACKS) for g in BACKS[step]]
        FRONT = [TXTG] + list(range(BATCH))

        def group(g):
            if g == TXTG:
                return TXT_TILES, IMG_TILES, h_txt, u_txt
            if g in PARTS:
                k0, k1 = PARTS[g]
                return k1 - k0, IMG_TILES + k0, h_txt[:, k0:k1, :], u_txt[:, k0:k1, :]
            return 2, 2 * g, h[g % 3], u[g % 3]

        def f_no(g):
            return 1 if g in PARTS else FRONT.index(g) + 1

        def b_no(g):
            return BACK.index(g) + 1

        def segments(g):
            k0, k1 = PARTS[g]
            for k in range(k0, k1):
                for b in range(BATCH):
                    lo, hi_ = max(k * P, b * TXT), min((k + 1) * P, (b + 1) * TXT)
                    if lo < hi_:
                        yield k, lo - k * P, hi_ - k * P, b * L + IMG + lo - b * TXT

        N_SEG = sum(len(list(segments(g))) for g in PARTS)

        def wait_rows_out(eng):
            for i in range(3):
                eng.wait_ge(h1_out[i], 16 * len(range(i, BATCH, 3)))
                eng.wait_ge(xn_out[i], 16 * len(range(i, BATCH, 3)))
            eng.wait_ge(rest_out, 16 * (2 + 2 * N_SEG))

        def over_slots(x):
            return x.rearrange("p (a j) -> p a j", a=1).broadcast_to([P, NT, SLOT_TILES])

        def per_token(x):
            return x.rearrange("p (t a) -> p t a", a=1).broadcast_to([P, NT, SLOT_TILES])

        block = ctx.enter_context(nc.Block())


        @block.sync
        def _(sp):
            sp.dma_start(small[:, 0:16], t["cols"]).then_inc(cols_in, 16)

            def load_x(b):
                if b >= 1:
                    sp.wait_ge(diff_v, b)
                    sp.wait_ge(diff_p, b)
                sp.dma_start(x_top, t["x"][b, 0:IMG, :].rearrange("(k p) w -> p k w", p=P)).then_inc(x_in, 16)
                sp.dma_start(x_below, t["x"][b, 1:IMG + 1, :].rearrange("(k p) w -> p k w", p=P)).then_inc(x_in, 16)

            def frees(e):
                return e - 1 if e < E - 1 else e

            def load_w1(e):
                if e >= 2:
                    sp.wait_ge(lo1_done, frees(e))
                sp.dma_start(w1_stage(e), t["w1"][e].rearrange("(k p) h -> p k h", p=P)).then_inc(w1_in[w_buf(e)], 16)

            def load_w2(e):
                if e >= 2:
                    sp.wait_ge(lo2_done, frees(e))
                sp.dma_start(w2_stage(e), t["w2"][e].rearrange("(k p) o -> p k o", p=P)).then_inc(w2_in[w_buf(e)], 16)

            load_x(0)
            sp.wait_ge(txt_zeroed, 1)
            sp.dma_start(h_txt[:, 0:TXT_TILES - 1, :],
                         t["txt"][0:(TXT_TILES - 1) * P].rearrange("(k p) d -> p k d", p=P)).then_inc(txt_in, 16)
            sp.dma_start(h_txt[0:TXT_LAST, TXT_TILES - 1, :], t["txt"][(TXT_TILES - 1) * P:NTXT]).then_inc(txt_in, 16)
            load_w1(0)
            load_w2(0)
            load_x(1)
            load_w1(1)
            load_w2(1)
            sp.wait_ge(zeroed, 1)
            sp.dma_start(out[NTOK:ROWS, :], zeros[:, 0:D]).then_inc(rest_out, 16)
            sp.dma_start(xn_dram[NTOK:ROWS, :], zeros).then_inc(rest_out, 16)

            def store(g, dst, src, txt_src, ready, signal):
                sp.wait_ge(ready, b_no(g))
                if g in PARTS:
                    for k, p0, p1, row in segments(g):
                        sp.dma_start(dst[row:row + p1 - p0, 0:D], txt_src[p0:p1, k, :]).then_inc(rest_out, 16)
                else:
                    sp.dma_start(dst[L * g:L * g + IMG, 0:D].rearrange("(k p) d -> p k d", p=P),
                                 src(g)).then_inc(signal[g % len(signal)], 16)

            for step in range(BATCH + 2):
                if step + 3 < BATCH + 1:
                    load_x(step + 2)
                for g in BACKS.get(step - 1, []):
                    store(g, xn_dram, lambda b: u[b % 3], u_txt, xn_done, xn_out)
                nxt = step + 2 if step + 2 < E - 1 else E - 1 if step == E - 2 else None
                if nxt is not None:
                    load_w1(nxt)
                    load_w2(nxt)
                for g in BACKS.get(step, []):
                    store(g, out, lambda b: h[b % 3], h_txt, h1_done, h1_out)
            sp.wait_ge(gates_done, 1)
            gates_at = xn_dram[0:NTOK, D:XW].rearrange("(b l) e -> b l e", b=BATCH)
            for b in range(BATCH):
                sp.dma_start(gates_at[b, 0:IMG, :].rearrange("(k p) e -> p k e", p=P),
                             r_a[:, 2 * b:2 * b + 2, :]).then_inc(gates_out, 16)
            wait_rows_out(sp)
            sp.dma_start(b2_rows, t["b2"]).then_inc(b2_in, 16)


        @block.gpsimd
        def _(pool):
            G = nc.gpsimd
            n = [0]

            def link(ins):
                n[0] += 1
                ins.then_inc(p_step, 1)
                pool.wait_ge(p_step, n[0])

            def per_column(x, k):
                return x.rearrange("p (a d) -> p a d", a=1).broadcast_to([P, k, D])

            G.memset(h_txt[96:P, TXT_TILES - 1, :], 0.0).then_inc(txt_zeroed, 1)
            pool.wait_ge(txt_zeroed, 1)
            G.memset(zeros, 0.0).then_inc(zeroed, 1)
            pool.wait_ge(zeroed, 1)
            link(G.memset(turned_txt[:, NTXT:], 0.0))
            link(G.memset(mhalf[:, :], -0.5))

            def rstd_of(g, which, no):
                k, t0, _, _ = group(g)
                pool.wait_ge(stats_done[which], no)
                link(G.tensor_scalar(vpe[:, which, t0:t0 + k], mv[:, which, t0:t0 + k, 1], EPS, None, ALU.add))
                ins = G.tensor_tensor(rstd[:, which, t0:t0 + k], vpe[:, which, t0:t0 + k], mhalf[:, 0:k], ALU.pow)
                if which < 2:
                    ins.then_inc(rstd_done[which], 1)
                    return
                link(ins)
                link(G.tensor_scalar(vpe[:, which, t0:t0 + k], mv[:, which, t0:t0 + k, 0], -1.0, None, ALU.mult))
                G.tensor_tensor(shift[:, t0:t0 + k], vpe[:, which, t0:t0 + k], rstd[:, which, t0:t0 + k],
                                ALU.mult).then_inc(rstd_done[which], 1)

            def diffs(b):
                pool.wait_ge(x_in, 32 * (b + 1))
                if b >= 1:
                    pool.wait_ge(sum_done, b)
                G.tensor_tensor(corner[:, 1, :, :], x_below[:, :, 0:D], x_top[:, :, 1:D + 1],
                                ALU.subtract).then_inc(diff_p, 1)

            def sums(b):
                pool.wait_ge(abs_done, b + 1)
                if b >= 3:
                    pool.wait_ge(h1_out[b % 3], 16 * (b // 3))
                    pool.wait_ge(xn_done, b_no(b - 3))
                G.tensor_tensor(h[b % 3], corner[:, 0, :, :], corner[:, 1, :, :], ALU.add).then_inc(sum_done, 1)

            def skip(g):
                k, _, _, ug = group(g)
                pool.wait_ge(u_done, f_no(g))
                pool.wait_ge(ut_psum, f_no(g))
                G.tensor_tensor(ug, ug, per_column(d_row, k), ALU.mult).then_inc(skip_done, 1)

            def add_beta(g):
                k, _, hg, _ = group(g)
                pool.wait_ge(u_done, f_no(g))
                G.tensor_tensor(hg, hg, per_column(beta_row, k), ALU.add).then_inc(beta_done, 1)

            def turn(b):
                pool.wait_ge(state_done, b + 1)
                if b >= 1:
                    pool.wait_ge(y_psum, b_no(b - 1))
                link(G.tensor_tensor(turned, state[:, 0:IMG], out_table[:, 0:IMG], ALU.mult))
                G.tensor_tensor(turned_txt[:, TXT * b:TXT * (b + 1)], state[:, IMG:L], out_table[:, IMG:L],
                                ALU.mult).then_inc(turned_done, 1)

            def gamma(g):
                k, _, _, ug = group(g)
                pool.wait_ge(t_done, b_no(g))
                G.tensor_tensor(ug, ug, per_column(gamma_row, k), ALU.mult).then_inc(gamma_done, 1)

            def largest(e):
                pool.wait_ge(squares_done, 2 * (e + 1))
                if e == 0:
                    pool.wait_ge(b1_max, 1)
                G.partition_all_reduce(wmax_all[:, e, :], wmax[:, e, :], P,
                                       bass.bass_isa.ReduceOp.max).then_inc(max_all, 1)

            diffs(0)
            pool.wait_ge(consts_in, 16 * N_CONST)
            link(G.tensor_scalar(d_row, d_row, 1.0, None, ALU.add))
            sums(0)
            diffs(1)
            rstd_of(TXTG, 0, 1)
            rstd_of(0, 0, 2)
            largest(0)
            skip(TXTG)
            add_beta(TXTG)
            for step in range(BATCH + 1):
                front, backs = step < BATCH, BACKS.get(step, [])
                if front:
                    skip(step)
                for g in backs:
                    rstd_of(g, 1, b_no(g))
                if front:
                    add_beta(step)
                for g in backs:
                    gamma(g)
                if front:
                    turn(step)
                if step + 1 < BATCH:
                    sums(step + 1)
                if step + 2 < BATCH:
                    diffs(step + 2)
                for g in backs:
                    rstd_of(g, 2, b_no(g))
                if step + 1 < BATCH:
                    rstd_of(step + 1, 0, f_no(step + 1))
                if step + 1 < E - 1:
                    largest(step + 1)
                if step == E - 1:
                    largest(E - 1)

            pool.wait_ge(consts2_in, 16 * N_CONST2)
            pool.wait_ge(tile_onehot, 1)
            k2 = slice(NT, 2 * NT)
            G.tensor_tensor(onehot_tile[:, k2, :], onehot_tile[:, k2, :], per_token(token_val[:, :]),
                            ALU.mult).then_inc(onehot_pool, 1)

            def hold():
                pool.sem_inc(held, 1)

            def gather_x(j, s):
                G.tensor_copy(token_index[:, s:s + 1], slot_token[:, bass.ds(j, 1)]).then_inc(x_idx, 1)
                pool.wait_ge(x_idx, j + 1)
                hold()
                G.indirect_dma_start(x_slot[s], None, xn_dram,
                                     bass.IndirectOffsetOnAxis(ap=token_index[:, s:s + 1], axis=0)
                                     ).then_inc(x_here[s], 16)

            def scatter(j, s, first=False):
                G.tensor_copy(token_index[:, 2 + s:3 + s], slot_token[:, bass.ds(j, 1)]).then_inc(y_idx, 1)
                pool.wait_ge(y_idx, j + 1)
                hold()
                pool.wait_ge(y_done, j + 1)
                hold()
                if not first:
                    pool.wait_ge(y_out, j * 16)
                    hold()
                G.indirect_dma_start(out, bass.IndirectOffsetOnAxis(ap=token_index[:, 2 + s:3 + s], axis=0),
                                     y_gated[s], None, compute_op=ALU.add).then_inc(y_out, 16)

            def pool_step(j, s, first=False, x=True):
                scatter(j, s, first)
                if x:
                    pool.wait_ge(x_turned, j + 3)
                    hold()
                    pool.wait_ge(gates_kept, j + 3)
                    hold()
                    gather_x(j + 4, s)

            pool.wait_ge(slots_done, 1)
            wait_rows_out(pool)
            pool.wait_ge(gates_out, 16 * (BATCH + N_SEG))
            gather_x(0, 0)
            gather_x(1, 1)
            for j in range(2, 4):
                pool.wait_ge(x_turned, j - 1)
                pool.wait_ge(gates_kept, j - 1)
                gather_x(j, j % 2)
            pool_step(0, 0, first=True)
            pool_step(1, 1)
            with pool.Fori(0, LOOPS) as i:
                for k in range(UNROLL):
                    pool_step(i * UNROLL + (PEEL + k), k % 2)
            for j in REST:
                pool_step(j, j % 2, x=j + 4 < SLOT_TILES)
            pool.wait_ge(y_out, 16 * SLOT_TILES)


        @block.scalar
        def _(act):
            A = nc.scalar
            n = [0]

            def link(ins):
                n[0] += 1
                ins.then_inc(a_step, 1)
                act.wait_ge(a_step, n[0])

            act.wait_ge(trig_in, 1)
            link(A.activation(ssm[:, 0:1], small[:, 0:1], ACT.Exp))
            link(A.activation(ssm[:, 1:2], ssm[:, 0:1], ACT.Exp, scale=-1.0))
            link(A.activation(ssm[:, 2:3], ssm[:, 20:21], ACT.Sin))
            A.activation(ssm[:, 3:4], ssm[:, 21:22], ACT.Sin).then_inc(trig_done, 1)

            for name, dst in (("ident", ident[:, :]), ("d_row", d_row), ("b1", b1_cols[:, :, :]), ("b_t", b_t),
                              ("c_t", c_t), ("beta_row", beta_row), ("gamma_row", gamma_row), ("gate_t", gate_t)):
                act.dma_start(dst, t[name]).then_inc(consts_in, 16)

            for name, dst in (("gateb_row", gateb_row), ("iota_slot", iota_slot[:, :]), ("iota_tile", iota_tile[:, :]),
                              ("token_val", token_val[:, :]), ("valid", valid[:, :]), ("prefix_w", prefix_w[:, :]),
                              ("ones_w", ones_w[:, :]), ("desc", desc[:, :]), ("pad_row", pad_row[:, :]),
                              ("ones_f", ones_f[:, :])):
                act.dma_start(dst, t[name]).then_inc(consts2_in, 16)

            def absolute(b):
                act.wait_ge(diff_v, b + 1)
                act.wait_ge(diff_p, b + 1)
                A.activation(corner, corner, ACT.Abs).then_inc(abs_done, 1)

            def copy_ut_txt():
                for i in range(KD * 2):
                    kd, part = i // 2, i % 2
                    lo, hi_ = (0, 4) if part == 0 else (4, 5)
                    act.wait_ge(ut_txt, i + 1)
                    A.activation(u_t_txt[:, kd, lo:hi_, :], ps_ut[:, 0:(hi_ - lo) * P].rearrange(
                        "p (a c) -> p a c", c=P), ACT.Copy).then_inc(ut_txt_done, 1)

            def copy_ut(b):
                act.wait_ge(ut_psum, f_no(b))
                if b >= 1:
                    act.wait_ge(v_psum, b)
                A.activation(u_t, ps_ut[:, :].rearrange("p (k a c) -> p k a c", k=KD, a=2),
                             ACT.Copy).then_inc(ut_done, 1)

            def normalise3(g):
                k, t0, hg, ug = group(g)
                act.wait_ge(rstd_done[2], b_no(g))
                for a in range(k):
                    ins = A.activation(ug[:, a, :], hg[:, a, :], ACT.Identity, bias=shift[:, t0 + a:t0 + a + 1],
                                       scale=rstd[:, 2, t0 + a:t0 + a + 1])
                ins.then_inc(xn_done, 1)

            def copy_xnt(g):
                k = group(g)[0]
                i = b_no(g)
                act.wait_ge(xnt_psum, i)
                if i > 1:
                    act.wait_ge(logits_done, i - 1)
                src = ps_xnt[:, :].rearrange("p (k a c) -> p k a c", k=KD, a=2)
                A.activation(xn_t[:, :, 0:k, :], src[:, :, 0:k, :], ACT.Copy).then_inc(xnt_done, 1)

            def square_sums(e, which):
                if which == 0:
                    act.wait_ge(w1_in[w_buf(e)], 16 * w_turn(e))
                    A.activation(w1_parts[:, e, 0], w1_stage(e), ACT.Square,
                                 accum_out=wmax[:, e, 0:1]).then_inc(squares_done, 1)
                else:
                    act.wait_ge(w2_in[w_buf(e)], 16 * w_turn(e))
                    A.activation(w2_parts[:, e, :, 0, :], w2_stage(e), ACT.Square,
                                 accum_out=wmax[:, e, 1:2]).then_inc(squares_done, 1)

            def high1(e):
                act.wait_ge(scale_done, e + 1)
                A.activation(w1_parts[:, e, 0], w1_stage(e), ACT.Copy, scale=wsc[:, e, 0:1]).then_inc(hi1_done, 1)

            def high2(e):
                A.activation(w2_parts[:, e, :, 0, :], w2_stage(e), ACT.Copy, scale=wsc[:, e, 1:2]).then_inc(hi2_done, 1)

            absolute(0)
            square_sums(0, 0)
            square_sums(0, 1)
            absolute(1)
            copy_ut_txt()
            for step in range(BATCH + 2):
                e = step if step < E - 1 else E - 1 if step == BATCH else None
                sq = step + 1 if step + 1 < E - 1 else E - 1 if step == E - 1 else None
                if e is not None:
                    high1(e)
                if step < BATCH:
                    copy_ut(step)
                for g in BACKS.get(step - 1, []):
                    normalise3(g)
                if e is not None:
                    high2(e)
                for g in BACKS.get(step - 1, []):
                    copy_xnt(g)
                if sq is not None:
                    square_sums(sq, 0)
                    square_sums(sq, 1)
                if step + 2 < BATCH:
                    absolute(step + 2)
            act.wait_ge(shifted, 1)
            A.activation(r_b, r_a, ACT.Exp).then_inc(exped, 1)
            act.wait_ge(gates_done, 1)
            for g in PARTS:
                for k, p0, p1, row in segments(g):
                    act.dma_start(xn_dram[row:row + p1 - p0, D:XW], r_a[p0:p1, IMG_TILES + k, :]).then_inc(gates_out, 16)

            def hold():
                act.sem_inc(held, 1)

            def x_high(j, s, early=False):
                act.wait_ge(x_turned, j + 1)
                if not early:
                    act.wait_ge(mm1_done, j * 2 - 2)
                A.activation(x_hi[s], ps_x[s][:, 0:D].rearrange("p (k c) -> p k c", k=KD), ACT.Copy,
                             scale=X_SCALE).then_inc(xhi_done, 1)

            def relu(j, s, half, e, early=False):
                act.wait_ge(mm1_done, j * 2 + (half + 1))
                hold()
                if not early:
                    act.wait_ge(split_done, j * 2 + (half - 3))
                    hold()
                for c in range(4 * half, 4 * half + 4):
                    ins = A.activation(h_act[s][:, c * P:(c + 1) * P],
                                       ps_h[s][half][:, (c % 4) * P:(c % 4 + 1) * P], ACT.Relu,
                                       bias=b1_scaled[:, bass.ds(e, 1), c], scale=hsc[:, 2, bass.ds(e, 1)])
                ins.then_inc(relu_done, 1)

            def act_step(j, s, x=True, early=False, x_early=False):
                e = act.value_load(tile_expert[0:1, bass.ds(j, 1)], min_val=0, max_val=E - 1)
                relu(j, s, 0, e, early)
                if x:
                    x_high(j + 1, 1 - s, x_early)
                relu(j, s, 1, e, early)

            act.wait_ge(slots_done, 1)
            x_high(0, 0, early=True)
            act_step(0, 0, early=True, x_early=True)
            act_step(1, 1, early=True)
            with act.Fori(0, LOOPS) as i:
                for k in range(UNROLL):
                    act_step(i * UNROLL + (PEEL + k), k % 2)
            for j in REST:
                act_step(j, j % 2, x=j + 1 < SLOT_TILES)


        @block.tensor
        def _(pe):
            def turn_txt():
                pe.wait_ge(u_done, 1)
                for i in range(KD * 2):
                    kd, part = i // 2, i % 2
                    lo, hi_ = (0, 4) if part == 0 else (4, 5)
                    if i:
                        pe.wait_ge(ut_txt_done, i)
                    for k in range(lo, hi_):
                        ins = pe.transpose(ps_ut[:, (k - lo) * P:(k - lo + 1) * P], u_txt[:, k, kd * P:(kd + 1) * P],
                                           ident[:, :])
                    ins.then_inc(ut_txt, 1)
                pe.wait_ge(ut_txt_done, 2 * KD)
                pe.sem_inc(ut_psum, 1)

            def turn_u(b):
                pe.wait_ge(u_done, f_no(b))
                if b >= 1:
                    pe.wait_ge(ut_done, b)
                for kd in range(KD):
                    for a in range(2):
                        ins = pe.transpose(ps_ut[:, (2 * kd + a) * P:(2 * kd + a + 1) * P],
                                           u[b % 3][:, a, kd * P:(kd + 1) * P], ident[:, :])
                ins.then_inc(ut_psum, 1)

            def project_in(b):
                pe.wait_ge(ut_done, b + 1)
                if b >= 1:
                    pe.wait_ge(drive_done, b)
                for kd in range(KD):
                    pe.matmul(ps_v[:, 0:IMG], b_t[:, kd, :], u_t[:, kd, :, :].rearrange("p a c -> p (a c)"),
                              start=(kd == 0), stop=(kd == KD - 1))
                flat = u_t_txt.rearrange("p k a c -> p k (a c)")
                for kd in range(KD):
                    ins = pe.matmul(ps_v[:, IMG:L], b_t[:, kd, :], flat[:, kd, TXT * b:TXT * (b + 1)],
                                    start=(kd == 0), stop=(kd == KD - 1))
                ins.then_inc(v_psum, 1)

            def project_out(g):
                i = b_no(g) - 1
                k = group(g)[0]
                if g in PARTS:
                    k0, k1 = PARTS[g]
                    src = turned_txt[:, k0 * P:k1 * P]
                    pe.wait_ge(turned_done, -(-min(k1 * P, NTXT) // TXT))
                else:
                    src = turned
                    pe.wait_ge(turned_done, g + 1)
                if i >= 2:
                    pe.wait_ge(sum2_done, i - 1)
                for a in range(k):
                    ins = pe.matmul(ps_y[i % 2][:, a * D:(a + 1) * D], src[:, a * P:(a + 1) * P], c_t,
                                    start=True, stop=True)
                ins.then_inc(y_psum, 1)

            def logits(g):
                i = b_no(g)
                k, t0, _, xn = group(g)
                pe.wait_ge(xn_done, i)
                if i > 1:
                    pe.wait_ge(xnt_done, i - 1)
                for kd in range(KD):
                    for a in range(k):
                        ins = pe.transpose(ps_xnt[:, (2 * kd + a) * P:(2 * kd + a + 1) * P],
                                           xn[:, a, kd * P:(kd + 1) * P], ident[:, :])
                ins.then_inc(xnt_psum, 1)
                pe.wait_ge(xnt_done, i)
                for a in range(k):
                    for kd in range(KD):
                        ins = pe.matmul(ps_logit[:, (t0 + a) * E:(t0 + a + 1) * E], xn_t[:, kd, a, :], gate_t[:, kd, :],
                                        start=(kd == 0), stop=(kd == KD - 1))
                ins.then_inc(logits_done, 1)

            pe.wait_ge(consts_in, 16 * N_CONST)
            turn_txt()
            for step in range(BATCH + 2):
                if step < BATCH:
                    turn_u(step)
                    project_in(step)
                for g in BACKS.get(step - 1, []):
                    logits(g)
                for g in BACKS.get(step + 1, []):
                    project_out(g)

            pe.wait_ge(consts2_in, 16 * N_CONST2)
            pe.wait_ge(picked_done, 1)
            flat = picked[:, :, :].rearrange("p e t -> p (e t)")
            pe.matmul(ps_rank[:, 0:NT * E], prefix_w[:, :], flat, start=True, stop=True)
            pe.matmul(ps_rank[:, NT * E:2 * NT * E], ones_w[:, :], flat, start=True, stop=True).then_inc(rank_psum, 1)
            pe.wait_ge(onehots_done, 1)
            for k in range(2 * NT):
                if k == NT:
                    pe.wait_ge(onehots_done, 2)
                    pe.wait_ge(onehot_pool, 1)
                ins = pe.matmul(ps_slot[:, 0:SLOT_TILES], onehot_slot[:, k, :], onehot_tile[:, k, :],
                                start=(k == 0), stop=(k == 2 * NT - 1))
            ins.then_inc(slot_psum, 1)

            def turn_x(j, s, cycle, early=False):
                pe.wait_ge(x_here[s], cycle * 16 + 16)
                if not early:
                    pe.wait_ge(xlo_done, j - 1)
                for kd in range(KD):
                    ins = pe.transpose(ps_x[s][:, kd * P:(kd + 1) * P], x_slot[s][:, kd * P:(kd + 1) * P], ident[:, :])
                ins.then_inc(x_turned, 1)

            def expert(j):
                return pe.value_load(tile_expert[0:1, bass.ds(j, 1)], min_val=0, max_val=E - 1)

            def start1(j, early=False):
                pe.wait_ge(xhi_done, j + 1)
                pe.wait_ge(xlo_done, j + 1)
                if not early:
                    pe.wait_ge(relu_done, j * 2 - 2)

            def chunk1(s, e, c):
                o = ps_h[s][c // 4][:, (c % 4) * P:(c % 4 + 1) * P]
                cols = slice(c * P, (c + 1) * P)
                for kd in range(KD):
                    hi_w = w1_parts[:, bass.ds(e, 1), 0, kd, cols].rearrange("p a c -> p (a c)")
                    lo_w = w1_parts[:, bass.ds(e, 1), 1, kd, cols].rearrange("p a c -> p (a c)")
                    pe.matmul(o, hi_w, x_hi[s][:, kd, :], start=(kd == 0), stop=False)
                    pe.matmul(o, hi_w, x_lo[s][:, kd, :], start=False, stop=False)
                    ins = pe.matmul(o, lo_w, x_hi[s][:, kd, :], start=False, stop=(kd == KD - 1))
                if c % 4 == 3:
                    ins.then_inc(mm1_done, 1)

            def start2(j, half, early=False):
                if half == 0 and not early:
                    pe.wait_ge(y_scaled, j - 1)
                pe.wait_ge(split_done, j * 2 + (half + 1))

            def chunk2(s, e, c):
                both = w2_parts[:, bass.ds(e, 1), c, :, :].rearrange("p a k o -> p (a k o)")
                hi_w = w2_parts[:, bass.ds(e, 1), c, 0, :].rearrange("p a o -> p (a o)")
                pe.matmul(ps_out[s][:, 0:2 * D], h_hi[s][:, c, :], both, start=(c == 0), stop=False,
                          skip_group_check=True)
                ins = pe.matmul(ps_out[s][:, 0:D], h_lo[s][:, c, :], hi_w, start=False, stop=(c == KH - 1),
                                skip_group_check=True)
                if c == KH - 1:
                    ins.then_inc(mm2_done, 1)

            def pe_step(j, s, cycle, e2, e1, early=False, x=True, nxt=None):
                if e1 is not None:
                    start1(j + 1, early and j == 0)
                e_next = None
                for half in range(2):
                    start2(j, half, early)
                    for c in range(4 * half, 4 * half + 4):
                        if e1 is not None:
                            chunk1(1 - s, e1, c)
                        chunk2(s, e2, c)
                    if half == 0:
                        if x:
                            turn_x(j + 2, s, cycle)
                        if nxt is not None:
                            e_next = expert(nxt)
                return e1, e_next

            pe.wait_ge(slots_done, 1)
            turn_x(0, 0, 0, early=True)
            e0, e1 = expert(0), expert(1)
            start1(0, early=True)
            for c in range(KH):
                chunk1(0, e0, c)
                if c == 3:
                    turn_x(1, 1, 0, early=True)
            e2, e1 = pe_step(0, 0, 1, e0, e1, early=True, nxt=2)
            pe_step(1, 1, 1, e2, e1, early=True)
            with pe.Fori(0, LOOPS) as i:
                e2, e1 = expert(i * UNROLL + PEEL), expert(i * UNROLL + (PEEL + 1))
                for k in range(UNROLL):
                    e2, e1 = pe_step(i * UNROLL + (PEEL + k), k % 2, i * (UNROLL // 2) + (2 + k // 2), e2, e1,
                                     nxt=i * UNROLL + (PEEL + k + 2) if k + 1 < UNROLL else None)
            e2, e1 = expert(REST[0]), expert(REST[1])
            for j in REST:
                e2, e1 = pe_step(j, j % 2, j // 2 + 1, e2, e1, x=j + 2 < SLOT_TILES,
                                 nxt=j + 2 if j + 2 < SLOT_TILES else None)

        @block.vector
        def _(dve):
            V = nc.vector
            n = [0]

            def link(ins):
                n[0] += 1
                ins.then_inc(v_step, 1)
                dve.wait_ge(v_step, n[0])

            def col(i):
                return ssm[:, i:i + 1]

            dve.wait_ge(cols_in, 16)
            theta = small[:, 1:2]
            link(V.tensor_scalar(col(22), theta, 1.0 / TWO_PI, ROUND, ALU.mult, ALU.add))
            link(V.tensor_scalar(col(22), col(22), ROUND, None, ALU.subtract))
            link(V.scalar_tensor_tensor(col(23), col(22), -PI_A, theta, ALU.mult, ALU.add))
            link(V.scalar_tensor_tensor(col(23), col(22), -PI_B, col(23), ALU.mult, ALU.add))
            link(V.scalar_tensor_tensor(col(23), col(22), -PI_C, col(23), ALU.mult, ALU.add))
            link(V.tensor_scalar(col(20), col(23), 0.5, None, ALU.mult))
            V.tensor_scalar(col(21), col(20), TWO_PI / 4, None, ALU.add).then_inc(trig_in, 1)

            def stats(g, which, src):
                k, t0, _, _ = group(g)
                for a in range(k):
                    ins = V.bn_stats(bst[:, a, :], src[:, a, :])
                link(ins)
                for a in range(k):
                    ins = V.bn_aggr(mv[:, which, t0 + a, :], bst[:, a, :])
                ins.then_inc(stats_done[which], 1)

            def diffs(b):
                dve.wait_ge(x_in, 32 * (b + 1))
                if b >= 1:
                    dve.wait_ge(sum_done, b)
                V.tensor_tensor(corner[:, 0, :, :], x_top[:, :, 0:D], x_below[:, :, 1:D + 1],
                                ALU.subtract).then_inc(diff_v, 1)

            def limit(b):
                dve.wait_ge(sum_done, b + 1)
                V.tensor_scalar(h[b % 3], h[b % 3], 1.0, None, ALU.min).then_inc(h_done, 1)
                dve.wait_ge(h_done, b + 1)

            def normalise(g, which, dst, src, signal, no):
                k, t0, _, _ = group(g)
                dve.wait_ge(rstd_done[which], no)
                for a in range(k):
                    ins = V.tensor_scalar(dst[:, a, :], src[:, a, :], mv[:, which, t0 + a, 0:1],
                                          rstd[:, which, t0 + a:t0 + a + 1], ALU.subtract, ALU.mult)
                ins.then_inc(signal, 1)

            def norm0(g):
                _, _, hg, ug = group(g)
                if g != TXTG and g >= 3:
                    dve.wait_ge(xn_out[g % 3], 16 * (g // 3))
                    dve.wait_ge(xnt_psum, b_no(g - 3))
                normalise(g, 0, ug, hg, u_done, f_no(g))

            def norm1(g):
                ug = group(g)[3]
                normalise(g, 1, ug, ug, t_done, b_no(g))

            def add_y(g):
                k, _, _, ug = group(g)
                dve.wait_ge(skip_done, f_no(g))
                dve.wait_ge(y_psum, b_no(g))
                V.tensor_tensor(ug, ug, ps_y[(b_no(g) - 1) % 2][:, 0:k * D].rearrange("p (a d) -> p a d", d=D),
                                ALU.add).then_inc(sum2_done, 1)
                dve.wait_ge(sum2_done, b_no(g))
                stats(g, 1, ug)

            def add_h(g):
                _, _, hg, ug = group(g)
                dve.wait_ge(gamma_done, b_no(g))
                dve.wait_ge(beta_done, f_no(g))
                V.tensor_tensor(hg, hg, ug, ALU.add).then_inc(h1_done, 1)
                dve.wait_ge(h1_done, b_no(g))
                stats(g, 2, hg)

            def recur(b):
                dve.wait_ge(v_psum, b + 1)
                V.tensor_tensor(drive, ps_v[:, 0:L], in_table, ALU.mult).then_inc(drive_done, 1)
                dve.wait_ge(drive_done, b + 1)
                if b >= 1:
                    dve.wait_ge(turned_done, b)
                V.tensor_tensor_scan(state, decay, drive, 0.0, ALU.mult, ALU.add).then_inc(state_done, 1)

            def largest_b1():
                link(V.tensor_tensor(b1_scaled[:, :, :], b1_cols[:, :, :], b1_cols[:, :, :], ALU.mult))
                V.tensor_reduce(wmax[:, :, 2], b1_scaled[:, :, :], AX.X, ALU.max).then_inc(b1_max, 1)

            def scale(e):
                dve.wait_ge(max_all, e + 1)
                link(V.tensor_scalar(pow2[:, e, :].bitcast(I32), wmax_all[:, e, :].bitcast(I32), 1, 0x7F800000,
                                     ALU.logical_shift_right, ALU.bitwise_and))
                link(V.tensor_scalar(pow2[:, e, :], pow2[:, e, :], 2.0 ** (64 - 13), TINY * 2.0 ** -13,
                                     ALU.mult, ALU.max))
                V.reciprocal(wsc[:, e, :], pow2[:, e, :]).then_inc(scale_done, 1)

            def low1(e):
                dve.wait_ge(hi1_done, e + 1)
                V.scalar_tensor_tensor(w1_parts[:, e, 1], w1_stage(e), wsc[:, e, 0:1], w1_parts[:, e, 0],
                                       ALU.mult, ALU.subtract).then_inc(lo1_done, 1)

            def low2(e):
                dve.wait_ge(hi2_done, e + 1)
                V.scalar_tensor_tensor(w2_parts[:, e, :, 1, :], w2_stage(e), wsc[:, e, 1:2], w2_parts[:, e, :, 0, :],
                                       ALU.mult, ALU.subtract).then_inc(lo2_done, 1)

            def tables():
                dve.wait_ge(trig_done, 1)
                s2, c2 = col(2), col(3)
                sin_1, cos_1 = col(4), col(5)
                link(V.tensor_tensor(sin_1, s2, c2, ALU.mult))
                link(V.tensor_scalar(sin_1, sin_1, 2.0, None, ALU.mult))
                link(V.tensor_tensor(cos_1, s2, s2, ALU.mult))
                link(V.tensor_scalar(cos_1, cos_1, -2.0, 1.0, ALU.mult, ALU.add))
                link(V.memset(cos_t[:, 0:1], 1.0))
                link(V.memset(sin_t[:, 0:1], 0.0))
                link(V.tensor_copy(cos_t[:, 1:2], cos_1))
                link(V.tensor_copy(sin_t[:, 1:2], sin_1))
                m = 1
                while m < L - 1:
                    cm, sm, f = cos_t[:, m:m + 1], sin_t[:, m:m + 1], col(6)
                    if m in (8, 64):
                        link(V.tensor_tensor(f, cm, cm, ALU.mult))
                        link(V.scalar_tensor_tensor(f, sm, sm, f, ALU.mult, ALU.add))
                        link(V.tensor_scalar(f, f, -0.5, 1.5, ALU.mult, ALU.add))
                        link(V.tensor_scalar(cm, cm, f, None, ALU.mult))
                        link(V.tensor_scalar(sm, sm, f, None, ALU.mult))
                    k = min(m, L - 1 - m)
                    c0, s0 = cos_t[:, 1:k + 1], sin_t[:, 1:k + 1]
                    c1, s1 = cos_t[:, m + 1:m + k + 1], sin_t[:, m + 1:m + k + 1]
                    s_sm, c_sm = out_table[:, 0:k], in_table[:, 0:k]
                    V.tensor_scalar(s_sm, s0, sm, None, ALU.mult)
                    link(V.tensor_scalar(c_sm, c0, sm, None, ALU.mult))
                    V.scalar_tensor_tensor(c1, c0, cm, s_sm, ALU.mult, ALU.subtract)
                    link(V.scalar_tensor_tensor(s1, s0, cm, c_sm, ALU.mult, ALU.add))
                    m *= 2
                q, r = col(0), col(1)
                re, im, den, cr, ci = col(10), col(11), col(12), col(13), col(14)
                link(V.tensor_scalar(re, cos_1, r, -1.0, ALU.mult, ALU.add))
                link(V.tensor_scalar(im, sin_1, r, None, ALU.mult))
                link(V.tensor_tensor(den, q, q, ALU.mult))
                link(V.scalar_tensor_tensor(den, theta, theta, den, ALU.mult, ALU.add))
                link(V.reciprocal(den, den))
                link(V.tensor_tensor(cr, im, theta, ALU.mult))
                link(V.tensor_tensor(col(15), re, q, ALU.mult))
                link(V.tensor_tensor(cr, cr, col(15), ALU.subtract))
                link(V.tensor_tensor(cr, cr, den, ALU.mult))
                link(V.tensor_tensor(ci, im, q, ALU.mult))
                link(V.scalar_tensor_tensor(ci, re, theta, ci, ALU.mult, ALU.add))
                link(V.tensor_tensor(ci, ci, den, ALU.mult))
                link(V.tensor_scalar(ci, ci, -1.0, None, ALU.mult))
                top, bottom = small[:, 2:3], small[:, 3:4]
                p_, q_ = col(16), col(17)
                link(V.tensor_tensor(p_, ci, bottom, ALU.mult))
                link(V.scalar_tensor_tensor(p_, cr, top, p_, ALU.mult, ALU.add))
                link(V.tensor_tensor(q_, cr, bottom, ALU.mult))
                link(V.scalar_tensor_tensor(q_, ci, top, q_, ALU.mult, ALU.subtract))
                link(V.tensor_scalar(in_table, sin_t, q_, None, ALU.mult))
                link(V.scalar_tensor_tensor(in_table, cos_t, p_, in_table, ALU.mult, ALU.add))
                link(V.tensor_scalar(out_table, sin_t, bottom, None, ALU.mult))
                link(V.scalar_tensor_tensor(out_table, cos_t, top, out_table, ALU.mult, ALU.subtract))
                link(V.memset(decay, 1.0))
                V.tensor_scalar(decay, decay, r, None, ALU.mult).then_inc(tables_done, 1)

            def hidden_scales():
                P1, P2, PB = pow2[:, :, 0], pow2[:, :, 1], pow2[:, :, 2]
                bound, h_scale, relu_scale, y_scale = (hsc[:, i, :] for i in range(4))
                link(V.tensor_scalar(bound, P1, 2.0 ** 8, None, ALU.mult))
                link(V.tensor_tensor(bound, bound, PB, ALU.add))
                link(V.tensor_scalar(bound, bound, 2.0 ** 14, None, ALU.mult))
                link(V.tensor_scalar(bound.bitcast(I32), bound.bitcast(I32), 0x7F800000, None, ALU.bitwise_and))
                link(V.reciprocal(h_scale, bound))
                link(V.tensor_scalar(h_scale, h_scale, 2.0 ** 14, None, ALU.mult))
                link(V.tensor_tensor(relu_scale, h_scale, P1, ALU.mult))
                link(V.tensor_scalar(relu_scale, relu_scale, 1.0 / X_SCALE, None, ALU.mult))
                link(V.tensor_tensor(y_scale, bound, P2, ALU.mult))
                link(V.tensor_scalar(y_scale, y_scale, 2.0 ** -14, None, ALU.mult))
                link(V.tensor_tensor(b1_scaled[:, :, :], b1_cols[:, :, :],
                                     h_scale.rearrange("p (e a) -> p e a", a=1).broadcast_to([P, E, KH]), ALU.mult))

            diffs(0)
            dve.wait_ge(txt_in, 32)
            stats(TXTG, 0, h_txt)
            tables()
            dve.wait_ge(consts_in, 16 * N_CONST)
            largest_b1()
            limit(0)
            stats(0, 0, h[0])
            diffs(1)
            norm0(TXTG)
            scale(0)
            for step in range(BATCH + 1):
                front, backs = step < BATCH, BACKS.get(step, [])
                if front:
                    norm0(step)
                for g in backs:
                    add_y(g)
                if step < E - 1:
                    low1(step)
                for g in backs:
                    norm1(g)
                if front:
                    recur(step)
                if step < E - 1:
                    low2(step)
                for g in backs:
                    add_h(g)
                if step + 1 < BATCH:
                    limit(step + 1)
                    stats(step + 1, 0, h[(step + 1) % 3])
                if step + 2 < BATCH:
                    diffs(step + 2)
                if step + 1 < E - 1:
                    scale(step + 1)
                if step == E - 1:
                    scale(E - 1)
                    hidden_scales()
            low1(E - 1)
            low2(E - 1)

            def over_e(x):
                return x.rearrange("p (t a) -> p t a", a=1).broadcast_to([P, NT, E])

            def over_t(x):
                return x.rearrange("p (a e) -> p a e", a=1).broadcast_to([P, NT, E])

            dve.wait_ge(consts2_in, 16 * N_CONST2)
            dve.wait_ge(logits_done, len(BACK))
            logit = ps_logit[:, 0:NT * E].rearrange("p (t e) -> p t e", e=E)
            link(V.tensor_tensor(r_a[:, :, :], logit, over_t(gateb_row), ALU.add))
            link(V.tensor_reduce(tr[0][:, :], r_a[:, :, :], AX.X, ALU.max))
            V.tensor_tensor(r_a[:, :, :], r_a[:, :, :], over_e(tr[0][:, :]), ALU.subtract).then_inc(shifted, 1)
            dve.wait_ge(exped, 1)
            link(V.tensor_reduce(tr[0][:, :], r_b[:, :, :], AX.X, ALU.add))
            link(V.reciprocal(tr[1][:, :], tr[0][:, :]))
            link(V.tensor_tensor(r_b[:, :, :], r_b[:, :, :], over_e(tr[1][:, :]), ALU.mult))
            for c in range(TOPK):
                src = r_b if c == 0 else r_c
                link(V.tensor_reduce(tr[0][:, :], src[:, :, :], AX.X, ALU.max))
                link(V.tensor_tensor(r_a[:, :, :], src[:, :, :], over_e(tr[0][:, :]), ALU.is_equal))
                link(V.tensor_tensor(r_a[:, :, :], r_a[:, :, :], over_t(desc[:, :]), ALU.mult))
                link(V.tensor_reduce(tr[0][:, :], r_a[:, :, :], AX.X, ALU.max))
                link(V.tensor_tensor(pick[c][:, :, :], r_a[:, :, :], over_e(tr[0][:, :]), ALU.is_equal))
                if c == 0:
                    link(V.scalar_tensor_tensor(r_c[:, :, :], pick[0][:, :, :], -2.0, r_b[:, :, :], ALU.mult, ALU.add))
            link(V.tensor_tensor(r_c[:, :, :], pick[0][:, :, :], pick[1][:, :, :], ALU.add))
            V.tensor_tensor(r_a[:, :, :], r_b[:, :, :], r_c[:, :, :], ALU.mult).then_inc(gates_done, 1)
            V.tensor_tensor(picked[:, :, :].rearrange("p e t -> p t e"), r_c[:, :, :], over_e(valid[:, :]),
                            ALU.mult).then_inc(picked_done, 1)
            dve.wait_ge(rank_psum, 1)
            total = ps_rank[:, NT * E:2 * NT * E]
            cum, before = cmp8[:, 0:NT, :].rearrange("p a b -> p (a b)"), cmp8[:, NT:2 * NT, :].rearrange("p a b -> p (a b)")
            link(V.tensor_tensor_scan(cum, ones_f[:, :], total, 0.0, ALU.mult, ALU.add))
            link(V.tensor_tensor(before, cum, total, ALU.subtract))
            cum_e = cum.rearrange("p (e t) -> p e t", t=NT)
            before_e = before.rearrange("p (e t) -> p e t", t=NT)
            count, tiles, tiles_cum, base = (small[:, 32 + E * i:32 + E * (i + 1)] for i in range(4))
            link(V.tensor_tensor(count, cum_e[:, :, NT - 1], before_e[:, :, 0], ALU.subtract))
            link(V.tensor_scalar(tiles, count, 1.0 / P, 127.0 / 256.0, ALU.mult, ALU.add))
            link(V.tensor_scalar(tiles, tiles, ROUND, ROUND, ALU.add, ALU.subtract))
            link(V.tensor_tensor_scan(tiles_cum, ones_f[:, 0:E], tiles, 0.0, ALU.mult, ALU.add))
            link(V.tensor_tensor(base, tiles_cum, tiles, ALU.subtract))
            link(V.scalar_tensor_tensor(base, base, float(P), before_e[:, :, 0], ALU.mult, ALU.subtract))
            link(V.tensor_tensor(before, before, ps_rank[:, 0:NT * E], ALU.add))
            slot_of = r_c[:, :, :]
            link(V.tensor_tensor(slot_of, before_e.rearrange("p e t -> p t e"), over_t(base), ALU.add))
            for c in range(TOPK):
                link(V.tensor_tensor(pick[c][:, :, :], pick[c][:, :, :], slot_of, ALU.mult))
                link(V.tensor_reduce(slot_f[:, c, :], pick[c][:, :, :], AX.X, ALU.add))
            link(V.tensor_scalar(tile_f[:, :, :], slot_f[:, :, :], 1.0 / P, -127.0 / 256.0, ALU.mult, ALU.add))
            link(V.tensor_scalar(tile_f[:, :, :], tile_f[:, :, :], ROUND, ROUND, ALU.add, ALU.subtract))
            V.scalar_tensor_tensor(within_f[:, :, :], tile_f[:, :, :], -float(P), slot_f[:, :, :],
                                   ALU.mult, ALU.add)
            def slot_onehot(c):
                return V.tensor_tensor(onehot_slot[:, c * NT:(c + 1) * NT, :],
                                       iota_slot[:, :].rearrange("p (a r) -> p a r", a=1).broadcast_to([P, NT, P]),
                                       within_f[:, c, :].rearrange("p (t a) -> p t a", a=1).broadcast_to([P, NT, P]),
                                       ALU.is_equal)

            V.tensor_tensor(onehot_tile[:, NT:2 * NT, :], over_slots(iota_tile[:, :]), per_token(tile_f[:, 1, :]),
                            ALU.is_equal).then_inc(tile_onehot, 1)
            link(V.tensor_tensor(onehot_tile[:, 0:NT, :], over_slots(iota_tile[:, :]), per_token(tile_f[:, 0, :]),
                                 ALU.is_equal))
            V.tensor_tensor(onehot_tile[:, 0:NT, :], onehot_tile[:, 0:NT, :], per_token(token_val[:, :]), ALU.mult)
            slot_onehot(0).then_inc(onehots_done, 1)
            slot_onehot(1).then_inc(onehots_done, 1)
            link(V.tensor_tensor(cmp8, iota_tile[:, :].rearrange("p (t a) -> p t a", a=1)
                                 .broadcast_to([P, SLOT_TILES, E]),
                                 tiles_cum.rearrange("p (a e) -> p a e", a=1).broadcast_to([P, SLOT_TILES, E]),
                                 ALU.is_ge))
            ends = small[:, 128:128 + SLOT_TILES]
            link(V.tensor_reduce(ends, cmp8, AX.X, ALU.add))
            link(V.tensor_scalar(tile_expert[:, :], ends, float(E - 1), None, ALU.min))
            dve.wait_ge(slot_psum, 1)
            val, is_pos, is_pad = ps_slot[:, 0:SLOT_TILES], small[:, 192:192 + SLOT_TILES], small[:, 256:256 + SLOT_TILES]
            tok = small[:, 320:320 + SLOT_TILES]
            link(V.tensor_scalar(is_pos, val, 0.0, None, ALU.is_gt))
            link(V.tensor_scalar(is_pad, val, 0.0, pad_row[:, 0:1], ALU.is_equal, ALU.mult))
            link(V.scalar_tensor_tensor(tok, val, float(MID), is_pos, ALU.add, ALU.subtract))
            V.tensor_tensor(slot_token[:, :], tok, is_pad, ALU.add).then_inc(slots_done, 1)

            def x_low(j, s, early=False):
                dve.wait_ge(xhi_done, j + 1)
                if not early:
                    dve.wait_ge(mm1_done, j * 2 - 2)
                V.scalar_tensor_tensor(x_lo[s], ps_x[s][:, 0:D].rearrange("p (k c) -> p k c", k=KD), X_SCALE, x_hi[s],
                                       ALU.mult, ALU.subtract).then_inc(xlo_done, 1)

            def split(j, s, half, early=False):
                if not early:
                    dve.wait_ge(mm2_done, j - 1)
                dve.wait_ge(relu_done, j * 2 + (half + 1))
                a = h_act[s][:, half * 512:(half + 1) * 512].rearrange("p (k c) -> p k c", c=P)
                k = slice(4 * half, 4 * half + 4)
                V.tensor_copy(h_hi[s][:, k, :], a).then_inc(hi_done, 1)
                dve.wait_ge(hi_done, j * 2 + (half + 1))
                V.tensor_tensor(h_lo[s][:, k, :], a, h_hi[s][:, k, :], ALU.subtract).then_inc(split_done, 1)

            def weigh(j, s, early=False):
                e = dve.value_load(tile_expert[0:1, bass.ds(j, 1)], min_val=0, max_val=E - 1)
                y_scale = hsc[:, 3, bass.ds(e, 1)]
                dve.wait_ge(mm2_done, j + 1)
                V.scalar_tensor_tensor(y_slot[s], ps_out[s][:, D:2 * D], y_scale,
                                       b2_rows[:, bass.ds(e, 1), :].rearrange("p a d -> p (a d)"),
                                       ALU.mult, ALU.add).then_inc(y_half, 1)
                dve.wait_ge(y_half, j + 1)
                V.scalar_tensor_tensor(y_slot[s], ps_out[s][:, 0:D], y_scale, y_slot[s],
                                       ALU.mult, ALU.add).then_inc(y_scaled, 1)
                dve.wait_ge(y_scaled, j + 1)
                if not early:
                    dve.wait_ge(y_out, j * 16 - 16)
                V.tensor_scalar(y_gated[s], y_slot[s], gate_slot[s][:, bass.ds(e, 1)], None,
                                ALU.mult).then_inc(y_done, 1)

            def keep_gates(j, s, cycle, early=False):
                dve.wait_ge(x_here[s], cycle * 16 + 16)
                if not early:
                    dve.wait_ge(y_done, j - 1)
                V.tensor_copy(gate_slot[s], x_slot[s][:, D:XW]).then_inc(gates_kept, 1)

            def dve_step(j, s, cycle, early=False, x=True, nxt=True):
                if nxt:
                    split(j + 1, 1 - s, 0, early and j == 0)
                if x:
                    x_low(j + 2, s)
                if nxt:
                    split(j + 1, 1 - s, 1, early and j == 0)
                weigh(j, s, early)
                if x:
                    keep_gates(j + 2, s, cycle)

            dve.wait_ge(b2_in, 16)
            x_low(0, 0, early=True)
            keep_gates(0, 0, 0, early=True)
            x_low(1, 1, early=True)
            keep_gates(1, 1, 0, early=True)
            split(0, 0, 0, early=True)
            split(0, 0, 1, early=True)
            dve_step(0, 0, 1, early=True)
            dve_step(1, 1, 1, early=True)
            with dve.Fori(0, LOOPS) as i:
                for k in range(UNROLL):
                    dve_step(i * UNROLL + (PEEL + k), k % 2, i * (UNROLL // 2) + (2 + k // 2))
            for j in REST:
                dve_step(j, j % 2, j // 2 + 1, x=j + 2 < SLOT_TILES, nxt=j + 1 < SLOT_TILES)


def kernel(x, txt, L0_attn_log_neg_real, L0_attn_imag, L0_attn_B_mat, L0_attn_C_mat, L0_attn_D, L0_attn_gamma,
           L0_attn_beta, L0_ffn_gate_w, L0_ffn_gate_b, L0_ffn_w1, L0_ffn_b1, L0_ffn_w2, L0_ffn_b2):
    import ml_dtypes
    import numpy as np
    import concourse.bacc as bacc
    from concourse.bass_utils import run_bass_kernel_spmd

    f = np.float32
    a = np.asarray

    def rows(v):
        return np.broadcast_to(a(v).reshape(1, -1), (P, a(v).size)).copy()

    tok = np.zeros((P, NT), np.int64)
    real = np.ones((P, NT), bool)
    for k in range(IMG_TILES):
        tok[:, k] = (k // 2) * L + (k % 2) * P + np.arange(P)
    for k in range(TXT_TILES):
        flat = k * P + np.arange(P)
        real[:, IMG_TILES + k] = flat < NTXT
        tok[:, IMG_TILES + k] = np.where(flat < NTXT, (flat // TXT) * L + IMG + flat % TXT, NTOK + np.arange(P))
    half = (np.arange(P) < STATE)
    cols = np.zeros((P, 16), f)
    cols[:, 0] = np.tile(a(L0_attn_log_neg_real), 2)
    cols[:, 1] = np.tile(a(L0_attn_imag), 2)
    cols[:, 2] = half
    cols[:, 3] = ~half
    ts = {
        "x": np.pad(a(x)[:, 0], ((0, 0), (0, 1), (0, 1))),
        "txt": a(txt).reshape(NTXT, D),
        "ident": np.eye(P, dtype=f),
        "cols": cols,
        "b1": a(L0_ffn_b1).reshape(E, KH, P).transpose(2, 0, 1).copy(),
        "b_t": np.concatenate([a(L0_attn_B_mat).T] * 2, 1).reshape(KD, P, P).transpose(1, 0, 2).copy(),
        "c_t": np.concatenate([a(L0_attn_C_mat).T] * 2, 0),
        "gate_t": a(L0_ffn_gate_w).T.reshape(KD, P, E).transpose(1, 0, 2).copy(),
        "d_row": rows(L0_attn_D), "gamma_row": rows(L0_attn_gamma), "beta_row": rows(L0_attn_beta),
        "gateb_row": rows(L0_ffn_gate_b),
        "ones_f": np.ones((P, NT * E), f),
        "iota_slot": rows(np.arange(P, dtype=np.float16)),
        "iota_tile": rows(np.arange(SLOT_TILES, dtype=f)),
        "token_val": np.where(real, np.where(tok < MID, tok - MID, tok - MID + 1), 0).astype(f),
        "valid": real.astype(f),
        "prefix_w": np.triu(np.ones((P, P)), 1).astype(ml_dtypes.bfloat16),
        "ones_w": np.ones((P, P), ml_dtypes.bfloat16),
        "desc": rows(np.arange(E, 0, -1, dtype=f)),
        "pad_row": (NTOK - MID + np.arange(P, dtype=f)).reshape(P, 1),
        "b2": rows(L0_ffn_b2).reshape(P, E, D),
        "w1": a(L0_ffn_w1), "w2": a(L0_ffn_w2),
    }
    ts = {k: np.ascontiguousarray(v) for k, v in ts.items()}
    nc = bacc.Bacc("TRN2", target_bir_lowering=False, num_devices=1)
    aps = {k: nc.dram_tensor(f"in_{k}", v.shape, mybir.dt.from_np(v.dtype), kind="ExternalInput").ap()
           for k, v in ts.items()}
    out = nc.dram_tensor("out", (ROWS, D), F32, kind="ExternalOutput").ap()
    build(nc, aps, out)
    r = run_bass_kernel_spmd(nc, [{f"in_{k}": v for k, v in ts.items()}], core_ids=[0])
    return r.results[0]["out"][:NTOK].reshape(BATCH, L, D)
```

```python
from contextlib import ExitStack

import concourse.bass as bass
from concourse import mybir

F32, F16, BF16 = mybir.dt.float32, mybir.dt.float16, mybir.dt.bfloat16
I32, U32 = mybir.dt.int32, mybir.dt.uint32
ALU, ACT, AX = mybir.AluOpType, mybir.ActivationFunctionType, mybir.AxisListType

P = 128
BATCH, IMG, TXT, D = 8, 256, 77, 256
L = IMG + TXT
NTOK = BATCH * L
NTXT = BATCH * TXT
IMG_TILES = BATCH * IMG // P
TXT_TILES = -(-NTXT // P)
TXT_LAST = NTXT - (TXT_TILES - 1) * P
NT = IMG_TILES + TXT_TILES
STATE = 64
E, HID, TOPK = 8, 1024, 2
KD, KH = D // P, HID // P
SLOT_TILES = (TOPK * NTOK + E * (P - 1)) // P
ROWS = NTOK + P
MID = NTOK // 2
XW = D + E
EPS = 1e-5
TWO_PI = 6.283185307179586
PI_A = 6.28125
PI_B = 0.0019350051879882812
PI_C = TWO_PI - PI_A - PI_B
ROUND = 12582912.0
X_SCALE = 2.0 ** 9
TINY = 2.0 ** -60
BST_RING = 8
UNROLL = 20
PEEL = 2
LOOPS = (SLOT_TILES - PEEL - 4) // UNROLL
REST = range(PEEL + LOOPS * UNROLL, SLOT_TILES)
X_RING = 5
DVE_HOTS = 7
PACK = 8


def build(nc, t, out):
    with ExitStack() as ctx:
        def sb(name, shape, dt=F32):
            return ctx.enter_context(nc.sbuf_tensor(name, shape, dt))

        def sem(name):
            return ctx.enter_context(nc.semaphore(name))

        w1_parts = sb("w1_parts", [P, E, 2, KD, HID], F16)
        w2_parts = sb("w2_parts", [P, E, KH, 2, D], F16)
        b1_cols = sb("b1_cols", [P, E, KH])
        b1_scaled = sb("b1_scaled", [P, E, KH])
        ident = sb("ident", [P, P])
        small = sb("small", [P, 384])
        slot_token = sb("slot_token", [P, SLOT_TILES], U32)
        tile_expert = sb("tile_expert", [P, SLOT_TILES], I32)
        tile_packed = sb("tile_packed", [P, SLOT_TILES], I32)
        token_index = sb("token_index", [P, X_RING + 2], U32)
        ARENA = 18216
        arena = sb("arena", [P, ARENA])
        cursor = [0]

        def take(*shape, dt=F32, bytes_each=4):
            n = 1
            for k in shape:
                n *= k
            words = -(-n * bytes_each // 4)
            a = arena[:, cursor[0]:cursor[0] + words]
            cursor[0] += words
            assert cursor[0] <= ARENA, cursor[0]
            if dt != F32:
                a = a.bitcast(dt)
            if len(shape) == 1:
                return a
            names = "abcd"[:len(shape)]
            return a.rearrange(f"p ({' '.join(names)}) -> p {' '.join(names)}", **dict(zip(names, shape)))

        w1_buf = [take(KD, HID), w1_parts[:, E - 1].rearrange("p a k h -> p (a k h)").bitcast(F32)
                  .rearrange("p (k h) -> p k h", k=KD)]
        w2_buf = [take(KH, D), w2_parts[:, E - 1].rearrange("p k a o -> p (k a o)").bitcast(F32)
                  .rearrange("p (k o) -> p k o", k=KH)]

        def w_buf(e):
            return e % 2 if e < E - 1 else 0

        def w_turn(e):
            return e // 2 + 1 if e < E - 1 else E // 2 + 1

        def w1_stage(e):
            return w1_buf[w_buf(e)]

        def w2_stage(e):
            return w2_buf[w_buf(e)]

        x_top = take(2, D + 1)
        x_below = take(2, D + 1)
        corner = take(2, 2, D)
        h = [take(2, D) for _ in range(3)]
        u = [take(2, D) for _ in range(3)]
        u_t = take(KD, 2, P)
        xn_t = take(KD, 2, P)
        h_txt = take(TXT_TILES, D)
        u_txt = take(TXT_TILES, D)
        u_t_txt = take(KD, TXT_TILES, P)
        tables_at = cursor[0]
        in_table = take(L)
        out_table = take(L)
        decay = take(L)
        drive_at = cursor[0]
        drive = take(L)
        state = take(L)
        tables_end = cursor[0]
        turned = take(IMG)
        turned_txt = take(TXT_TILES * P)
        b_t = take(KD, P)
        c_t = take(D)
        gate_t = take(KD, E)
        diag = take(KD, P)
        gamma_row = take(D)
        beta_row = take(D)
        gateb_row = take(E)
        zeros = take(XW)
        cursor[0] = tables_at
        cmp8 = take(SLOT_TILES, E)
        r_a, r_b, r_c = (take(NT, E) for _ in range(3))
        pick = [take(NT, E) for _ in range(2)]
        slot_f, tile_f = take(TOPK, NT), take(TOPK, NT)
        picked = take(E, NT, dt=BF16, bytes_each=2)
        assert cursor[0] <= tables_end
        cursor[0] = 0
        onehot_slot = take(2 * NT, P, dt=F16, bytes_each=2)
        onehot_tile = take(2 * NT, SLOT_TILES, dt=F16, bytes_each=2)
        cursor[0] = 0
        h_act = [take(HID) for _ in range(2)]
        h_hi = [take(KH, P, dt=F16, bytes_each=2) for _ in range(2)]
        h_lo = [take(KH, P, dt=F16, bytes_each=2) for _ in range(2)]
        cursor[0] = max(cursor[0], 2 * NT * (P + SLOT_TILES) // 2)
        x_slot = [take(XW) for _ in range(X_RING)]
        x_hi = [take(KD, P, dt=F16, bytes_each=2) for _ in range(2)]
        x_lo = [take(KD, P, dt=F16, bytes_each=2) for _ in range(2)]
        y_slot = [take(D) for _ in range(2)]
        y_gated = [take(D) for _ in range(2)]
        b2_rows = take(E, D)
        iota_slot = sb("iota_slot", [P, P], F16)
        iota_tile = sb("iota_tile", [P, SLOT_TILES])
        token_val = sb("token_val", [P, NT])
        valid = sb("valid", [P, NT])
        prefix_w = sb("prefix_w", [P, P], BF16)
        ones_w = sb("ones_w", [P, P], BF16)
        ones_f = sb("ones_f", [P, NT * E])
        desc = sb("desc", [P, E])
        pad_row = sb("pad_row", [P, 1])
        mv = sb("mv", [P, 3, NT, 2])
        rstd = sb("rstd", [P, 3, NT])
        vpe = sb("vpe", [P, 3, NT])
        shift = sb("shift", [P, 2, NT])
        bst = sb("bst", [P, 3, BST_RING, 6])
        mhalf = sb("mhalf", [P, TXT_TILES])
        tr = [sb(f"tr{i}", [P, NT]) for i in range(3)]
        within_f = sb("within_f", [P, TOPK, NT])
        ssm = sb("ssm", [P, 40])
        wmax = sb("wmax", [P, E, 3])
        wmax_all = sb("wmax_all", [P, E, 3])
        pow2 = sb("pow2", [P, E, 3])
        wsc = sb("wsc", [P, E, 3])
        hsc = sb("hsc", [P, 4, E])
        cos_sin = arena[:, drive_at:drive_at + 2 * L].rearrange("p (a l) -> p a l", a=2)
        cos_t, sin_t = drive, state

        bank = [ctx.enter_context(nc.psum_tensor(f"bank{i}", [P, 512], F32)) for i in range(8)]
        ps_ut, ps_v, ps_xnt, ps_logit, ps_rank, ps_slot = (bank[i] for i in (0, 1, 3, 4, 5, 6))
        ps_y = [bank[2], bank[7]]
        ps_h = [[bank[0], bank[1]], [bank[2], bank[3]]]
        ps_out = bank[4:6]
        ps_x = bank[6:8]

        xn_dram = nc.dram_tensor("xn_rows", [ROWS, XW], F32, kind="Internal").ap()

        cols_in, consts_in = sem("cols_in"), sem("consts_in")
        late_in, consts2_in = sem("late_in"), sem("consts2_in")
        txt_in = sem("txt_in")
        x_in = sem("x_in")
        w1_in, w2_in = ([sem(f"w{w}_in{i}") for i in range(2)] for w in (1, 2))
        v_step = sem("v_step")
        p_step = sem("p_step")
        a_step = sem("a_step")
        zeroed = sem("zeroed")
        txt_zeroed = sem("txt_zeroed")
        trig_in = sem("trig_in")
        trig_done = sem("trig_done")
        tables_done = sem("tables_done")
        diffs_done, abs_done, sum_done = sem("diffs_done"), sem("abs_done"), sem("sum_done")
        h_done = sem("h_done")
        stats_done = [sem(f"stats_done{i}") for i in range(3)]
        rstd_done = [sem(f"rstd_done{i}") for i in range(3)]
        u_done = sem("u_done")
        ut_txt, ut_txt_done = sem("ut_txt"), sem("ut_txt_done")
        ut_psum, ut_done = sem("ut_psum"), sem("ut_done")
        diag_done = sem("diag_done")
        v_psum, state_done = sem("v_psum"), sem("state_done")
        drive_done = sem("drive_done")
        turned_done = sem("turned_done")
        y_psum, y_read = sem("y_psum"), sem("y_read")
        beta_done, txt_beta = sem("beta_done"), sem("txt_beta")
        angle_done, factors_done = sem("angle_done"), sem("factors_done")
        decay_done = sem("decay_done")
        h1_done, h1_out = sem("h1_done"), [sem(f"h1_out{i}") for i in range(3)]
        xn_done, xn_out = sem("xn_done"), [sem(f"xn_out{i}") for i in range(3)]
        rest_out = sem("rest_out")
        xnt_psum, xnt_done = sem("xnt_psum"), sem("xnt_done")
        logits_done = sem("logits_done")
        squares_done, max_all = sem("squares_done"), sem("max_all")
        b1_max = sem("b1_max")
        scale_done = sem("scale_done")
        hi1_done, hi2_done = sem("hi1_done"), sem("hi2_done")
        lo1_done, lo2_done = sem("lo1_done"), sem("lo2_done")
        shifted, exped = sem("shifted"), sem("exped")
        gates_done = sem("gates_done")
        gates_out, gates_out2 = sem("gates_out"), sem("gates_out2")
        picked_done, rank_psum = sem("picked_done"), sem("rank_psum")
        onehots_done, onehot_pool, slot_psum = sem("onehots_done"), sem("onehot_pool"), sem("slot_psum")
        within_ready, onehot_abs, onehots_rest = sem("within_ready"), sem("onehot_abs"), sem("onehots_rest")
        slots_done, experts_done, inverse_done = sem("slots_done"), sem("experts_done"), sem("inverse_done")
        b2_in = sem("b2_in")
        held = sem("held")
        x_idx, y_idx = sem("x_idx"), sem("y_idx")
        tile_onehot = sem("tile_onehot")
        x_here = [sem(f"x_here{i}") for i in range(X_RING)]
        x_turned = sem("x_turned")
        xhi_done, xlo_done = sem("xhi_done"), sem("xlo_done")
        mm1_done, relu_done, split_done = sem("mm1_done"), sem("relu_done"), sem("split_done")
        hi_done = sem("hi_done")
        mm2_done, y_half, y_scaled, y_done = sem("mm2_done"), sem("y_half"), sem("y_scaled"), sem("y_done")
        y_out = sem("y_out")

        N_CONST, N_LATE, N_CONST2 = 5, 3, 10
        TXTG = "text"

        PARTS = {"t0": (0, 2), "t1": (2, 4), "t2": (4, 5)}
        BACKS = {b + 1: [b] for b in range(BATCH)}
        for part, (k0, k1) in PARTS.items():
            BACKS[-(-min(k1 * P, NTXT) // TXT)].append(part)
        BACK = [g for step in sorted(BACKS) for g in BACKS[step]]
        FRONT = [TXTG] + list(range(BATCH))

        def group(g):
            if g == TXTG:
                return TXT_TILES, IMG_TILES, h_txt, u_txt
            if g in PARTS:
                k0, k1 = PARTS[g]
                return k1 - k0, IMG_TILES + k0, h_txt[:, k0:k1, :], u_txt[:, k0:k1, :]
            return 2, 2 * g, h[g % 3], u[g % 3]

        def f_no(g):
            return 1 if g in PARTS else FRONT.index(g) + 1

        def b_no(g):
            return BACK.index(g) + 1

        def segments(g):
            k0, k1 = PARTS[g]
            for k in range(k0, k1):
                for b in range(BATCH):
                    lo, hi_ = max(k * P, b * TXT), min((k + 1) * P, (b + 1) * TXT)
                    if lo < hi_:
                        yield k, lo - k * P, hi_ - k * P, b * L + IMG + lo - b * TXT

        N_SEG = sum(len(list(segments(g))) for g in PARTS)
        SP_SEG = 2 * N_SEG // 3

        def text_gates(eng, i, signal):
            k, p0, p1, row = [seg for g in PARTS for seg in segments(g)][i]
            eng.dma_start(xn_dram[row:row + p1 - p0, D:XW], r_a[p0:p1, IMG_TILES + k, :]).then_inc(signal, 16)

        def wait_rows_out(eng):
            for i in range(3):
                eng.wait_ge(h1_out[i], 16 * len(range(i, BATCH, 3)))
                eng.wait_ge(xn_out[i], 16 * len(range(i, BATCH, 3)))
            eng.wait_ge(rest_out, 16 * (2 + 2 * N_SEG))

        def over_slots(x):
            return x.rearrange("p (a j) -> p a j", a=1).broadcast_to([P, NT, SLOT_TILES])

        def per_token(x):
            return x.rearrange("p (t a) -> p t a", a=1).broadcast_to([P, NT, SLOT_TILES])

        block = ctx.enter_context(nc.Block())


        @block.sync
        def _(sp):
            sp.dma_start(small[:, 0:16], t["cols"]).then_inc(cols_in, 16)

            def load_x(b):
                if b >= 1:
                    sp.wait_ge(diffs_done, b)
                sp.dma_start(x_top, t["x"][b, 0:IMG, :].rearrange("(k p) w -> p k w", p=P)).then_inc(x_in, 16)
                sp.dma_start(x_below, t["x"][b, 1:IMG + 1, :].rearrange("(k p) w -> p k w", p=P)).then_inc(x_in, 16)

            def frees(e):
                return e - 1 if e < E - 1 else e

            def load_w1(e):
                if e >= 2:
                    sp.wait_ge(lo1_done, frees(e))
                sp.dma_start(w1_stage(e), t["w1"][e].rearrange("(k p) h -> p k h", p=P)).then_inc(w1_in[w_buf(e)], 16)

            def load_w2(e):
                if e >= 2:
                    sp.wait_ge(lo2_done, frees(e))
                sp.dma_start(w2_stage(e), t["w2"][e].rearrange("(k p) o -> p k o", p=P)).then_inc(w2_in[w_buf(e)], 16)

            load_x(0)
            sp.wait_ge(txt_zeroed, 1)
            sp.dma_start(h_txt[:, 0:TXT_TILES - 1, :],
                         t["txt"][0:(TXT_TILES - 1) * P].rearrange("(k p) d -> p k d", p=P)).then_inc(txt_in, 16)
            sp.dma_start(h_txt[0:TXT_LAST, TXT_TILES - 1, :], t["txt"][(TXT_TILES - 1) * P:NTXT]).then_inc(txt_in, 16)
            load_x(1)
            load_w1(0)
            load_w2(0)
            load_w1(1)
            load_w2(1)
            sp.wait_ge(zeroed, 1)
            sp.dma_start(out[NTOK:ROWS, :], zeros[:, 0:D]).then_inc(rest_out, 16)
            sp.dma_start(xn_dram[NTOK:ROWS, :], zeros).then_inc(rest_out, 16)

            for name, dst in (("gateb_row", gateb_row), ("iota_slot", iota_slot[:, :]), ("iota_tile", iota_tile[:, :]),
                              ("token_val", token_val[:, :]), ("valid", valid[:, :]), ("prefix_w", prefix_w[:, :]),
                              ("ones_w", ones_w[:, :]), ("desc", desc[:, :]), ("pad_row", pad_row[:, :]),
                              ("ones_f", ones_f[:, :])):
                sp.dma_start(dst, t[name]).then_inc(consts2_in, 16)

            def store(g, dst, src, txt_src, ready, signal):
                sp.wait_ge(ready, b_no(g))
                if g in PARTS:
                    for k, p0, p1, row in segments(g):
                        sp.dma_start(dst[row:row + p1 - p0, 0:D], txt_src[p0:p1, k, :]).then_inc(rest_out, 16)
                else:
                    sp.dma_start(dst[L * g:L * g + IMG, 0:D].rearrange("(k p) d -> p k d", p=P),
                                 src(g)).then_inc(signal[g % len(signal)], 16)

            for step in range(BATCH + 2):
                if step + 2 < BATCH:
                    load_x(step + 2)
                for g in BACKS.get(step - 1, []):
                    store(g, xn_dram, lambda b: u[b % 3], u_txt, xn_done, xn_out)
                nxt = step + 2 if step + 2 < E - 1 else E - 1 if step == E - 2 else None
                if nxt is not None:
                    load_w1(nxt)
                    load_w2(nxt)
                for g in BACKS.get(step, []):
                    store(g, out, lambda b: h[b % 3], h_txt, h1_done, h1_out)
            sp.wait_ge(gates_done, 1)
            gates_at = xn_dram[0:NTOK, D:XW].rearrange("(b l) e -> b l e", b=BATCH)
            image_gates = r_a[:, 0:IMG_TILES, :].rearrange("p (b k) e -> p b k e", k=IMG // P)
            for k in range(IMG // P):
                sp.dma_start(gates_at[:, k * P:(k + 1) * P, :].rearrange("b p e -> p b e"),
                             image_gates[:, :, k, :]).then_inc(gates_out, 16)
            for i in range(SP_SEG):
                text_gates(sp, i, gates_out)
            wait_rows_out(sp)
            sp.dma_start(b2_rows, t["b2"]).then_inc(b2_in, 16)


        @block.gpsimd
        def _(pool):
            G = nc.gpsimd
            n = [0]

            def link(ins):
                n[0] += 1
                ins.then_inc(p_step, 1)
                pool.wait_ge(p_step, n[0])

            def per_column(x, k):
                return x.rearrange("p (a d) -> p a d", a=1).broadcast_to([P, k, D])

            G.memset(h_txt[96:P, TXT_TILES - 1, :], 0.0).then_inc(txt_zeroed, 1)
            pool.wait_ge(txt_zeroed, 1)
            G.memset(zeros, 0.0).then_inc(zeroed, 1)
            pool.wait_ge(zeroed, 1)
            link(G.memset(turned_txt[:, NTXT:], 0.0))
            link(G.memset(mhalf[:, :], -0.5))

            def rstd_of(g, which, no):
                k, t0, _, _ = group(g)
                pool.wait_ge(stats_done[which], no)
                link(G.tensor_scalar(vpe[:, which, t0:t0 + k], mv[:, which, t0:t0 + k, 1], EPS, None, ALU.add))
                ins = G.tensor_tensor(rstd[:, which, t0:t0 + k], vpe[:, which, t0:t0 + k], mhalf[:, 0:k], ALU.pow)
                if which == 1 or g == TXTG:
                    ins.then_inc(rstd_done[which], 1)
                    return
                link(ins)
                link(G.tensor_scalar(vpe[:, which, t0:t0 + k], mv[:, which, t0:t0 + k, 0], -1.0, None, ALU.mult))
                G.tensor_tensor(shift[:, which // 2, t0:t0 + k], vpe[:, which, t0:t0 + k], rstd[:, which, t0:t0 + k],
                                ALU.mult).then_inc(rstd_done[which], 1)

            def diffs(b):
                pool.wait_ge(x_in, 32 * (b + 1))
                if b >= 1:
                    pool.wait_ge(sum_done, b)
                G.tensor_tensor(corner[:, 0, :, :], x_top[:, :, 0:D], x_below[:, :, 1:D + 1], ALU.subtract)
                G.tensor_tensor(corner[:, 1, :, :], x_below[:, :, 0:D], x_top[:, :, 1:D + 1],
                                ALU.subtract).then_inc(diffs_done, 1)

            def sums(b):
                pool.wait_ge(abs_done, b + 1)
                if b >= 3:
                    pool.wait_ge(h1_out[b % 3], 16 * (b // 3))
                    pool.wait_ge(xn_done, b_no(b - 3))
                G.tensor_tensor(h[b % 3], corner[:, 0, :, :], corner[:, 1, :, :], ALU.add).then_inc(sum_done, 1)

            def add_beta(g):
                k, _, hg, _ = group(g)
                pool.wait_ge(u_done, f_no(g))
                G.tensor_tensor(hg, hg, per_column(beta_row, k), ALU.add
                                ).then_inc(txt_beta if g in PARTS else beta_done, 1)

            def turn(b):
                pool.wait_ge(state_done, b + 1)
                if b >= 1:
                    pool.wait_ge(y_psum, b_no(b - 1))
                link(G.tensor_tensor(turned, state[:, 0:IMG], out_table[:, 0:IMG], ALU.mult))
                G.tensor_tensor(turned_txt[:, TXT * b:TXT * (b + 1)], state[:, IMG:L], out_table[:, IMG:L],
                                ALU.mult).then_inc(turned_done, 1)

            def factors():
                def col(i):
                    return ssm[:, i:i + 1]

                def op(dst, x, y, alu):
                    link(G.tensor_tensor(dst, x, y, alu))

                q, r, cos_1, sin_1 = col(0), col(1), col(5), col(4)
                theta, top, bottom = small[:, 1:2], small[:, 2:3], small[:, 3:4]
                re, im, den, cr, ci, tmp = (col(i) for i in (10, 11, 12, 13, 14, 15))
                pool.wait_ge(angle_done, 1)
                op(re, cos_1, r, ALU.mult)
                link(G.tensor_scalar(re, re, -1.0, None, ALU.add))
                op(im, sin_1, r, ALU.mult)
                op(den, q, q, ALU.mult)
                op(tmp, theta, theta, ALU.mult)
                op(den, den, tmp, ALU.add)
                op(den, den, mhalf[:, 0:1], ALU.pow)
                op(den, den, den, ALU.mult)
                op(cr, im, theta, ALU.mult)
                op(tmp, re, q, ALU.mult)
                op(cr, cr, tmp, ALU.subtract)
                op(cr, cr, den, ALU.mult)
                op(ci, im, q, ALU.mult)
                op(tmp, re, theta, ALU.mult)
                op(ci, ci, tmp, ALU.add)
                op(ci, ci, den, ALU.mult)
                link(G.tensor_scalar(ci, ci, -1.0, None, ALU.mult))
                op(col(16), ci, bottom, ALU.mult)
                op(tmp, cr, top, ALU.mult)
                op(col(16), col(16), tmp, ALU.add)
                op(col(17), ci, top, ALU.mult)
                op(tmp, cr, bottom, ALU.mult)
                G.tensor_tensor(col(17), col(17), tmp, ALU.subtract).then_inc(factors_done, 1)

            def largest(e):
                pool.wait_ge(squares_done, 2 * (e + 1))
                if e == 0:
                    pool.wait_ge(b1_max, 1)
                G.partition_all_reduce(wmax_all[:, e, :], wmax[:, e, :], P,
                                       bass.bass_isa.ReduceOp.max).then_inc(max_all, 1)

            diffs(0)
            sums(0)
            rstd_of(TXTG, 0, 1)
            diffs(1)
            rstd_of(0, 0, 2)
            factors()
            link(G.memset(decay, 1.0))
            G.tensor_scalar(decay, decay, ssm[:, 1:2], None, ALU.mult).then_inc(decay_done, 1)
            pool.wait_ge(consts_in, 16 * N_CONST)
            flat_diag = diag.rearrange("p k c -> p (k c)")
            link(G.tensor_scalar(flat_diag, flat_diag, 1.0, None, ALU.add))
            G.tensor_tensor(diag, diag, ident[:, :].rearrange("p (a c) -> p a c", a=1).broadcast_to([P, KD, P]),
                            ALU.mult).then_inc(diag_done, 1)
            sums(1)
            largest(0)
            for step in range(BATCH + 1):
                front, backs = step < BATCH, BACKS.get(step, [])
                if front:
                    add_beta(step)
                for g in backs:
                    rstd_of(g, 1, b_no(g))
                if 0 < step and step + 1 < BATCH:
                    sums(step + 1)
                if front:
                    turn(step)
                for g in backs:
                    rstd_of(g, 2, b_no(g))
                if step + 1 < BATCH:
                    rstd_of(step + 1, 0, f_no(step + 1))
                if step + 1 < E - 1:
                    largest(step + 1)
                if step == E - 1:
                    largest(E - 1)
                if step + 2 < BATCH:
                    diffs(step + 2)
                for g in BACKS.get(step + 1, []):
                    if g in PARTS:
                        add_beta(g)

            pool.wait_ge(consts2_in, 16 * N_CONST2)
            pool.wait_ge(picked_done, 1)
            link(G.tensor_tensor(r_a, r_b, r_c, ALU.mult))
            pool.wait_ge(inverse_done, 1)
            G.tensor_tensor(r_a, r_a, tr[1][:, :].rearrange("p (t a) -> p t a", a=1).broadcast_to([P, NT, E]),
                            ALU.mult).then_inc(gates_done, 1)
            pool.wait_ge(gates_done, 1)
            for i in range(SP_SEG, N_SEG):
                text_gates(pool, i, gates_out2)
            for c in range(TOPK):
                pool.wait_ge(tile_onehot, c + 1)
                k = slice(c * NT, (c + 1) * NT)
                G.tensor_tensor(onehot_tile[:, k, :], onehot_tile[:, k, :], per_token(token_val[:, :]),
                                ALU.mult).then_inc(onehot_pool, 1)

            def hold():
                pool.sem_inc(held, 1)

            def gather_x(j, r):
                G.tensor_copy(token_index[:, r:r + 1], slot_token[:, bass.ds(j, 1)]).then_inc(x_idx, 1)
                pool.wait_ge(x_idx, j + 1)
                hold()
                G.indirect_dma_start(x_slot[r], None, xn_dram,
                                     bass.IndirectOffsetOnAxis(ap=token_index[:, r:r + 1], axis=0)
                                     ).then_inc(x_here[r], 16)

            def scatter(j, s, first=False):
                column = token_index[:, X_RING + s:X_RING + s + 1]
                G.tensor_copy(column, slot_token[:, bass.ds(j, 1)]).then_inc(y_idx, 1)
                pool.wait_ge(y_idx, j + 1)
                hold()
                pool.wait_ge(y_done, j + 1)
                hold()
                if not first:
                    pool.wait_ge(y_out, j * 16)
                    hold()
                G.indirect_dma_start(out, bass.IndirectOffsetOnAxis(ap=column, axis=0),
                                     y_gated[s], None, compute_op=ALU.add).then_inc(y_out, 16)

            def pool_step(j, s, r, first=False, x=True):
                if x:
                    gather_x(j + X_RING - 1, (r + X_RING - 1) % X_RING)
                scatter(j, s, first)

            pool.wait_ge(slots_done, 1)
            wait_rows_out(pool)
            pool.wait_ge(gates_out, 16 * (IMG // P + SP_SEG))
            pool.wait_ge(gates_out2, 16 * (N_SEG - SP_SEG))
            for j in range(X_RING - 1):
                gather_x(j, j)
            for j in range(PEEL):
                pool_step(j, j, j, first=j == 0)
            with pool.Fori(0, LOOPS) as i:
                for k in range(UNROLL):
                    pool_step(i * UNROLL + (PEEL + k), k % 2, (PEEL + k) % X_RING)
            for j in REST:
                pool_step(j, j % 2, j % X_RING, x=j + X_RING - 1 < SLOT_TILES)
            pool.wait_ge(y_out, 16 * SLOT_TILES)


        @block.scalar
        def _(act):
            A = nc.scalar
            n = [0]

            def link(ins):
                n[0] += 1
                ins.then_inc(a_step, 1)
                act.wait_ge(a_step, n[0])

            for name, dst in (("ident", ident[:, :]), ("b_t", b_t), ("d_row", diag.rearrange("p k c -> p (k c)")),
                              ("beta_row", beta_row), ("b1", b1_cols[:, :, :])):
                act.dma_start(dst, t[name]).then_inc(consts_in, 16)

            act.wait_ge(trig_in, 1)
            link(A.activation(ssm[:, 0:1], small[:, 0:1], ACT.Exp))
            link(A.activation(ssm[:, 1:2], ssm[:, 0:1], ACT.Exp, scale=-1.0))
            link(A.activation(ssm[:, 2:3], ssm[:, 20:21], ACT.Sin))
            A.activation(ssm[:, 3:4], ssm[:, 21:22], ACT.Sin).then_inc(trig_done, 1)

            def absolute(b):
                act.wait_ge(diffs_done, b + 1)
                A.activation(corner, corner, ACT.Abs).then_inc(abs_done, 1)

            def copy_ut_txt():
                for i in range(KD * 2):
                    kd, part = i // 2, i % 2
                    lo, hi_ = (0, 4) if part == 0 else (4, 5)
                    act.wait_ge(ut_txt, i + 1)
                    A.activation(u_t_txt[:, kd, lo:hi_, :], ps_ut[:, 0:(hi_ - lo) * P].rearrange(
                        "p (a c) -> p a c", c=P), ACT.Copy).then_inc(ut_txt_done, 1)

            def copy_ut(b):
                act.wait_ge(ut_psum, f_no(b))
                if b >= 1:
                    act.wait_ge(y_psum, b_no(b - 1))
                A.activation(u_t, ps_ut[:, :].rearrange("p (k a c) -> p k a c", k=KD, a=2),
                             ACT.Copy).then_inc(ut_done, 1)

            def normalise1(b):
                _, t0, hb, ub = group(b)
                act.wait_ge(rstd_done[0], f_no(b))
                if b >= 3:
                    act.wait_ge(xn_out[b % 3], 16 * (b // 3))
                    act.wait_ge(xnt_psum, b_no(b - 3))
                for a in range(2):
                    ins = A.activation(ub[:, a, :], hb[:, a, :], ACT.Identity, bias=shift[:, 0, t0 + a:t0 + a + 1],
                                       scale=rstd[:, 0, t0 + a:t0 + a + 1])
                ins.then_inc(u_done, 1)

            def normalise3(g):
                k, t0, hg, ug = group(g)
                act.wait_ge(rstd_done[2], b_no(g))
                for a in range(k):
                    ins = A.activation(ug[:, a, :], hg[:, a, :], ACT.Identity, bias=shift[:, 1, t0 + a:t0 + a + 1],
                                       scale=rstd[:, 2, t0 + a:t0 + a + 1])
                ins.then_inc(xn_done, 1)

            def copy_xnt(g):
                k = group(g)[0]
                i = b_no(g)
                act.wait_ge(xnt_psum, i)
                if i > 1:
                    act.wait_ge(logits_done, i - 1)
                src = ps_xnt[:, :].rearrange("p (k a c) -> p k a c", k=KD, a=2)
                A.activation(xn_t[:, :, 0:k, :], src[:, :, 0:k, :], ACT.Copy).then_inc(xnt_done, 1)

            def square_sums(e, which):
                if which == 0:
                    act.wait_ge(w1_in[w_buf(e)], 16 * w_turn(e))
                    A.activation(w1_parts[:, e, 0], w1_stage(e), ACT.Square,
                                 accum_out=wmax[:, e, 0:1]).then_inc(squares_done, 1)
                else:
                    act.wait_ge(w2_in[w_buf(e)], 16 * w_turn(e))
                    A.activation(w2_parts[:, e, :, 0, :], w2_stage(e), ACT.Square,
                                 accum_out=wmax[:, e, 1:2]).then_inc(squares_done, 1)

            def high1(e):
                act.wait_ge(scale_done, e + 1)
                A.activation(w1_parts[:, e, 0], w1_stage(e), ACT.Copy, scale=wsc[:, e, 0:1]).then_inc(hi1_done, 1)

            def high2(e):
                A.activation(w2_parts[:, e, :, 0, :], w2_stage(e), ACT.Copy, scale=wsc[:, e, 1:2]).then_inc(hi2_done, 1)

            absolute(0)
            for name, dst in (("c_t", c_t), ("gamma_row", gamma_row), ("gate_t", gate_t)):
                act.dma_start(dst, t[name]).then_inc(late_in, 16)
            act.wait_ge(u_done, 1)
            normalise1(0)
            copy_ut_txt()
            for step in range(BATCH + 2):
                e = step if step < E - 1 else E - 1 if step == BATCH else None
                sq = step + 1 if step + 1 < E - 1 else E - 1 if step == E - 1 else None
                if step == 0:
                    copy_ut(0)
                    absolute(1)
                    square_sums(0, 0)
                    square_sums(0, 1)
                elif step < BATCH:
                    normalise1(step)
                if step == BATCH:
                    for g in BACKS[step - 1]:
                        normalise3(g)
                        copy_xnt(g)
                if e is not None:
                    high1(e)
                if step > BATCH:
                    for g in BACKS[BATCH]:
                        normalise3(g)
                    copy_xnt(BACKS[BATCH][0])
                    high2(E - 1)
                    for g in BACKS[BATCH][1:]:
                        copy_xnt(g)
                if 0 < step < BATCH:
                    copy_ut(step)
                if step < BATCH:
                    for g in BACKS.get(step - 1, []):
                        normalise3(g)
                if 0 < step and step + 1 < BATCH:
                    absolute(step + 1)
                if e is not None and step < BATCH:
                    high2(e)
                before = BACKS.get(step - 1, []) if step < BATCH else []
                for g in before[:1]:
                    copy_xnt(g)
                if sq is not None:
                    square_sums(sq, 0)
                for g in before[1:]:
                    copy_xnt(g)
                if sq is not None:
                    square_sums(sq, 1)
            act.wait_ge(shifted, 1)
            A.activation(r_b, r_a, ACT.Exp).then_inc(exped, 1)
            act.wait_ge(within_ready, 1)
            for k in range(DVE_HOTS, NT):
                A.activation(onehot_slot[:, NT + k, :], iota_slot[:, :], ACT.Abs, bias=within_f[:, 1, k:k + 1],
                             scale=-1.0).then_inc(onehot_abs, 1)
            act.wait_ge(onehot_abs, NT - DVE_HOTS)
            hots = onehot_slot[:, NT + DVE_HOTS:2 * NT, :]
            A.activation(hots, hots, ACT.Relu, bias=ones_f[:, 0:1], scale=-1.0).then_inc(onehots_rest, 1)

            def hold():
                act.sem_inc(held, 1)

            def x_high(j, s):
                act.wait_ge(x_turned, j + 1)
                A.activation(x_hi[s], ps_x[s][:, 0:D].rearrange("p (k c) -> p k c", k=KD), ACT.Copy,
                             scale=X_SCALE).then_inc(xhi_done, 1)

            def relu(j, s, half, e):
                act.wait_ge(mm1_done, j * 2 + (half + 1))
                hold()
                for c in range(4 * half, 4 * half + 4):
                    ins = A.activation(h_act[s][:, c * P:(c + 1) * P],
                                       ps_h[s][half][:, (c % 4) * P:(c % 4 + 1) * P], ACT.Relu,
                                       bias=b1_scaled[:, bass.ds(e, 1), c], scale=hsc[:, 2, bass.ds(e, 1)])
                ins.then_inc(relu_done, 1)

            def act_step(j, s, x=True):
                e = act.value_load(tile_expert[0:1, bass.ds(j, 1)], min_val=0, max_val=E - 1)
                relu(j, s, 0, e)
                relu(j, s, 1, e)
                if x:
                    x_high(j + 2, s)

            act.wait_ge(experts_done, 1)
            x_high(0, 0)
            x_high(1, 1)
            act_step(0, 0)
            act_step(1, 1)
            with act.Fori(0, LOOPS) as i:
                for k in range(UNROLL):
                    act_step(i * UNROLL + (PEEL + k), k % 2)
            for j in REST:
                act_step(j, j % 2, x=j + 2 < SLOT_TILES)


        @block.tensor
        def _(pe):
            def turn_txt():
                pe.wait_ge(u_done, 1)
                for i in range(KD * 2):
                    kd, part = i // 2, i % 2
                    lo, hi_ = (0, 4) if part == 0 else (4, 5)
                    if i:
                        pe.wait_ge(ut_txt_done, i)
                    for k in range(lo, hi_):
                        ins = pe.transpose(ps_ut[:, (k - lo) * P:(k - lo + 1) * P], u_txt[:, k, kd * P:(kd + 1) * P],
                                           ident[:, :])
                    ins.then_inc(ut_txt, 1)
                pe.wait_ge(ut_txt_done, 2 * KD)
                pe.sem_inc(ut_psum, 1)

            def turn_u(b):
                pe.wait_ge(u_done, f_no(b))
                if b >= 1:
                    pe.wait_ge(ut_done, b)
                for kd in range(KD):
                    for a in range(2):
                        ins = pe.transpose(ps_ut[:, (2 * kd + a) * P:(2 * kd + a + 1) * P],
                                           u[b % 3][:, a, kd * P:(kd + 1) * P], ident[:, :])
                ins.then_inc(ut_psum, 1)

            def project_in(b):
                pe.wait_ge(ut_done, b + 1)
                if b >= 1:
                    pe.wait_ge(drive_done, b)
                for kd in range(KD):
                    pe.matmul(ps_v[:, 0:IMG], b_t[:, kd, :], u_t[:, kd, :, :].rearrange("p a c -> p (a c)"),
                              start=(kd == 0), stop=(kd == KD - 1))
                flat = u_t_txt.rearrange("p k a c -> p k (a c)")
                for kd in range(KD):
                    ins = pe.matmul(ps_v[:, IMG:L], b_t[:, kd, :], flat[:, kd, TXT * b:TXT * (b + 1)],
                                    start=(kd == 0), stop=(kd == KD - 1))
                ins.then_inc(v_psum, 1)

            def project_out(g):
                i = b_no(g) - 1
                k = group(g)[0]
                if g in PARTS:
                    k0, k1 = PARTS[g]
                    src, u_src = turned_txt[:, k0 * P:k1 * P], u_t_txt[:, :, k0:k1, :]
                    pe.wait_ge(turned_done, -(-min(k1 * P, NTXT) // TXT))
                else:
                    src, u_src = turned, u_t
                    pe.wait_ge(turned_done, g + 1)
                if i == 0:
                    pe.wait_ge(diag_done, 1)
                    pe.wait_ge(late_in, 16 * N_LATE)
                if i >= 2:
                    pe.wait_ge(y_read, i - 1)
                for a in range(k):
                    pe.matmul(ps_y[i % 2][:, a * D:(a + 1) * D], src[:, a * P:(a + 1) * P], c_t,
                              start=True, stop=False, skip_group_check=True)
                    for kd in range(KD):
                        ins = pe.matmul(ps_y[i % 2][:, a * D + kd * P:a * D + (kd + 1) * P], u_src[:, kd, a, :],
                                        diag[:, kd, :], start=False, stop=(kd == KD - 1), skip_group_check=True)
                ins.then_inc(y_psum, 1)

            def logits(g):
                i = b_no(g)
                k, t0, _, xn = group(g)
                pe.wait_ge(xn_done, i)
                if i > 1:
                    pe.wait_ge(xnt_done, i - 1)
                for kd in range(KD):
                    for a in range(k):
                        ins = pe.transpose(ps_xnt[:, (2 * kd + a) * P:(2 * kd + a + 1) * P],
                                           xn[:, a, kd * P:(kd + 1) * P], ident[:, :])
                ins.then_inc(xnt_psum, 1)
                pe.wait_ge(xnt_done, i)
                for a in range(k):
                    for kd in range(KD):
                        ins = pe.matmul(ps_logit[:, (t0 + a) * E:(t0 + a + 1) * E], xn_t[:, kd, a, :], gate_t[:, kd, :],
                                        start=(kd == 0), stop=(kd == KD - 1))
                ins.then_inc(logits_done, 1)

            pe.wait_ge(consts_in, 16 * N_CONST)
            turn_txt()
            for step in range(BATCH + 2):
                if step < BATCH:
                    turn_u(step)
                    project_in(step)
                for g in BACKS.get(step - 1, []):
                    logits(g)
                for g in BACKS.get(step + 1, []):
                    project_out(g)

            pe.wait_ge(consts2_in, 16 * N_CONST2)
            pe.wait_ge(picked_done, 1)
            flat = picked.rearrange("p e t -> p (e t)")
            pe.matmul(ps_rank[:, 0:NT * E], prefix_w[:, :], flat, start=True, stop=True)
            pe.matmul(ps_rank[:, NT * E:2 * NT * E], ones_w[:, :], flat, start=True, stop=True).then_inc(rank_psum, 1)
            pe.wait_ge(onehots_done, 1)
            pe.wait_ge(onehot_pool, 1)
            for k in range(2 * NT):
                if k == NT:
                    pe.wait_ge(onehots_done, 2)
                    pe.wait_ge(onehot_pool, 2)
                if k == NT + DVE_HOTS:
                    pe.wait_ge(onehots_rest, 1)
                ins = pe.matmul(ps_slot[:, 0:SLOT_TILES], onehot_slot[:, k, :], onehot_tile[:, k, :],
                                start=(k == 0), stop=(k == 2 * NT - 1))
            ins.then_inc(slot_psum, 1)

            def turn_x(j, s, r, cycle):
                pe.wait_ge(x_here[r], cycle * 16 + 16)
                for kd in range(KD):
                    ins = pe.transpose(ps_x[s][:, kd * P:(kd + 1) * P], x_slot[r][:, kd * P:(kd + 1) * P], ident[:, :])
                ins.then_inc(x_turned, 1)

            def pack(j):
                return pe.value_load(tile_packed[0:1, bass.ds(j, 1)], min_val=0, max_val=E ** PACK - 1)

            def lowest(packed):
                return pe.snap(packed % E, min_val=0, max_val=E - 1)

            def dropped(packed):
                return pe.snap(packed // E, min_val=0, max_val=E ** (PACK - 1) - 1)

            def start1(j):
                pe.wait_ge(xlo_done, j + 1)

            def chunk1(s, e, c):
                o = ps_h[s][c // 4][:, (c % 4) * P:(c % 4 + 1) * P]
                cols = slice(c * P, (c + 1) * P)
                for kd in range(KD):
                    hi_w = w1_parts[:, bass.ds(e, 1), 0, kd, cols].rearrange("p a c -> p (a c)")
                    lo_w = w1_parts[:, bass.ds(e, 1), 1, kd, cols].rearrange("p a c -> p (a c)")
                    pe.matmul(o, hi_w, x_hi[s][:, kd, :], start=(kd == 0), stop=False)
                    pe.matmul(o, hi_w, x_lo[s][:, kd, :], start=False, stop=False)
                    ins = pe.matmul(o, lo_w, x_hi[s][:, kd, :], start=False, stop=(kd == KD - 1))
                if c % 4 == 3:
                    ins.then_inc(mm1_done, 1)

            def start2(j, half):
                pe.wait_ge(split_done, j * 2 + (half + 1))

            def chunk2(s, e, c):
                both = w2_parts[:, bass.ds(e, 1), c, :, :].rearrange("p a k o -> p (a k o)")
                hi_w = w2_parts[:, bass.ds(e, 1), c, 0, :].rearrange("p a o -> p (a o)")
                pe.matmul(ps_out[s][:, 0:2 * D], h_hi[s][:, c, :], both, start=(c == 0), stop=False,
                          skip_group_check=True)
                ins = pe.matmul(ps_out[s][:, 0:D], h_lo[s][:, c, :], hi_w, start=False, stop=(c == KH - 1),
                                skip_group_check=True)
                if c == KH - 1:
                    ins.then_inc(mm2_done, 1)

            def pe_step(j, s, r, cycle, e2, e1, x=True):
                if e1 is not None:
                    start1(j + 1)
                for c in range(KH):
                    if e1 is not None:
                        chunk1(1 - s, e1, c)
                    if c % (KH // 2) == 0:
                        start2(j, c // (KH // 2))
                    chunk2(s, e2, c)
                    if c == 1 and x:
                        turn_x(j + 2, s, r, cycle)

            pe.wait_ge(experts_done, 1)
            turn_x(0, 0, 0, 0)
            turn_x(1, 1, 1, 0)
            start1(0)
            packed = pack(0)
            e2 = lowest(packed)
            for c in range(KH):
                chunk1(0, e2, c)
            for j in range(PEEL):
                packed = dropped(packed)
                e1 = lowest(packed)
                pe_step(j, j, j + 2, 0, e2, e1)
                e2 = e1
            with pe.Fori(0, LOOPS) as i:
                for k in range(UNROLL):
                    if k % (PACK - 1) == 0:
                        packed = pack(i * UNROLL + (PEEL + k))
                        e2 = lowest(packed)
                    packed = dropped(packed)
                    e1 = lowest(packed)
                    pe_step(i * UNROLL + (PEEL + k), k % 2, (PEEL + k + 2) % X_RING,
                            i * (UNROLL // X_RING) + (PEEL + k + 2) // X_RING, e2, e1)
                    e2 = e1
            packed = pack(REST[0])
            e2 = lowest(packed)
            for j in REST:
                e1 = None
                if j + 1 < SLOT_TILES:
                    packed = dropped(packed)
                    e1 = lowest(packed)
                pe_step(j, j % 2, (j + 2) % X_RING, (j + 2) // X_RING, e2, e1, x=j + 2 < SLOT_TILES)
                e2 = e1

        @block.vector
        def _(dve):
            V = nc.vector
            n = [0]

            def link(ins):
                n[0] += 1
                ins.then_inc(v_step, 1)
                dve.wait_ge(v_step, n[0])

            def col(i):
                return ssm[:, i:i + 1]

            dve.wait_ge(cols_in, 16)
            theta = small[:, 1:2]
            link(V.tensor_scalar(col(22), theta, 1.0 / TWO_PI, ROUND, ALU.mult, ALU.add))
            link(V.tensor_scalar(col(22), col(22), ROUND, None, ALU.subtract))
            link(V.scalar_tensor_tensor(col(23), col(22), -PI_A, theta, ALU.mult, ALU.add))
            link(V.scalar_tensor_tensor(col(23), col(22), -PI_B, col(23), ALU.mult, ALU.add))
            link(V.scalar_tensor_tensor(col(23), col(22), -PI_C, col(23), ALU.mult, ALU.add))
            link(V.tensor_scalar(col(20), col(23), 0.5, None, ALU.mult))
            V.tensor_scalar(col(21), col(20), TWO_PI / 4, None, ALU.add).then_inc(trig_in, 1)

            def stats(g, which, src):
                k, t0, _, _ = group(g)
                for a in range(k):
                    ins = V.bn_stats(bst[:, which, (t0 + a) % BST_RING, :], src[:, a, :])
                link(ins)
                for a in range(k):
                    ins = V.bn_aggr(mv[:, which, t0 + a, :], bst[:, which, (t0 + a) % BST_RING, :])
                ins.then_inc(stats_done[which], 1)

            def limit(b):
                dve.wait_ge(sum_done, b + 1)
                V.tensor_scalar(h[b % 3], h[b % 3], 1.0, None, ALU.min).then_inc(h_done, 1)
                dve.wait_ge(h_done, b + 1)

            def normalise_text():
                dve.wait_ge(rstd_done[0], 1)
                for a in range(TXT_TILES):
                    k = IMG_TILES + a
                    ins = V.tensor_scalar(u_txt[:, a, :], h_txt[:, a, :], mv[:, 0, k, 0:1], rstd[:, 0, k:k + 1],
                                          ALU.subtract, ALU.mult)
                ins.then_inc(u_done, 1)

            def centre(g):
                k, t0, _, ug = group(g)
                dve.wait_ge(y_psum, b_no(g))
                x = ps_y[(b_no(g) - 1) % 2][:, 0:k * D].rearrange("p (a d) -> p a d", d=D)
                stats(g, 1, x)
                dve.wait_ge(stats_done[1], b_no(g))
                for a in range(k):
                    ins = V.scalar_tensor_tensor(ug[:, a, :], x[:, a, :], mv[:, 1, t0 + a, 0:1], gamma_row,
                                                 ALU.subtract, ALU.mult)
                ins.then_inc(y_read, 1)

            def add_h(g):
                k, t0, hg, ug = group(g)
                dve.wait_ge(rstd_done[1], b_no(g))
                if g in PARTS:
                    dve.wait_ge(txt_beta, list(PARTS).index(g) + 1)
                else:
                    dve.wait_ge(beta_done, g + 1)
                dve.wait_ge(y_read, b_no(g))
                for a in range(k):
                    ins = V.scalar_tensor_tensor(hg[:, a, :], ug[:, a, :], rstd[:, 1, t0 + a:t0 + a + 1], hg[:, a, :],
                                                 ALU.mult, ALU.add)
                ins.then_inc(h1_done, 1)

            def stats2(g):
                dve.wait_ge(h1_done, b_no(g))
                stats(g, 2, group(g)[2])

            def recur(b):
                dve.wait_ge(v_psum, b + 1)
                if b == 0:
                    dve.wait_ge(tables_done, 1)
                    dve.wait_ge(decay_done, 1)
                V.tensor_tensor(drive, ps_v[:, 0:L], in_table, ALU.mult).then_inc(drive_done, 1)
                dve.wait_ge(drive_done, b + 1)
                if b >= 1:
                    dve.wait_ge(turned_done, b)
                V.tensor_tensor_scan(state, decay, drive, 0.0, ALU.mult, ALU.add).then_inc(state_done, 1)

            def largest_b1():
                link(V.tensor_tensor(b1_scaled[:, :, :], b1_cols[:, :, :], b1_cols[:, :, :], ALU.mult))
                V.tensor_reduce(wmax[:, :, 2], b1_scaled[:, :, :], AX.X, ALU.max).then_inc(b1_max, 1)

            def scale(e):
                dve.wait_ge(max_all, e + 1)
                link(V.tensor_scalar(pow2[:, e, :].bitcast(I32), wmax_all[:, e, :].bitcast(I32), 1, 0x7F800000,
                                     ALU.logical_shift_right, ALU.bitwise_and))
                link(V.tensor_scalar(pow2[:, e, :], pow2[:, e, :], 2.0 ** (64 - 13), TINY * 2.0 ** -13,
                                     ALU.mult, ALU.max))
                V.reciprocal(wsc[:, e, :], pow2[:, e, :]).then_inc(scale_done, 1)

            def low1(e):
                dve.wait_ge(hi1_done, e + 1)
                V.scalar_tensor_tensor(w1_parts[:, e, 1], w1_stage(e), wsc[:, e, 0:1], w1_parts[:, e, 0],
                                       ALU.mult, ALU.subtract).then_inc(lo1_done, 1)

            def low2(e):
                dve.wait_ge(hi2_done, e + 1)
                V.scalar_tensor_tensor(w2_parts[:, e, :, 1, :], w2_stage(e), wsc[:, e, 1:2], w2_parts[:, e, :, 0, :],
                                       ALU.mult, ALU.subtract).then_inc(lo2_done, 1)

            def tables():
                cross_t = in_table[:, 0:L - 1].rearrange("p (a l) -> p a l", a=2)
                dve.wait_ge(trig_done, 1)
                s2, c2 = col(2), col(3)
                sin_1, cos_1 = col(4), col(5)
                link(V.tensor_tensor(sin_1, s2, c2, ALU.mult))
                link(V.tensor_scalar(sin_1, sin_1, 2.0, None, ALU.mult))
                link(V.tensor_tensor(cos_1, s2, s2, ALU.mult))
                link(V.tensor_scalar(cos_1, cos_1, -2.0, 1.0, ALU.mult, ALU.add))
                V.tensor_copy(cos_t[:, 1:2], cos_1)
                V.tensor_copy(sin_t[:, 1:2], sin_1)
                V.memset(cos_t[:, 0:1], 1.0)
                link(V.memset(sin_t[:, 0:1], 0.0))
                dve.sem_inc(angle_done, 1)
                m = 1
                while m < L - 1:
                    cm, sm, f = cos_t[:, m:m + 1], sin_t[:, m:m + 1], col(6)
                    if m in (8, 64):
                        link(V.tensor_tensor(f, cm, cm, ALU.mult))
                        link(V.scalar_tensor_tensor(f, sm, sm, f, ALU.mult, ALU.add))
                        link(V.tensor_scalar(f, f, -0.5, 1.5, ALU.mult, ALU.add))
                        link(V.tensor_scalar(cos_sin[:, :, m:m + 1], cos_sin[:, :, m:m + 1], f, None, ALU.mult))
                    k = min(m, L - 1 - m)
                    cross = cross_t[:, :, 0:k]
                    link(V.tensor_scalar(cross, cos_sin[:, :, 1:k + 1], sm, None, ALU.mult))
                    V.scalar_tensor_tensor(cos_t[:, m + 1:m + k + 1], cos_t[:, 1:k + 1], cm, cross[:, 1, :],
                                           ALU.mult, ALU.subtract)
                    link(V.scalar_tensor_tensor(sin_t[:, m + 1:m + k + 1], sin_t[:, 1:k + 1], cm, cross[:, 0, :],
                                                ALU.mult, ALU.add))
                    m *= 2
                dve.wait_ge(factors_done, 1)
                link(V.tensor_scalar(in_table, sin_t, col(17), None, ALU.mult))
                V.scalar_tensor_tensor(in_table, cos_t, col(16), in_table, ALU.mult, ALU.add)
                link(V.tensor_scalar(out_table, sin_t, small[:, 3:4], None, ALU.mult))
                V.scalar_tensor_tensor(out_table, cos_t, small[:, 2:3], out_table,
                                       ALU.mult, ALU.subtract).then_inc(tables_done, 1)

            def hidden_scales():
                P1, P2, PB = pow2[:, :, 0], pow2[:, :, 1], pow2[:, :, 2]
                bound, h_scale, relu_scale, y_scale = (hsc[:, i, :] for i in range(4))
                link(V.tensor_scalar(bound, P1, 2.0 ** 8, None, ALU.mult))
                link(V.tensor_tensor(bound, bound, PB, ALU.add))
                link(V.tensor_scalar(bound, bound, 2.0 ** 14, None, ALU.mult))
                link(V.tensor_scalar(bound.bitcast(I32), bound.bitcast(I32), 0x7F800000, None, ALU.bitwise_and))
                link(V.reciprocal(h_scale, bound))
                link(V.tensor_scalar(h_scale, h_scale, 2.0 ** 14, None, ALU.mult))
                link(V.tensor_tensor(relu_scale, h_scale, P1, ALU.mult))
                link(V.tensor_scalar(relu_scale, relu_scale, 1.0 / X_SCALE, None, ALU.mult))
                link(V.tensor_tensor(y_scale, bound, P2, ALU.mult))
                link(V.tensor_scalar(y_scale, y_scale, 2.0 ** -14, None, ALU.mult))
                link(V.tensor_tensor(b1_scaled[:, :, :], b1_cols[:, :, :],
                                     h_scale.rearrange("p (e a) -> p e a", a=1).broadcast_to([P, E, KH]), ALU.mult))

            dve.wait_ge(txt_in, 32)
            stats(TXTG, 0, h_txt)
            limit(0)
            stats(0, 0, h[0])
            normalise_text()
            dve.wait_ge(consts_in, 16 * N_CONST)
            largest_b1()
            tables()
            recur(0)
            limit(1)
            stats(1, 0, h[1])
            scale(0)
            low1(0)
            low2(0)
            scale(1)
            dve.wait_ge(late_in, 16 * N_LATE)
            for step in range(1, BATCH + 1):
                backs = BACKS.get(step, [])
                for g in backs:
                    centre(g)
                if step < E - 1:
                    low1(step)
                for g in backs:
                    add_h(g)
                if step < BATCH:
                    recur(step)
                for g in backs:
                    stats2(g)
                if step + 1 < BATCH:
                    limit(step + 1)
                    stats(step + 1, 0, h[(step + 1) % 3])
                if step < E - 1:
                    low2(step)
                if step + 1 < E - 1:
                    scale(step + 1)
                if step == E - 1:
                    scale(E - 1)
            hidden_scales()
            low1(E - 1)
            low2(E - 1)

            def over_e(x):
                return x.rearrange("p (t a) -> p t a", a=1).broadcast_to([P, NT, E])

            def over_t(x):
                return x.rearrange("p (a e) -> p a e", a=1).broadcast_to([P, NT, E])

            dve.wait_ge(consts2_in, 16 * N_CONST2)
            dve.wait_ge(logits_done, len(BACK))
            logit = ps_logit[:, 0:NT * E].rearrange("p (t e) -> p t e", e=E)
            link(V.tensor_tensor(r_a, logit, over_t(gateb_row), ALU.add))
            link(V.tensor_reduce(tr[0][:, :], r_a, AX.X, ALU.max))
            V.tensor_tensor(r_a, r_a, over_e(tr[0][:, :]), ALU.subtract).then_inc(shifted, 1)
            dve.wait_ge(shifted, 1)
            link(V.scalar_tensor_tensor(r_c, r_a, 0.0, over_t(desc[:, :]), ALU.is_equal, ALU.mult))
            link(V.tensor_reduce(tr[0][:, :], r_c, AX.X, ALU.max))
            link(V.tensor_tensor(pick[0], r_c, over_e(tr[0][:, :]), ALU.is_equal))
            dve.wait_ge(exped, 1)
            link(V.scalar_tensor_tensor(r_c, pick[0], -2.0, r_b, ALU.mult, ALU.add))
            link(V.tensor_reduce(tr[0][:, :], r_c, AX.X, ALU.max))
            link(V.tensor_tensor(r_a, r_c, over_e(tr[0][:, :]), ALU.is_equal))
            link(V.tensor_tensor(r_a, r_a, over_t(desc[:, :]), ALU.mult))
            link(V.tensor_reduce(tr[0][:, :], r_a, AX.X, ALU.max))
            link(V.tensor_tensor(pick[1], r_a, over_e(tr[0][:, :]), ALU.is_equal))
            link(V.tensor_tensor(r_c, pick[0], pick[1], ALU.add))
            V.tensor_tensor(picked.rearrange("p e t -> p t e"), r_c, over_e(valid[:, :]),
                            ALU.mult).then_inc(picked_done, 1)
            link(V.tensor_reduce(tr[0][:, :], r_b, AX.X, ALU.add))
            V.reciprocal(tr[1][:, :], tr[0][:, :]).then_inc(inverse_done, 1)
            dve.wait_ge(rank_psum, 1)
            total = ps_rank[:, NT * E:2 * NT * E]
            cum, before = cmp8[:, 0:NT, :].rearrange("p a b -> p (a b)"), cmp8[:, NT:2 * NT, :].rearrange("p a b -> p (a b)")
            link(V.tensor_tensor_scan(cum, ones_f[:, :], total, 0.0, ALU.mult, ALU.add))
            link(V.tensor_tensor(before, cum, total, ALU.subtract))
            cum_e = cum.rearrange("p (e t) -> p e t", t=NT)
            before_e = before.rearrange("p (e t) -> p e t", t=NT)
            count, tiles, tiles_cum, base = (small[:, 32 + E * i:32 + E * (i + 1)] for i in range(4))
            link(V.tensor_tensor(count, cum_e[:, :, NT - 1], before_e[:, :, 0], ALU.subtract))
            link(V.tensor_scalar(tiles, count, 1.0 / P, 127.0 / 256.0, ALU.mult, ALU.add))
            link(V.tensor_scalar(tiles, tiles, ROUND, ROUND, ALU.add, ALU.subtract))
            link(V.tensor_tensor_scan(tiles_cum, ones_f[:, 0:E], tiles, 0.0, ALU.mult, ALU.add))
            link(V.tensor_tensor(base, tiles_cum, tiles, ALU.subtract))
            link(V.scalar_tensor_tensor(base, base, float(P), before_e[:, :, 0], ALU.mult, ALU.subtract))
            link(V.tensor_tensor(before, before, ps_rank[:, 0:NT * E], ALU.add))
            slot_of = r_c[:, :, :]
            dve.wait_ge(gates_done, 1)
            link(V.tensor_tensor(slot_of, before_e.rearrange("p e t -> p t e"), over_t(base), ALU.add))
            for c in range(TOPK):
                link(V.tensor_tensor(pick[c][:, :, :], pick[c][:, :, :], slot_of, ALU.mult))
                link(V.tensor_reduce(slot_f[:, c, :], pick[c][:, :, :], AX.X, ALU.add))
            link(V.tensor_scalar(tile_f, slot_f, 1.0 / P, -127.0 / 256.0, ALU.mult, ALU.add))
            link(V.tensor_scalar(tile_f, tile_f, ROUND, ROUND, ALU.add, ALU.subtract))
            V.scalar_tensor_tensor(within_f[:, :, :], tile_f, -float(P), slot_f,
                                   ALU.mult, ALU.add).then_inc(within_ready, 1)
            dve.wait_ge(within_ready, 1)
            def slot_onehot(c, t0, t1):
                n = t1 - t0
                return V.tensor_tensor(onehot_slot[:, c * NT + t0:c * NT + t1, :],
                                       iota_slot[:, :].rearrange("p (a r) -> p a r", a=1).broadcast_to([P, n, P]),
                                       within_f[:, c, t0:t1].rearrange("p (t a) -> p t a", a=1)
                                       .broadcast_to([P, n, P]), ALU.is_equal)

            for c in range(TOPK):
                V.tensor_tensor(onehot_tile[:, c * NT:(c + 1) * NT, :], over_slots(iota_tile[:, :]),
                                per_token(tile_f[:, c, :]), ALU.is_equal).then_inc(tile_onehot, 1)
            slot_onehot(0, 0, NT).then_inc(onehots_done, 1)
            slot_onehot(1, 0, DVE_HOTS).then_inc(onehots_done, 1)
            link(V.tensor_tensor(cmp8, iota_tile[:, :].rearrange("p (t a) -> p t a", a=1)
                                 .broadcast_to([P, SLOT_TILES, E]),
                                 tiles_cum.rearrange("p (a e) -> p a e", a=1).broadcast_to([P, SLOT_TILES, E]),
                                 ALU.is_ge))
            dve.wait_ge(slot_psum, 1)
            val, is_pos, is_pad = ps_slot[:, 0:SLOT_TILES], small[:, 192:192 + SLOT_TILES], small[:, 256:256 + SLOT_TILES]
            tok = small[:, 320:320 + SLOT_TILES]
            link(V.tensor_scalar(is_pos, val, 0.0, None, ALU.is_gt))
            link(V.tensor_scalar(is_pad, val, 0.0, pad_row[:, 0:1], ALU.is_equal, ALU.mult))
            link(V.scalar_tensor_tensor(tok, val, float(MID), is_pos, ALU.add, ALU.subtract))
            V.tensor_tensor(slot_token[:, :], tok, is_pad, ALU.add).then_inc(slots_done, 1)
            ends, ends2 = small[:, 128:128 + SLOT_TILES + PACK], small[:, 64:64 + SLOT_TILES + PACK]
            link(V.memset(small[:, 64:192], 0.0))
            link(V.tensor_reduce(ends[:, 0:SLOT_TILES], cmp8, AX.X, ALU.add))
            link(V.tensor_scalar(ends[:, 0:SLOT_TILES], ends[:, 0:SLOT_TILES], float(E - 1), None, ALU.min))
            V.tensor_copy(tile_expert[:, :], ends[:, 0:SLOT_TILES])
            n4, n2 = SLOT_TILES + PACK // 2, SLOT_TILES + PACK - 2
            link(V.scalar_tensor_tensor(ends2[:, 0:n2], ends[:, 1:n2 + 1], float(E), ends[:, 0:n2], ALU.mult, ALU.add))
            link(V.scalar_tensor_tensor(ends[:, 0:n4], ends2[:, 2:n4 + 2], float(E ** 2), ends2[:, 0:n4],
                                        ALU.mult, ALU.add))
            V.scalar_tensor_tensor(tile_packed[:, :], ends[:, 4:SLOT_TILES + 4], float(E ** 4), ends[:, 0:SLOT_TILES],
                                   ALU.mult, ALU.add).then_inc(experts_done, 1)

            def x_low(j, s):
                dve.wait_ge(xhi_done, j + 1)
                V.scalar_tensor_tensor(x_lo[s], ps_x[s][:, 0:D].rearrange("p (k c) -> p k c", k=KD), X_SCALE, x_hi[s],
                                       ALU.mult, ALU.subtract).then_inc(xlo_done, 1)

            def split(j, s, half):
                dve.wait_ge(relu_done, j * 2 + (half + 1))
                a = h_act[s][:, half * 512:(half + 1) * 512].rearrange("p (k c) -> p k c", c=P)
                k = slice(4 * half, 4 * half + 4)
                V.tensor_copy(h_hi[s][:, k, :], a).then_inc(hi_done, 1)
                dve.wait_ge(hi_done, j * 2 + (half + 1))
                V.tensor_tensor(h_lo[s][:, k, :], a, h_hi[s][:, k, :], ALU.subtract).then_inc(split_done, 1)

            def scale_y(j, s, e):
                y_scale = hsc[:, 3, bass.ds(e, 1)]
                dve.wait_ge(mm2_done, j + 1)
                V.scalar_tensor_tensor(y_slot[s], ps_out[s][:, D:2 * D], y_scale,
                                       b2_rows[:, bass.ds(e, 1), :].rearrange("p a d -> p (a d)"),
                                       ALU.mult, ALU.add).then_inc(y_half, 1)
                dve.wait_ge(y_half, j + 1)
                V.scalar_tensor_tensor(y_slot[s], ps_out[s][:, 0:D], y_scale, y_slot[s],
                                       ALU.mult, ALU.add).then_inc(y_scaled, 1)

            def gate_y(j, s, r, e, early=False):
                dve.wait_ge(y_scaled, j + 1)
                if not early:
                    dve.wait_ge(y_out, j * 16 - 16)
                V.tensor_scalar(y_gated[s], y_slot[s], x_slot[r][:, bass.ds(e + D, 1)], None,
                                ALU.mult).then_inc(y_done, 1)

            def dve_step(j, s, r, early=False, nxt=True, x=True, nxt2=True):
                e = dve.value_load(tile_expert[0:1, bass.ds(j, 1)], min_val=0, max_val=E - 1)
                scale_y(j, s, e)
                if nxt:
                    split(j + 1, 1 - s, 1)
                gate_y(j, s, r, e, early)
                if x:
                    x_low(j + 3, 1 - s)
                if nxt2:
                    split(j + 2, s, 0)

            dve.wait_ge(b2_in, 16)
            x_low(0, 0)
            x_low(1, 1)
            split(0, 0, 0)
            split(0, 0, 1)
            x_low(2, 0)
            split(1, 1, 0)
            for j in range(PEEL):
                dve_step(j, j, j, early=True)
            with dve.Fori(0, LOOPS) as i:
                for k in range(UNROLL):
                    dve_step(i * UNROLL + (PEEL + k), k % 2, (PEEL + k) % X_RING)
            for j in REST:
                dve_step(j, j % 2, j % X_RING, nxt=j + 1 < SLOT_TILES, x=j + 3 < SLOT_TILES,
                         nxt2=j + 2 < SLOT_TILES)


def kernel(x, txt, L0_attn_log_neg_real, L0_attn_imag, L0_attn_B_mat, L0_attn_C_mat, L0_attn_D, L0_attn_gamma,
           L0_attn_beta, L0_ffn_gate_w, L0_ffn_gate_b, L0_ffn_w1, L0_ffn_b1, L0_ffn_w2, L0_ffn_b2):
    import ml_dtypes
    import numpy as np
    import concourse.bacc as bacc
    from concourse.bass_utils import run_bass_kernel_spmd

    f = np.float32
    a = np.asarray

    def rows(v):
        return np.broadcast_to(a(v).reshape(1, -1), (P, a(v).size)).copy()

    tok = np.zeros((P, NT), np.int64)
    real = np.ones((P, NT), bool)
    for k in range(IMG_TILES):
        tok[:, k] = (k // 2) * L + (k % 2) * P + np.arange(P)
    for k in range(TXT_TILES):
        flat = k * P + np.arange(P)
        real[:, IMG_TILES + k] = flat < NTXT
        tok[:, IMG_TILES + k] = np.where(flat < NTXT, (flat // TXT) * L + IMG + flat % TXT, NTOK + np.arange(P))
    half = (np.arange(P) < STATE)
    cols = np.zeros((P, 16), f)
    cols[:, 0] = np.tile(a(L0_attn_log_neg_real), 2)
    cols[:, 1] = np.tile(a(L0_attn_imag), 2)
    cols[:, 2] = half
    cols[:, 3] = ~half
    ts = {
        "x": np.pad(a(x)[:, 0], ((0, 0), (0, 1), (0, 1))),
        "txt": a(txt).reshape(NTXT, D),
        "ident": np.eye(P, dtype=f),
        "cols": cols,
        "b1": a(L0_ffn_b1).reshape(E, KH, P).transpose(2, 0, 1).copy(),
        "b_t": np.concatenate([a(L0_attn_B_mat).T] * 2, 1).reshape(KD, P, P).transpose(1, 0, 2).copy(),
        "c_t": np.concatenate([a(L0_attn_C_mat).T] * 2, 0),
        "gate_t": a(L0_ffn_gate_w).T.reshape(KD, P, E).transpose(1, 0, 2).copy(),
        "d_row": rows(L0_attn_D), "gamma_row": rows(L0_attn_gamma), "beta_row": rows(L0_attn_beta),
        "gateb_row": rows(L0_ffn_gate_b),
        "ones_f": np.ones((P, NT * E), f),
        "iota_slot": rows(np.arange(P, dtype=np.float16)),
        "iota_tile": rows(np.arange(SLOT_TILES, dtype=f)),
        "token_val": np.where(real, np.where(tok < MID, tok - MID, tok - MID + 1), 0).astype(f),
        "valid": real.astype(f),
        "prefix_w": np.triu(np.ones((P, P)), 1).astype(ml_dtypes.bfloat16),
        "ones_w": np.ones((P, P), ml_dtypes.bfloat16),
        "desc": rows(np.arange(E, 0, -1, dtype=f)),
        "pad_row": (NTOK - MID + np.arange(P, dtype=f)).reshape(P, 1),
        "b2": rows(L0_ffn_b2).reshape(P, E, D),
        "w1": a(L0_ffn_w1), "w2": a(L0_ffn_w2),
    }
    ts = {k: np.ascontiguousarray(v) for k, v in ts.items()}
    nc = bacc.Bacc("TRN2", target_bir_lowering=False, num_devices=1)
    aps = {k: nc.dram_tensor(f"in_{k}", v.shape, mybir.dt.from_np(v.dtype), kind="ExternalInput").ap()
           for k, v in ts.items()}
    out = nc.dram_tensor("out", (ROWS, D), F32, kind="ExternalOutput").ap()
    build(nc, aps, out)
    r = run_bass_kernel_spmd(nc, [{f"in_{k}": v for k, v in ts.items()}], core_ids=[0])
    return r.results[0]["out"][:NTOK].reshape(BATCH, L, D)
```
